# Optimizing a Trainium2 kernel written in Bass

```python
import numpy as np
import jax
import jax.numpy as jnp

def _softmax(x, axis=-1):
    return jax.nn.softmax(x, axis=axis)

def _gelu(x):
    return jax.nn.gelu(x, approximate=True)

def _silu(x):
    return jax.nn.silu(x)

def _sigmoid(x):
    return jax.nn.sigmoid(x)

def _layernorm(x, axis=-1, eps=1e-05):
    m = jnp.mean(x, axis=axis, keepdims=True)
    v = jnp.var(x, axis=axis, keepdims=True)
    return (x - m) / jnp.sqrt(v + eps)

def _scatter_add(tgt, idx, src, axis=0):
    return tgt.at[idx].add(src)

def _segment_sum(src, seg, n):
    return jax.ops.segment_sum(src, seg, n)
kernel_name = 'mk_pixart_resid_d1_seqx_r4_3ef942'

def setup_inputs(seed: int=0):
    np.random.seed(seed)
    _w = jnp.asarray

    def _rec_inputs():
        import jax
        import jax.numpy as jnp
        _rk = jax.random.key(seed)
        x = 7.22e-05 + 1 * jax.random.normal(jax.random.fold_in(_rk, 1), (8, 512, 256), jnp.float32)
        _lenS = 512 - jax.random.randint(jax.random.fold_in(_rk, 7), (8,), 0, max(1, 512 // 4) + 1, jnp.int32)
        _lenS2 = 64 - jax.random.randint(jax.random.fold_in(_rk, 8), (8,), 0, max(1, 64 // 4) + 1, jnp.int32)
        _ctx_1024P = jax.random.normal(jax.random.fold_in(_rk, 11), (8, 16, 256), jnp.float32)
        _ctx_1024c = jax.random.dirichlet(jax.random.fold_in(_rk, 511), 0.3 * jnp.ones((16,), jnp.float32), (8, 64))
        _ctx_1024t = jnp.einsum('bsk,bkd->bsd', _ctx_1024c, _ctx_1024P)
        _ctx_1024t = _ctx_1024t * jax.lax.rsqrt(jnp.mean(jnp.square(_ctx_1024t)) + 1e-12) * 0.953939
        ctx_1024 = 4.13588e-05 + 0.999923 * (_ctx_1024t + 0.3 * jax.random.normal(jax.random.fold_in(_rk, 611), (8, 64, 256), jnp.float32))
        condB_tau = jax.random.uniform(jax.random.fold_in(_rk, 12), (8,), jnp.float32, 0.0, 1.45372)
        fside_BxS2_0 = 0.0088954 + 1.00633 * jax.random.normal(jax.random.fold_in(_rk, 13), (8, 64), jnp.float32)
        return (x, ctx_1024, condB_tau, fside_BxS2_0)
    x, ctx_1024, condB_tau, fside_BxS2_0 = _rec_inputs()

    def _L0_xcond_setup():
        import jax, jax.numpy as jnp
        import numpy as np
        D_MODEL = 256
        N_HEADS = 16
        key = jax.random.key(seed)
        ks = jax.random.split(key, 16)
        B, L, S, D = (4, 512, 512, D_MODEL)
        inp = {'q': jax.random.normal(ks[0], (B, L, D), jnp.float32), 'k': jax.random.normal(ks[1], (B, S, D), jnp.float32), 'v': jax.random.normal(ks[2], (B, S, D), jnp.float32), 'tau': jax.random.uniform(ks[3], (B, 1), jnp.float32, 0.5, 1.5), 'delta': jax.random.normal(ks[4], (B, S), jnp.float32)}
        s = 1.0 / np.sqrt(D)
        inp['Wq'] = jax.random.normal(ks[5], (D, D), jnp.float32) * s
        inp['bq'] = jnp.zeros((D,), jnp.float32)
        inp['Wk'] = jax.random.normal(ks[6], (D, D), jnp.float32) * s
        inp['bk'] = jnp.zeros((D,), jnp.float32)
        inp['Wv'] = jax.random.normal(ks[7], (D, D), jnp.float32) * s
        inp['bv'] = jnp.zeros((D,), jnp.float32)
        inp['Wo'] = jax.random.normal(ks[8], (D, D), jnp.float32) * s
        inp['bo'] = jnp.zeros((D,), jnp.float32)
        return inp
    _L0_xcond_all = _L0_xcond_setup()
    _L0_xcond_in = {k: v for k, v in _L0_xcond_all.items() if k in ('Wq', 'bq', 'Wk', 'bk', 'Wv', 'bv', 'Wo', 'bo')}
    del _L0_xcond_all

    def _L0_ffn_setup():
        import jax, jax.numpy as jnp
        import numpy as np
        DIM = 256
        NQ = 16
        NKV = 4
        HD = DIM // NQ
        HID = 512
        E = 8
        B, S = (1, 256)
        EPS = 1e-06

        def rmsnorm(x, w):
            ms = jnp.mean(x * x, axis=-1, keepdims=True)
            return w * (x * jax.lax.rsqrt(ms + EPS))

        def rope_tables(seq_len, head_dim):
            inv_freq = 1.0 / 10000.0 ** (jnp.arange(0, head_dim, 2, dtype=jnp.float32) / head_dim)
            t = jnp.arange(seq_len, dtype=jnp.float32)
            freqs = jnp.einsum('i,j->ij', t, inv_freq)
            return (jnp.cos(freqs), jnp.sin(freqs))

        def apply_rope(x, cos, sin):
            c = cos[None, :, None, :]
            s = sin[None, :, None, :]
            half = x.shape[-1] // 2
            x1, x2 = (x[..., :half], x[..., half:])
            return jnp.concatenate([x1 * c - x2 * s, x1 * s + x2 * c], axis=-1)

        def _forward(x, ln1_w, ln2_w, Wq, bq, Wk, bk, Wv, bv, qn_w, kn_w, Wg, bg, Wo, bo, Wr, br, W1, b1, W2, b2):
            batch, seq, _ = x.shape
            cos, sin = rope_tables(seq, HD)
            h = rmsnorm(x, ln1_w)
            q = (h @ Wq + bq).reshape(batch, seq, NQ, HD)
            k = (h @ Wk + bk).reshape(batch, seq, NKV, HD)
            v = (h @ Wv + bv).reshape(batch, seq, NKV, HD)
            q = rmsnorm(apply_rope(q, cos, sin), qn_w)
            k = rmsnorm(apply_rope(k, cos, sin), kn_w)
            rep = NQ // NKV
            k = jnp.repeat(k, rep, axis=2)
            v = jnp.repeat(v, rep, axis=2)
            scores = jnp.einsum('bthd,bshd->bhts', q, k) / np.sqrt(HD)
            causal = jnp.tril(jnp.ones((seq, seq), dtype=bool))
            scores = jnp.where(causal[None, None], scores, -jnp.inf)
            attn = jax.nn.softmax(scores, axis=-1)
            out = jnp.einsum('bhts,bshd->bthd', attn, v)
            gate = jax.nn.sigmoid(out @ Wg + bg)
            out = (out * gate).reshape(batch, seq, DIM)
            x = x + out @ Wo + bo
            h2 = rmsnorm(x, ln2_w)
            logits = h2 @ Wr + br
            top1 = jnp.argmax(logits, axis=-1).reshape(-1)
            xt = h2.reshape(-1, DIM)
            u = jnp.einsum('td,edf->tef', xt, W1) + b1
            u1, u2 = (u[..., :HID], u[..., HID:])
            act = u1 * jax.nn.sigmoid(u2)
            y_all = jnp.einsum('teh,ehd->ted', act, W2) + b2
            y = jnp.take_along_axis(y_all, top1[:, None, None], axis=1)[:, 0, :]
            return x + y.reshape(batch, seq, DIM)
        key = jax.random.key(seed)
        ks = jax.random.split(key, 20)
        sc = lambda fan_in: 1.0 / np.sqrt(fan_in)
        d = {}
        d['x'] = jax.random.normal(ks[0], (B, S, DIM), dtype=jnp.float32)
        d['ln1_w'] = jnp.ones((DIM,), jnp.float32)
        d['ln2_w'] = jnp.ones((DIM,), jnp.float32)
        d['Wq'] = jax.random.normal(ks[1], (DIM, DIM), jnp.float32) * sc(DIM)
        d['bq'] = jnp.zeros((DIM,), jnp.float32)
        d['Wk'] = jax.random.normal(ks[2], (DIM, HD * NKV), jnp.float32) * sc(DIM)
        d['bk'] = jnp.zeros((HD * NKV,), jnp.float32)
        d['Wv'] = jax.random.normal(ks[3], (DIM, HD * NKV), jnp.float32) * sc(DIM)
        d['bv'] = jnp.zeros((HD * NKV,), jnp.float32)
        d['qn_w'] = jnp.ones((HD,), jnp.float32)
        d['kn_w'] = jnp.ones((HD,), jnp.float32)
        d['Wg'] = jax.random.normal(ks[4], (HD, HD), jnp.float32) * sc(HD)
        d['bg'] = jnp.zeros((HD,), jnp.float32)
        d['Wo'] = jax.random.normal(ks[5], (DIM, DIM), jnp.float32) * sc(DIM)
        d['bo'] = jnp.zeros((DIM,), jnp.float32)
        d['Wr'] = jax.random.normal(ks[6], (DIM, E), jnp.float32) * sc(DIM)
        d['br'] = jnp.zeros((E,), jnp.float32)
        d['W1'] = jax.random.normal(ks[7], (E, DIM, 2 * HID), jnp.float32) * sc(DIM)
        d['b1'] = jnp.zeros((E, 2 * HID), jnp.float32)
        d['W2'] = jax.random.normal(ks[8], (E, HID, DIM), jnp.float32) * sc(HID)
        d['b2'] = jnp.zeros((E, DIM), jnp.float32)
        return d
    _L0_ffn_all = _L0_ffn_setup()
    _L0_ffn_in = {k: v for k, v in _L0_ffn_all.items() if k in ('ln1_w', 'ln2_w', 'Wq', 'bq', 'Wk', 'bk', 'Wv', 'bv', 'qn_w', 'kn_w', 'Wg', 'bg', 'Wo', 'bo', 'Wr', 'br', 'W1', 'b1', 'W2', 'b2')}
    del _L0_ffn_all
    return {'x': x, 'ctx_1024': ctx_1024, 'condB_tau': condB_tau, 'fside_BxS2_0': fside_BxS2_0, 'L0_xcond_Wq': _L0_xcond_in['Wq'], 'L0_xcond_bq': _L0_xcond_in['bq'], 'L0_xcond_Wk': _L0_xcond_in['Wk'], 'L0_xcond_bk': _L0_xcond_in['bk'], 'L0_xcond_Wv': _L0_xcond_in['Wv'], 'L0_xcond_bv': _L0_xcond_in['bv'], 'L0_xcond_Wo': _L0_xcond_in['Wo'], 'L0_xcond_bo': _L0_xcond_in['bo'], 'L0_ffn_ln1_w': _L0_ffn_in['ln1_w'], 'L0_ffn_ln2_w': _L0_ffn_in['ln2_w'], 'L0_ffn_Wq': _L0_ffn_in['Wq'], 'L0_ffn_bq': _L0_ffn_in['bq'], 'L0_ffn_Wk': _L0_ffn_in['Wk'], 'L0_ffn_bk': _L0_ffn_in['bk'], 'L0_ffn_Wv': _L0_ffn_in['Wv'], 'L0_ffn_bv': _L0_ffn_in['bv'], 'L0_ffn_qn_w': _L0_ffn_in['qn_w'], 'L0_ffn_kn_w': _L0_ffn_in['kn_w'], 'L0_ffn_Wg': _L0_ffn_in['Wg'], 'L0_ffn_bg': _L0_ffn_in['bg'], 'L0_ffn_Wo': _L0_ffn_in['Wo'], 'L0_ffn_bo': _L0_ffn_in['bo'], 'L0_ffn_Wr': _L0_ffn_in['Wr'], 'L0_ffn_br': _L0_ffn_in['br'], 'L0_ffn_W1': _L0_ffn_in['W1'], 'L0_ffn_b1': _L0_ffn_in['b1'], 'L0_ffn_W2': _L0_ffn_in['W2'], 'L0_ffn_b2': _L0_ffn_in['b2']}

def reference(x, ctx_1024, condB_tau, fside_BxS2_0, L0_xcond_Wq, L0_xcond_bq, L0_xcond_Wk, L0_xcond_bk, L0_xcond_Wv, L0_xcond_bv, L0_xcond_Wo, L0_xcond_bo, L0_ffn_ln1_w, L0_ffn_ln2_w, L0_ffn_Wq, L0_ffn_bq, L0_ffn_Wk, L0_ffn_bk, L0_ffn_Wv, L0_ffn_bv, L0_ffn_qn_w, L0_ffn_kn_w, L0_ffn_Wg, L0_ffn_bg, L0_ffn_Wo, L0_ffn_bo, L0_ffn_Wr, L0_ffn_br, L0_ffn_W1, L0_ffn_b1, L0_ffn_W2, L0_ffn_b2):
    import jax
    import jax.numpy as jnp

    def _L0_xcond_ref(q, k, v, tau, delta, Wq, bq, Wk, bk, Wv, bv, Wo, bo):
        import jax, jax.numpy as jnp
        import numpy as np
        D_MODEL = 256
        N_HEADS = 16
        B, L, D = q.shape
        S = k.shape[1]
        H = N_HEADS
        E = D // H
        qh = (q @ Wq.T + bq).reshape(B, L, H, E)
        kh = (k @ Wk.T + bk).reshape(B, S, H, E)
        vh = (v @ Wv.T + bv).reshape(B, S, H, E)
        scale = 1.0 / np.sqrt(E).astype(np.float32)
        scores = jnp.einsum('blhe,bshe->bhls', qh, kh)
        scores = scores * tau[:, None, None, :] + delta[:, None, None, :]
        a = jax.nn.softmax(scale * scores, axis=-1)
        out = jnp.einsum('bhls,bshd->blhd', a, vh).reshape(B, L, D)
        return out @ Wo.T + bo

    def _L0_ffn_ref(x, ln1_w, ln2_w, Wq, bq, Wk, bk, Wv, bv, qn_w, kn_w, Wg, bg, Wo, bo, Wr, br, W1, b1, W2, b2):
        import jax, jax.numpy as jnp
        import numpy as np
        DIM = 256
        NQ = 16
        NKV = 4
        HD = DIM // NQ
        HID = 512
        E = 8
        B, S = (1, 256)
        EPS = 1e-06

        def rmsnorm(x, w):
            ms = jnp.mean(x * x, axis=-1, keepdims=True)
            return w * (x * jax.lax.rsqrt(ms + EPS))

        def rope_tables(seq_len, head_dim):
            inv_freq = 1.0 / 10000.0 ** (jnp.arange(0, head_dim, 2, dtype=jnp.float32) / head_dim)
            t = jnp.arange(seq_len, dtype=jnp.float32)
            freqs = jnp.einsum('i,j->ij', t, inv_freq)
            return (jnp.cos(freqs), jnp.sin(freqs))

        def apply_rope(x, cos, sin):
            c = cos[None, :, None, :]
            s = sin[None, :, None, :]
            half = x.shape[-1] // 2
            x1, x2 = (x[..., :half], x[..., half:])
            return jnp.concatenate([x1 * c - x2 * s, x1 * s + x2 * c], axis=-1)

        def _forward(x, ln1_w, ln2_w, Wq, bq, Wk, bk, Wv, bv, qn_w, kn_w, Wg, bg, Wo, bo, Wr, br, W1, b1, W2, b2):
            batch, seq, _ = x.shape
            cos, sin = rope_tables(seq, HD)
            h = rmsnorm(x, ln1_w)
            q = (h @ Wq + bq).reshape(batch, seq, NQ, HD)
            k = (h @ Wk + bk).reshape(batch, seq, NKV, HD)
            v = (h @ Wv + bv).reshape(batch, seq, NKV, HD)
            q = rmsnorm(apply_rope(q, cos, sin), qn_w)
            k = rmsnorm(apply_rope(k, cos, sin), kn_w)
            rep = NQ // NKV
            k = jnp.repeat(k, rep, axis=2)
            v = jnp.repeat(v, rep, axis=2)
            scores = jnp.einsum('bthd,bshd->bhts', q, k) / np.sqrt(HD)
            causal = jnp.tril(jnp.ones((seq, seq), dtype=bool))
            scores = jnp.where(causal[None, None], scores, -jnp.inf)
            attn = jax.nn.softmax(scores, axis=-1)
            out = jnp.einsum('bhts,bshd->bthd', attn, v)
            gate = jax.nn.sigmoid(out @ Wg + bg)
            out = (out * gate).reshape(batch, seq, DIM)
            x = x + out @ Wo + bo
            h2 = rmsnorm(x, ln2_w)
            logits = h2 @ Wr + br
            top1 = jnp.argmax(logits, axis=-1).reshape(-1)
            xt = h2.reshape(-1, DIM)
            u = jnp.einsum('td,edf->tef', xt, W1) + b1
            u1, u2 = (u[..., :HID], u[..., HID:])
            act = u1 * jax.nn.sigmoid(u2)
            y_all = jnp.einsum('teh,ehd->ted', act, W2) + b2
            y = jnp.take_along_axis(y_all, top1[:, None, None], axis=1)[:, 0, :]
            return x + y.reshape(batch, seq, DIM)
        return _forward(x, ln1_w, ln2_w, Wq, bq, Wk, bk, Wv, bv, qn_w, kn_w, Wg, bg, Wo, bo, Wr, br, W1, b1, W2, b2)
    x = x + _L0_xcond_ref(_layernorm(x, axis=-1), ctx_1024, ctx_1024, condB_tau[:, None], fside_BxS2_0, L0_xcond_Wq, L0_xcond_bq, L0_xcond_Wk, L0_xcond_bk, L0_xcond_Wv, L0_xcond_bv, L0_xcond_Wo, L0_xcond_bo)
    x = x + _L0_ffn_ref(_layernorm(x, axis=-1), L0_ffn_ln1_w, L0_ffn_ln2_w, L0_ffn_Wq, L0_ffn_bq, L0_ffn_Wk, L0_ffn_bk, L0_ffn_Wv, L0_ffn_bv, L0_ffn_qn_w, L0_ffn_kn_w, L0_ffn_Wg, L0_ffn_bg, L0_ffn_Wo, L0_ffn_bo, L0_ffn_Wr, L0_ffn_br, L0_ffn_W1, L0_ffn_b1, L0_ffn_W2, L0_ffn_b2)
    return x

_drawn_inputs = setup_inputs


def setup_inputs(seed=0):
    import zlib

    import numpy as np

    out = dict(_drawn_inputs(seed))
    spreads = {'L0_xcond_bq': (0.0, 0.1),
     'L0_xcond_bk': (0.0, 0.8),
     'L0_xcond_bv': (0.0, 0.1),
     'L0_xcond_bo': (0.0, 0.1),
     'L0_ffn_ln1_w': (1.0, 0.2),
     'L0_ffn_ln2_w': (1.0, 0.2),
     'L0_ffn_bq': (0.0, 0.294),
     'L0_ffn_bk': (0.0, 0.322),
     'L0_ffn_bv': (0.0, 0.1),
     'L0_ffn_qn_w': (1.0, 0.2),
     'L0_ffn_kn_w': (1.0, 0.2),
     'L0_ffn_bg': (0.0, 0.1),
     'L0_ffn_bo': (0.0, 0.1),
     'L0_ffn_br': (0.0, 0.1),
     'L0_ffn_b1': (0.0, 0.305),
     'L0_ffn_b2': (0.0, 0.1)}
    factors = {}
    for name, (base, spread) in spreads.items():
        noise = np.random.default_rng([zlib.crc32(name.encode()), seed]).standard_normal(out[name].shape)
        drawn = base * np.exp(spread * noise) if base else spread * noise
        out[name] = jnp.asarray(drawn.astype(out[name].dtype))
    for name, factor in factors.items():
        out[name] = (out[name] * factor).astype(out[name].dtype)
    return out
```

```python
from contextlib import ExitStack

import numpy as np

import concourse.bass as bass
from concourse import mybir

F32 = mybir.dt.float32
F32R = mybir.dt.float32r
BF16 = mybir.dt.bfloat16
I32 = mybir.dt.int32
U32 = mybir.dt.uint32
ALU = mybir.AluOpType
ACT = mybir.ActivationFunctionType
X = mybir.AxisListType.X

P = 128
B, L, D = 8, 512, 256
S = 64
H, E = 16, 16
KV = 4
HS = H + KV
QKV = (H + 2 * KV) * E
NE, HID = 8, 512
C = D // P
T = L // P
TT = B * T
N = B * L
NT = TT + NE - 1
PAIRS = H // 2
LN_EPS, RMS_EPS = 1e-5, 1e-6
SCALE = 0.25
HI_MASK = -4096
ARENA = 45600
OUT_OF_RANGE = 8192

def columns(parts):
    at, n = {}, 0
    for name, width in parts:
        at[name] = (n, width)
        n += width
    return at, n


CONST, CONST_N = columns([
    ("ident", P), ("causal", P), ("before", P), ("ones", P), ("same_head", P), ("row", P),
    ("head_of", PAIRS), ("half", 2), ("part", 3), ("cos", T * E // 2), ("sin", T * E // 2), ("negsin", T * E // 2),
    ("tile_limit", TT), ("earlier", NE * NE), ("rank", NE), ("tile_no", NT + 1), ("token", TT), ("partition", 1),
])
PAR, PAR_N = columns([
    ("c_bo", D), ("bqkv", QKV), ("f_bo", D), ("ln2", D), ("qkn", HS * E), ("br", NE), ("c_bv", D),
    ("tau", B), ("c_bq", C), ("c_bk", C), ("bg", 1), ("ln1", C), ("Wg", P),
])
WGT, WGT_N = columns([("c_q", D), ("c_o", D), ("qkv", QKV), ("f_o", D), ("r", NE)])
CTX, CTX_N = columns([("c_k", D), ("c_v", D), ("ctx", B * S)])


class Steps:

    def __init__(self, sem, names):
        self.sem, self.names = sem, list(names)
        self.n = len(self.names)
        self.index = {name: i for i, name in enumerate(self.names)}
        assert len(self.index) == self.n

    def value(self, b, name):
        return b * self.n + (self.index[name] + 1)


def wait(eng, steps, b, name):
    v = steps.value(b, name)
    if isinstance(v, int) and v <= 0:
        return
    eng.wait_ge(steps.sem, v)


FRONT_PE = ["xT0", "xT1", "cq0", "cq1",
            "cs00", "cs01", "cs10", "cs11",
            "cT00", "cT01", "cs20", "cs21",
            "co0", "cT10", "cT11", "cs30", "cs31",
            "co1", "cT20", "cT21", "co2", "cT30", "cT31", "co3",
            "coT0", "coT1", "wo0", "wo1", "hT0", "hT1",
            "qkv0", "qkv1", "qkv2", "qkv3",
            "stk0", "stq0", "stq1", "stq2", "stq3", "stk1", "stq4", "stq5", "stq6", "stq7"]
ST_UNITS = [n for n in FRONT_PE if n.startswith("st")]
ST_ACT = ST_UNITS[0::2]
FRONT_ACT = ["xT0", "xT1", "cexp0", "cexp1", "cT00", "cT01", "cexp2", "cT10", "cT11", "cexp3",
             "cT20", "cT21", "cT30", "cT31", "coT0", "coT1", "h", "hT0", "hT1"] + ST_ACT
FRONT_DVE = (["ln1_stats", "ln1_aggr", "xn", "cq0", "cq1"]
             + ["cmax0", "csub00", "csub01", "cmax1", "csub10", "csub11", "cmax2", "csub20", "csub21",
                "crec0", "co0", "cmax3", "csub30", "csub31", "crec1", "co1", "crec2", "co2", "crec3", "co3",
                "x1_0", "x1_1", "ln2_stats", "ln2_aggr", "y",
                "qkv0", "qkv1", "qkv2", "qkv3", "cosmul", "rope", "square", "meansq", "qnorm", "qweight",
                "hi0", "lo0", "hi1", "lo1"]
             + [n for n in ST_UNITS if n not in ST_ACT])
FRONT_DVE = ([n for n in FRONT_DVE if not n.startswith(("st", "hi1", "lo1"))]
             + [n for n in ST_UNITS[:5] if n not in ST_ACT] + ["hi1", "lo1"]
             + [n for n in ST_UNITS[5:] if n not in ST_ACT])
FRONT_POOL = ["kbd", "ln1_eps", "ln1_rstd", "xbo", "ln2_eps", "ln2_rstd", "rstd2", "meansq", "meansq_eps", "rms",
              "ybo", "sin1", "sin2", "qk_eps", "qk_rstd"]
SCORES = [f"s{s}{u}" for s in range(PAIRS) for u in range(3)]
ATTN_PE = []
for s in range(PAIRS):
    ATTN_PE += [f"s{s}0", f"s{s}1", f"s{s}2"] + ([f"pv{s - 1}"] if s else [])
ATTN_PE += [f"pv{PAIRS - 1}"]
ATTN_ACT = SCORES
ATTN_POOL = SCORES
ATTN_DVE = ["v"]
for s in range(PAIRS):
    ATTN_DVE += [f"rec{s}", f"o{s}"]
BACK_PE = ["oT0", "oT1", "z0", "z1", "wo0", "wo1", "hT0", "hT1", "lg"]
BACK_ACT = ["oT0", "oT1", "e0", "e1", "hT0", "hT1"]
BACK_DVE = ["e1p", "gate", "gated", "in0", "in1", "stats", "aggr", "h2", "lg"]
BACK_POOL = ["msq", "ms", "ms_eps", "rms", "res", "h2w"]

FRONT_BANK = {}
for i, name in enumerate(FRONT_PE):
    FRONT_BANK[name] = 0
for name in FRONT_PE:
    if name[:2] in ("xT", "cq", "wo", "hT") or name.startswith(("coT", "qkv")):
        FRONT_BANK[name] = int(name[-1]) % 2
    elif name[:2] in ("cs", "cT"):
        FRONT_BANK[name] = int(name[-1])
    elif name.startswith("co"):
        FRONT_BANK[name] = int(name[-1]) % 2
for i, name in enumerate(ST_UNITS):
    FRONT_BANK[name] = i % 2


def before_in_bank(units, bank, name):
    same = [n for n in units if bank[n] == bank[name]]
    i = same.index(name)
    return (same[i - 1], 0) if i else (same[-1], 1)


def build(nc, ins, out):
    with ExitStack() as ctx:
        def sb(name, shape, dt=F32):
            return ctx.enter_context(nc.sbuf_tensor(name, shape, dt))

        def sem(name):
            return ctx.enter_context(nc.semaphore(name))

        ps_s = ctx.enter_context(nc.psum_tensor("ps_scores", [P, 2, 2 * L], F32))
        ps_v = ctx.enter_context(nc.psum_tensor("ps_attended", [P, 512], F32))
        ps_f = ctx.enter_context(nc.psum_tensor("ps_front", [P, 2, 512], F32))
        ps_b = ctx.enter_context(nc.psum_tensor("ps_back", [P, 512], F32))

        const = sb("const", [P, CONST_N])
        routed = sb("routed", [P, 2, NT + 1], I32)
        tile_expert = sb("tile_expert", [P, NT + 1], I32)
        rows_in = sb("rows_in", [P, 2, 1], I32)
        rows_out = sb("rows_out", [P, 2, 1], I32)
        logits = sb("logits", [P, TT, NE])
        half_power = sb("half_power", [P, HS * T])
        sq = sb("sq", [P, PAIRS, L], F32R)
        sk = sb("sk", [P, 2, L], F32R)

        WEX = C * 2 * HID + HID // P * D
        arena = sb("arena", [P, ARENA])
        used = [2 * WEX]

        def take(*shape):
            n = int(np.prod(shape))
            at = used[0]
            used[0] += n
            v = arena[:, at:at + n]
            if len(shape) == 2:
                return v.rearrange("p (a b) -> p a b", a=shape[0])
            if len(shape) == 3:
                return v.rearrange("p (a b c) -> p a b c", a=shape[0], b=shape[1])
            if len(shape) == 4:
                return v.rearrange("p (a b c d) -> p a b c d", a=shape[0], b=shape[1], c=shape[2])
            return v

        par = take(PAR_N)
        wgt = take(C, WGT_N)
        kT = take(C, B * S)
        kbd = take(C, PAIRS, S)
        vbd = take(B, PAIRS, 2, E + 1)
        x_in = take(T, D)
        xn = take(T, D)
        xnT = take(C, L)
        cqT = take(C, L)
        cs = take(2, H * S)
        cpT = take(PAIRS, P)
        co = take(T, D)
        coT = take(C, L)
        x1 = take(2, T, D)
        y = take(2, T, D)
        qkv = take(T, QKV)
        rope_a = take(T, HS * E)
        rope_b = take(T, HS * E)
        pt_at = used[0]
        pt = take(2, 5 * L)
        stack_at = used[0]
        stack = take(T, PAIRS + 2, 4, E)
        v_aug = take(T, KV, E + 1)
        ao = take(T, H, E)
        aoT = take(C, L)
        gate = take(C, L)
        h2 = take(T, D)
        h2T = take(C, L)
        stats = take(3, T, 6)
        mv = take(3, T, 2)
        tiny = take(12, T)
        cmax = take(2, H)
        crec = take(H)
        prec = take(2 * T)
        qk_ms = take(HS * T)
        qk_rs = take(HS * T)
        assert used[0] <= ARENA, used[0]
        ctxw = arena[:, pt_at:pt_at + C * CTX_N].rearrange("p (c n) -> p c n", c=C)
        delta_r = arena[0:3, stack_at:stack_at + B * S]
        delta_s = arena[0:3, stack_at + B * S:stack_at + 2 * B * S]
        delta_parts = arena[0:3, stack_at + 2 * B * S:stack_at + 4 * B * S].bitcast(BF16).rearrange("p (k n) -> p k n", k=4)
        delta3 = sb("delta3", [3, B * S], BF16)
        ones3 = sb("ones3", [3, P], BF16)

        carrier = sb("carrier", [1, 2])

        def wait_apart(eng, steps, b, name):
            wait(eng, steps, b, name)
            if eng is nc.gpsimd:
                nc.gpsimd.tensor_tensor(carrier[:, 1:2], half_power[0:1, 0:1], half_power[0:1, 0:1], ALU.mult)
            else:
                nc.vector.memset(carrier[:, 0:1], 0.0)

        def cst(name, rows=P):
            a, n = CONST[name]
            return const[0:rows, a:a + n]

        def prm(name, rows=P):
            a, n = PAR[name]
            return par[0:rows, a:a + n]

        def w(name):
            a, n = WGT[name]
            return wgt[:, :, a:a + n]

        def cx(name):
            a, n = CTX[name]
            return ctxw[:, :, a:a + n]

        ident = cst("ident")
        wg = prm("Wg")
        rows_dram = nc.dram_tensor("rows_scratch", (N, 2 * D), F32, kind="Internal").ap()

        SETUP_LOADS = 5
        SETUP_DVE = 2 + B + 13
        f_pe, f_act = Steps(sem("front_pe"), FRONT_PE), Steps(sem("front_act"), FRONT_ACT)
        f_dve, f_pool = Steps(sem("front_dve"), FRONT_DVE), Steps(sem("front_pool"), FRONT_POOL)
        a_pe, a_act = Steps(sem("attn_pe"), ATTN_PE), Steps(sem("attn_act"), ATTN_ACT)
        a_dve, a_pool = Steps(sem("attn_dve"), ATTN_DVE), Steps(sem("attn_pool"), ATTN_POOL)
        b_pe, b_act = Steps(sem("back_pe"), BACK_PE), Steps(sem("back_act"), BACK_ACT)
        b_dve, b_pool = Steps(sem("back_dve"), BACK_DVE), Steps(sem("back_pool"), BACK_POOL)
        x_loaded = sem("x_loaded")
        rows_stored = sem("rows_stored")
        loaded = sem("loaded")
        su_pe, su_dve, su_pool = sem("setup_pe"), sem("setup_dve"), sem("setup_pool")

        front_reader = {}
        for n in FRONT_PE:
            if n in FRONT_ACT:
                front_reader[n] = (f_act, n)
            elif n[:2] == "cs":
                front_reader[n] = (f_dve, "csub" + n[2:])
            elif n[:2] == "wo":
                front_reader[n] = (f_dve, "x1_" + n[2:])
            else:
                front_reader[n] = (f_dve, n)
        back_reader = {"oT0": (b_act, "oT0"), "oT1": (b_act, "oT1"), "z0": (b_act, "e0"), "z1": (b_act, "e1"),
                       "wo0": (b_dve, "in0"), "wo1": (b_dve, "in1"), "hT0": (b_act, "hT0"), "hT1": (b_act, "hT1"),
                       "lg": (b_dve, "lg")}

        UNITS = [
            [(0, 0, L)],
            [(1, 0, 3 * P), (3, 3 * P, P)],
            [(2, 0, 2 * P)],
        ]
        UNIT_W = [L, L, L // 2]
        UNIT_AT = [0, 2 * L, 4 * L]

        def pt_block(s, x, kb, qt):
            for u, parts in enumerate(UNITS):
                for k, col, _ in parts:
                    if k == kb:
                        a = UNIT_AT[u] + x * UNIT_W[u] + col + (qt - kb) * P
                        return pt[:, s % 2, a:a + P]


        at = [0]

        def take2(*shape):
            n = int(np.prod(shape))
            v = arena[:, at[0]:at[0] + n]
            at[0] += n
            if len(shape) == 2:
                return v.rearrange("p (a b) -> p a b", a=shape[0])
            if len(shape) == 3:
                return v.rearrange("p (a b c) -> p a b c", a=shape[0], b=shape[1])
            return v

        wex = take2(NE, WEX)
        b1 = take2(NE, 2 * HID)
        b2 = take2(NE, D)
        hot_at = at[0]
        got = take2(2, 2 * D)
        gT = take2(2, C, P)
        ub = take2(2, 2 * HID)
        sg = take2(2, HID)
        act_ = take2(2, HID)
        actT = take2(2, HID)
        res = take2(2, D)
        yo = take2(2, D)
        small = [take2(TT, NE) for _ in range(9)]
        rsmall = take2(12, TT + NE)
        assert at[0] <= ARENA, at[0]
        at[0] = hot_at
        row_hot = take2(TT, P)
        tile_hot = take2(TT, 2, NT + 1)

        w_ready = [sem(f"expert{e}_loaded") for e in range(NE)]
        r_pe, r_dve = sem("routing_pe"), sem("routing_dve")
        up_pe, down_pe = Steps(sem("up_pe"), ["gT", "u"]), Steps(sem("down_pe"), ["aT", "y"])
        up_act, down_act = Steps(sem("up_act"), ["gT", "res"]), Steps(sem("down_act"), ["sig", "aT"])
        m_dve = Steps(sem("expert_dve"), ["ub", "act", "y_b2", "y"])
        m_pool = Steps(sem("expert_rows_pool"), ["in"])
        m_pool_out = Steps(sem("expert_rows_out_pool"), ["out"])
        rows_got = [sem(f"rows_got{d}") for d in range(2)]
        out_stored = [sem(f"out_stored{d}") for d in range(2)]

        def expert_weights(sp, e):
            sp.dma_start(wex[:, e, 0:C * 2 * HID].rearrange("p (c n) -> p c n", c=C),
                         ins["W1"][e].rearrange("(c p) n -> p c n", p=P)).then_inc(w_ready[e], 16)
            sp.dma_start(wex[:, e, C * 2 * HID:WEX].rearrange("p (c n) -> p c n", c=HID // P),
                         ins["W2"][e].rearrange("(c p) n -> p c n", p=P)).then_inc(w_ready[e], 16)

        def moe_loads(sp):
            sp.wait_ge(b_dve.sem, B * b_dve.n)
            sp.wait_ge(rows_stored, 32 * B)
            for e in range(NE):
                if e >= 2:
                    expert_weights(sp, e)
                sp.dma_start(b1[:, e, :], ins["b1"][e:e + 1, :].to_broadcast([P, 2 * HID])).then_inc(w_ready[e], 16)
                sp.dma_start(b2[:, e, :], ins["b2"][e:e + 1, :].to_broadcast([P, D])).then_inc(w_ready[e], 16)

        def pe_routing(pe):
            pe.wait_ge(r_dve, R_HOT)
            hot = small[2].rearrange("p t e -> p (t e)")
            nc.tensor.matmul(ps_f[:, 0, 0:TT * NE], cst("before"), hot, start=True, stop=True)
            nc.tensor.matmul(ps_f[:, 1, 0:TT * NE], cst("ones"), hot, start=True, stop=True).then_inc(r_pe, 1)
            pe.wait_ge(r_dve, R_ONE_HOTS)
            for t in range(TT):
                last = nc.tensor.matmul(ps_v[:, 0:2 * (NT + 1)], row_hot[:, t, :], tile_hot[:, t, :, :].rearrange("p a j -> p (a j)"),
                                        start=(t == 0), stop=(t == TT - 1))
            last.then_inc(r_pe, 1)

        R_HOT, R_ONE_HOTS, R_DONE = 5, 29, 35

        def dve_routing(dve):
            count = [0]

            def done(inst):
                count[0] += 1
                inst.then_inc(r_dve, 1)
                dve.wait_ge(r_dve, count[0])

            def over_e(v):
                return v.unsqueeze(2).to_broadcast([P, TT, NE])

            v = nc.vector
            tt = v.tensor_tensor
            wait(dve, b_dve, B - 1, "lg")
            dve.wait_ge(rows_stored, 32 * B)
            mx, rank = rsmall[:, 0, 0:TT], cst("rank")
            eq, score, hot = small[0], small[1], small[2]
            done(v.tensor_reduce(mx, logits[:], X, ALU.max))
            done(tt(eq, logits[:], over_e(mx), ALU.is_ge))
            done(tt(score, eq, rank.unsqueeze(1).to_broadcast([P, TT, NE]), ALU.mult))
            done(v.tensor_reduce(mx, score, X, ALU.max))
            done(tt(hot, score, over_e(mx), ALU.is_equal))
            assert count[0] == R_HOT
            dve.wait_ge(r_pe, 1)
            et = [small[i].rearrange("p t e -> p (t e)").rearrange("p (e t) -> p e t", e=NE) for i in (3, 4, 5, 6)]
            tot, run = et[0], et[1]
            done(v.tensor_copy(tot, ps_f[:, 1, 0:TT * NE].rearrange("p (t e) -> p e t", e=NE)))
            cur, k = tot, 1
            for nxt in (et[1], et[2], et[1], et[2], et[1]):
                v.tensor_copy(nxt[:, :, 0:k], cur[:, :, 0:k])
                done(tt(nxt[:, :, k:], cur[:, :, k:], cur[:, :, 0:TT - k], ALU.add))
                cur, k = nxt, 2 * k
            run = cur
            before = et[2]
            done(tt(before, run, tot, ALU.subtract))
            done(tt(et[3], run[:, :, TT - 1:TT].to_broadcast([P, NE, TT]), cst("tile_limit").unsqueeze(1).to_broadcast([P, NE, TT]), ALU.is_gt))
            tiles, first, first_row = rsmall[:, 1, 0:NE], rsmall[:, 2, 0:NE], rsmall[:, 3, 0:NE]
            done(v.tensor_reduce(tiles, et[3], X, ALU.add))
            square = small[7].rearrange("p t e -> p (t e)")[:, 0:NE * NE].rearrange("p (a b) -> p a b", a=NE)
            done(tt(square, tiles.unsqueeze(1).to_broadcast([P, NE, NE]), cst("earlier").rearrange("p (a b) -> p a b", a=NE), ALU.mult))
            done(v.tensor_reduce(first, square, X, ALU.add))
            done(v.tensor_scalar(first_row, first, float(P), None, ALU.mult))
            base = et[3]
            done(tt(base, before, first_row.unsqueeze(2).to_broadcast([P, NE, TT]), ALU.add))
            row_te = small[8]
            done(tt(row_te, ps_f[:, 0, 0:TT * NE].rearrange("p (t e) -> p t e", e=NE), base.rearrange("p e t -> p t e"), ALU.add))
            done(tt(row_te, row_te, hot, ALU.mult))
            row = rsmall[:, 4, 0:TT]
            done(v.tensor_reduce(row, row_te, X, ALU.add))
            row_i, tile_i, in_tile_i = (rsmall[:, k, 0:TT].bitcast(I32) for k in (5, 6, 7))
            tile_f, in_tile_f = rsmall[:, 8, 0:TT], rsmall[:, 9, 0:TT]
            done(v.tensor_copy(row_i, row))
            done(v.tensor_scalar(tile_i, row_i, 7, None, ALU.logical_shift_right))
            done(v.tensor_scalar(in_tile_i, row_i, P - 1, None, ALU.bitwise_and))
            done(v.tensor_copy(tile_f, tile_i))
            done(v.tensor_copy(in_tile_f, in_tile_i))
            done(tt(row_hot, cst("row").unsqueeze(1).to_broadcast([P, TT, P]), in_tile_f.unsqueeze(2).to_broadcast([P, TT, P]), ALU.is_equal))
            done(tt(tile_hot[:, :, 0, :], cst("tile_no").unsqueeze(1).to_broadcast([P, TT, NT + 1]),
                    tile_f.unsqueeze(2).to_broadcast([P, TT, NT + 1]), ALU.is_equal))
            done(tt(tile_hot[:, :, 1, :], tile_hot[:, :, 0, :], cst("token").unsqueeze(2).to_broadcast([P, TT, NT + 1]), ALU.mult))
            assert count[0] == R_ONE_HOTS, count[0]
            nt1 = NT + 1
            cmp = arena[:, hot_at + 6656:hot_at + 6656 + nt1 * NE].rearrange("p (j e) -> p j e", e=NE)
            te = rsmall[:, 10, 0:nt1]
            done(tt(cmp, cst("tile_no").unsqueeze(2).to_broadcast([P, nt1, NE]), first.unsqueeze(1).to_broadcast([P, nt1, NE]), ALU.is_ge))
            done(v.tensor_reduce(te, cmp, X, ALU.add))
            done(v.tensor_scalar(tile_expert[:], te, -1.0, None, ALU.add))
            dve.wait_ge(r_pe, 2)
            pad = rsmall[:, 11, 0:nt1]
            done(v.tensor_scalar(pad, ps_v[:, 0:nt1], -float(OUT_OF_RANGE), float(OUT_OF_RANGE), ALU.mult, ALU.add))
            done(v.tensor_copy(routed[:, 0, :], ps_v[:, nt1:2 * nt1]))
            done(tt(routed[:, 1, :], ps_v[:, nt1:2 * nt1], pad, ALU.add))
            assert count[0] == R_DONE, count[0]

        def tiles(eng, first, iteration, last):
            first()
            for j in range(8):
                iteration(j, j // 2, j % 2)
            with eng.Fori(4, (NT - 1) // 2) as k:
                for d in range(2):
                    iteration(2 * k + d, k, d)
            last()

        def pe_up(pe, j, d):
            e = pe.value_load(tile_expert[0:1, bass.ds(j, 1)], min_val=0, max_val=NE - 1)
            wait_rows(pe, j, d)
            wait(pe, up_act, j - 1, "gT")
            for c in range(C):
                last = nc.tensor.transpose(ps_f[:, 0, c * P:(c + 1) * P], got[:, d, c * P:(c + 1) * P], ident)
            last.then_inc(up_pe.sem, 1)
            if isinstance(j, int) and j < NE:
                pe.wait_ge(w_ready[j], 64)
            wait(pe, up_act, j, "gT")
            wait(pe, m_dve, j - 2, "ub")
            for half in range(2):
                for c in range(C):
                    a = c * 2 * HID + half * HID
                    last = nc.tensor.matmul(ps_s[:, d, half * HID:(half + 1) * HID], gT[:, d, c, :],
                                            wex[:, bass.ds(e, 1), a:a + HID].rearrange("p x n -> p (x n)"),
                                            start=(c == 0), stop=(c == C - 1))
            last.then_inc(up_pe.sem, 1)
            return e

        def pe_down(pe, j, d, e):
            wait(pe, m_dve, j, "act")
            wait(pe, down_act, j - 1, "aT")
            for c in range(HID // P):
                last = nc.tensor.transpose(ps_f[:, 1, c * P:(c + 1) * P], act_[:, d, c * P:(c + 1) * P], ident)
            last.then_inc(down_pe.sem, 1)
            wait(pe, down_act, j, "aT")
            wait(pe, m_dve, j - 2, "y_b2")
            for c in range(HID // P):
                a = C * 2 * HID + c * D
                last = nc.tensor.matmul(y_bank(d), actT[:, d, c * P:(c + 1) * P],
                                        wex[:, bass.ds(e, 1), a:a + D].rearrange("p x n -> p (x n)"),
                                        start=(c == 0), stop=(c == HID // P - 1))
            last.then_inc(down_pe.sem, 1)

        def y_bank(d):
            return ps_v[:, 0:D] if d else ps_b[:, 0:D]

        def wait_rows(eng, j, d):
            eng.wait_ge(rows_got[d], ((j - d) // 2) * 16 + 16)

        def pe_moe(pe):
            pe.wait_ge(r_dve, R_DONE)

            def step(j, k, d):
                pe_up(pe, j + 1, 1 - d)
                e = pe.value_load(tile_expert[0:1, bass.ds(j, 1)], min_val=0, max_val=NE - 1)
                pe_down(pe, j, d, e)

            def last():
                e = pe.value_load(tile_expert[0:1, NT - 1:NT], min_val=0, max_val=NE - 1)
                pe_down(pe, NT - 1, 0, e)

            tiles(pe, lambda: pe_up(pe, 0, 0), step, last)

        def act_moe(act):
            act.wait_ge(r_dve, R_DONE)

            def up(j, d):
                wait(act, up_pe, j, "gT")
                wait(act, up_pe, j - 2, "u")
                nc.scalar.activation(gT[:, d, :, :].rearrange("p c n -> p (c n)"), ps_f[:, 0, 0:C * P], ACT.Copy).then_inc(up_act.sem, 1)
                wait(act, m_dve, j - 2, "y")
                wait_rows(act, j, d)
                nc.scalar.activation(res[:, d, :], got[:, d, D:2 * D], ACT.Copy).then_inc(up_act.sem, 1)

            def down(j, d):
                wait(act, m_dve, j, "ub")
                wait(act, m_dve, j - 2, "act")
                nc.scalar.activation(sg[:, d, :], ub[:, d, HID:2 * HID], ACT.Sigmoid).then_inc(down_act.sem, 1)
                wait(act, down_pe, j, "aT")
                wait(act, down_pe, j - 2, "y")
                nc.scalar.activation(actT[:, d, :], ps_f[:, 1, :], ACT.Copy).then_inc(down_act.sem, 1)

            def step(j, k, d):
                up(j + 1, 1 - d)
                down(j, d)

            tiles(act, lambda: up(0, 0), step, lambda: down(NT - 1, 0))

        def dve_moe(dve):
            def step(j, k, d):
                if isinstance(j, int) and j < NE:
                    dve.wait_ge(w_ready[j], 64)
                e = dve.value_load(tile_expert[0:1, bass.ds(j, 1)], min_val=0, max_val=NE - 1)
                wait(dve, up_pe, j, "u")
                nc.vector.tensor_tensor(ub[:, d, :], ps_s[:, d, :], b1[:, bass.ds(e, 1), :].rearrange("p x n -> p (x n)"), ALU.add).then_inc(m_dve.sem, 1)
                wait(dve, down_act, j, "sig")
                wait(dve, down_pe, j - 2, "aT")
                nc.vector.tensor_tensor(act_[:, d, :], ub[:, d, 0:HID], sg[:, d, :], ALU.mult).then_inc(m_dve.sem, 1)
                wait(dve, down_pe, j, "y")
                stored(dve, k - 1, d)
                nc.vector.tensor_tensor(yo[:, d, :], y_bank(d), b2[:, bass.ds(e, 1), :].rearrange("p x n -> p (x n)"), ALU.add).then_inc(m_dve.sem, 1)
                wait(dve, m_dve, j, "y_b2")
                wait(dve, up_act, j, "res")
                nc.vector.tensor_tensor(yo[:, d, :], yo[:, d, :], res[:, d, :], ALU.add).then_inc(m_dve.sem, 1)

            tiles(dve, lambda: None, step, lambda: step(NT - 1, (NT - 1) // 2, 0))

        def stored(eng, k, d):
            if isinstance(k, int) and k < 0:
                return
            eng.wait_ge(out_stored[d], k * 16 + 16)

        def pool_routing(pool):
            pool.wait_ge(r_dve, R_DONE)

        def pool_moe(pool):
            def gather(j, k, d):
                if not (isinstance(k, int) and k < 1):
                    pool.wait_ge(rows_got[d], k * 16)
                wait(pool, up_pe, j - 2, "gT")
                wait(pool, up_act, j - 2, "res")
                nc.gpsimd.tensor_copy(rows_in[:, d, :], routed[:, 0, bass.ds(j, 1)]).then_inc(m_pool.sem, 1)
                wait_apart(pool, m_pool, j, "in")
                nc.gpsimd.indirect_dma_start(out=got[:, d, :], out_offset=None, in_=rows_dram,
                                             in_offset=bass.IndirectOffsetOnAxis(ap=rows_in[:, d, :].bitcast(U32), axis=0)).then_inc(rows_got[d], 16)

            def scatter(j, k, d):
                stored(pool, k - 1, d)
                nc.gpsimd.tensor_copy(rows_out[:, d, :], routed[:, 1, bass.ds(j, 1)]).then_inc(m_pool_out.sem, 1)
                wait(pool, m_pool_out, j, "out")
                wait_apart(pool, m_dve, j, "y")
                nc.gpsimd.indirect_dma_start(out=out, out_offset=bass.IndirectOffsetOnAxis(ap=rows_out[:, d, :].bitcast(U32), axis=0),
                                             in_=yo[:, d, :], in_offset=None, bounds_check=N - 1, oob_is_err=False).then_inc(out_stored[d], 16)

            def step(j, k, d):
                if not (isinstance(j, int) and j + 2 >= NT):
                    gather(j + 2, k + 1, d)
                scatter(j, k, d)

            def first():
                gather(0, 0, 0)
                gather(1, 0, 1)

            first()
            for j in range(8):
                step(j, j // 2, j % 2)
            with pool.Fori(4, (NT - 1) // 2 - 1) as k:
                for d in range(2):
                    step(2 * k + d, k, d)
            for j in range(NT - 3, NT):
                step(j, j // 2, j % 2)
            for d in range(2):
                stored(pool, (NT - 1 - d) // 2, d)




        def bank_free(eng, unit, b):
            prev, ago = before_in_bank(FRONT_PE, FRONT_BANK, unit)
            st, name = front_reader[prev]
            wait(eng, st, b - ago, name)

        def fb(unit):
            return ps_f[:, FRONT_BANK[unit], :]

        def pe_transposes(unit, b, blocks):
            for i, blk in enumerate(blocks):
                last = nc.tensor.transpose(fb(unit)[:, i * P:(i + 1) * P], blk, ident)
            last.then_inc(f_pe.sem, 1)

        def pe_setup(pe):
            pe.wait_ge(loaded, 16 * SETUP_LOADS)
            for g in range(C):
                for c in range(C):
                    last = nc.tensor.matmul(ps_f[:, g, :], cx("c_k")[:, c, g * P:(g + 1) * P], cx("ctx")[:, c, :],
                                            start=(c == 0), stop=(c == C - 1))
            last.then_inc(su_pe, 1)
            for b in range(B):
                bank = ps_s[:, (b % 4) // 2, (b % 2) * 512:(b % 2) * 512 + D]
                if b >= 4:
                    pe.wait_ge(su_dve, 2 + b - 3)
                for x in range(2):
                    for c in range(C):
                        last = nc.tensor.matmul(bank[x * S:(x + 1) * S, :], cx("ctx")[:, c, b * S:(b + 1) * S], cx("c_v")[:, c, :],
                                                start=(c == 0), stop=(c == C - 1))
                last.then_inc(su_pe, 1)

        def pe_front(pe, p, b):
            if p == 1:
                wait(pe, f_dve, b, "xn")
                for c in range(C):
                    bank_free(pe, f"xT{c}", b)
                    pe_transposes(f"xT{c}", b, [xn[:, t, c * P:(c + 1) * P] for t in range(T)])
            if p == 2:
                wait(pe, f_act, b, "xT1")
                for g in range(C):
                    bank_free(pe, f"cq{g}", b)
                    for c in range(C):
                        last = nc.tensor.matmul(fb(f"cq{g}"), w("c_q")[:, c, g * P:(g + 1) * P], xnT[:, c, :],
                                                start=(c == 0), stop=(c == C - 1))
                    last.then_inc(f_pe.sem, 1)

            def scores(t):
                if t == 0:
                    wait(pe, f_dve, b, "cq1")
                    wait(pe, f_pool, b, "kbd")
                for g in range(C):
                    bank_free(pe, f"cs{t}{g}", b)
                    nc.tensor.matmul(fb(f"cs{t}{g}"), cqT[:, g, t * P:(t + 1) * P], kbd[:, g, :, :].rearrange("p h s -> p (h s)"),
                                     start=True, stop=False)
                    nc.tensor.matmul(fb(f"cs{t}{g}").rearrange("p (h s) -> p h s", h=PAIRS), ones3[:],
                                     delta3[:, bass.ds(b * S, S)].unsqueeze(1).to_broadcast([3, PAIRS, S]),
                                     start=False, stop=True).then_inc(f_pe.sem, 1)

            def probs_T(t):
                wait(pe, f_act, b, f"cexp{t}")
                for g in range(2):
                    bank_free(pe, f"cT{t}{g}", b)
                    pe_transposes(f"cT{t}{g}", b, [cs[:, t % 2, (4 * g + i) * P:(4 * g + i + 1) * P] for i in range(4)])

            def attended(t):
                wait(pe, f_act, b, f"cT{t}1")
                bank_free(pe, f"co{t}", b)
                for j in range(PAIRS):
                    last = nc.tensor.matmul(fb(f"co{t}")[:, j * 34:(j + 1) * 34], cpT[:, j, :],
                                            vbd[:, bass.ds(b, 1), j, :, :].rearrange("p a x e -> p (a x e)"), start=True, stop=True)
                last.then_inc(f_pe.sem, 1)

            if p == 3:
                scores(0)
            if p == 4:
                scores(1)
            if p == 5:
                probs_T(0)
                scores(2)
            if p == 6:
                attended(0)
                probs_T(1)
            if p == 7:
                scores(3)
            if p == 8:
                attended(1)
                probs_T(2)
            if p == 9:
                attended(2)
                probs_T(3)
            if p == 10:
                attended(3)
            if p == 11:
                wait(pe, f_dve, b, "co3")
                for c in range(C):
                    bank_free(pe, f"coT{c}", b)
                    pe_transposes(f"coT{c}", b, [co[:, t, c * P:(c + 1) * P] for t in range(T)])
            if p == 12:
                wait(pe, f_act, b, "coT1")
                for k in range(2):
                    bank_free(pe, f"wo{k}", b)
                    for i in range(2):
                        t = 2 * k + i
                        for c in range(C):
                            last = nc.tensor.matmul(fb(f"wo{k}")[:, i * D:(i + 1) * D], coT[:, c, t * P:(t + 1) * P], w("c_o")[:, c, :],
                                                    start=(c == 0), stop=(c == C - 1))
                    last.then_inc(f_pe.sem, 1)
            if p == 14:
                wait(pe, f_act, b, "h")
                for c in range(C):
                    bank_free(pe, f"hT{c}", b)
                    pe_transposes(f"hT{c}", b, [xn[:, t, c * P:(c + 1) * P] for t in range(T)])
            if p in (15, 16):
                wait(pe, f_act, b, "hT1")
                for t in (2 * (p - 15), 2 * (p - 15) + 1):
                    bank_free(pe, f"qkv{t}", b)
                    for c in range(C):
                        last = nc.tensor.matmul(fb(f"qkv{t}")[:, 0:QKV], xnT[:, c, t * P:(t + 1) * P], w("qkv")[:, c, :],
                                                start=(c == 0), stop=(c == C - 1))
                    last.then_inc(f_pe.sem, 1)
            if p in (20, 23):
                m = int(p == 23)
                wait(pe, f_dve, b, f"lo{m}")
                for n in ST_UNITS[5 * m:5 * m + 5]:
                    bank_free(pe, n, b)
                    i = 8 if n[2] == "k" else 2 * (int(n[3]) % 4)
                    pe_transposes(n, b, [stack[:, t, i:i + 2, :, :].rearrange("p x k e -> p (x k e)") for t in range(T)])

        def pe_scores(pe, b, s, u):
            n = 3 * s + u
            if u == 0:
                unit = f"stq{s}"
                wait(pe, *((f_act if unit in ST_ACT else f_dve), b, unit))
                if s % 4 == 0:
                    unit = f"stk{s // 4}"
                    wait(pe, *((f_act if unit in ST_ACT else f_dve), b, unit))
            if n >= 2:
                wait(pe, a_act, b, SCORES[n - 2])
            else:
                wait(pe, a_act, b - 1, SCORES[n - 2])
            m = s // 4
            for x in range(2):
                for kb, col, width in UNITS[u]:
                    a = x * L + col
                    last = nc.tensor.matmul(ps_s[:, n % 2, a:a + width], sk[x * 64:(x + 1) * 64, m, kb * P:(kb + 1) * P],
                                            sq[x * 64:(x + 1) * 64, s, kb * P:kb * P + width], start=True, stop=True)
            last.then_inc(a_pe.sem, 1)

        def pe_attended(pe, b, s):
            wait(pe, a_pool, b, f"s{s}2")
            if s == 0:
                wait(pe, a_dve, b, "v")
                wait(pe, a_dve, b - 1, f"o{PAIRS - 1}")
            else:
                wait(pe, a_dve, b, f"o{s - 1}")
            for qt in range(T):
                for x in range(2):
                    o = (2 * qt + x) * (E + 1)
                    for kb in range(qt + 1):
                        last = nc.tensor.matmul(ps_v[:, o:o + E + 1], pt_block(s, x, kb, qt), v_aug[:, kb, 2 * (s // 4) + x, :],
                                                start=(kb == 0), stop=(kb == qt))
            last.then_inc(a_pe.sem, 1)

        def back_free(eng, unit, b):
            i = BACK_PE.index(unit)
            st, name = back_reader[BACK_PE[i - 1]]
            wait(eng, st, b if i else b - 1, name)

        def pe_back(pe, p, b):
            if p == 0:
                wait(pe, a_dve, b, f"o{PAIRS - 1}")
                for c in range(C):
                    back_free(pe, f"oT{c}", b)
                    for t in range(T):
                        last = nc.tensor.transpose(ps_b[:, t * P:(t + 1) * P], ao[:, t, c * 8:(c + 1) * 8, :].rearrange("p h e -> p (h e)"), ident)
                    last.then_inc(b_pe.sem, 1)
            if p == 2:
                for c in range(C):
                    back_free(pe, f"z{c}", b)
                    nc.tensor.matmul(ps_b[:], wg, aoT[:, c, :], start=True, stop=True).then_inc(b_pe.sem, 1)
            if p == 5:
                wait(pe, b_dve, b, "gated")
                for k in range(2):
                    back_free(pe, f"wo{k}", b)
                    for i in range(2):
                        t = 2 * k + i
                        for c in range(C):
                            last = nc.tensor.matmul(ps_b[:, i * D:(i + 1) * D], aoT[:, c, t * P:(t + 1) * P], w("f_o")[:, c, :],
                                                    start=(c == 0), stop=(c == C - 1))
                    last.then_inc(b_pe.sem, 1)
            if p == 10:
                wait(pe, b_pool, b, "h2w")
                for c in range(C):
                    back_free(pe, f"hT{c}", b)
                    for t in range(T):
                        last = nc.tensor.transpose(ps_b[:, t * P:(t + 1) * P], h2[:, t, c * P:(c + 1) * P], ident)
                    last.then_inc(b_pe.sem, 1)
            if p == 12:
                back_free(pe, "lg", b)
                for t in range(T):
                    for c in range(C):
                        last = nc.tensor.matmul(ps_b[:, t * NE:(t + 1) * NE], h2T[:, c, t * P:(t + 1) * P], w("r")[:, c, :],
                                                start=(c == 0), stop=(c == C - 1))
                last.then_inc(b_pe.sem, 1)

        def pe_iteration(pe, i, front, attn, back):
            for s in range(PAIRS):
                for u in range(3):
                    if attn:
                        pe_scores(pe, i, s, u)
                        if u == 2 and s:
                            pe_attended(pe, i, s - 1)
                    if back:
                        pe_back(pe, 3 * s + u, i - 1)
                    if front:
                        pe_front(pe, 3 * s + u, i + 1)
            if attn:
                pe_attended(pe, i, PAIRS - 1)

        def pipeline(eng, iteration):
            iteration(eng, -1, True, False, False)
            iteration(eng, 0, True, True, False)
            iteration(eng, 1, True, True, True)
            with eng.Fori(2, B - 1) as i:
                iteration(eng, i, True, True, True)
            iteration(eng, B - 1, False, True, True)
            iteration(eng, B, False, False, True)

        def act_evacuate(dst, unit, b, first=None):
            wait(nc.scalar, f_pe, b, unit)
            nc.scalar.activation(dst, fb(unit), ACT.Copy).then_inc(f_act.sem, 1)

        def act_front(act, p, b):
            if p == 1:
                wait(act, f_pe, b - 1, "qkv3")
                act_evacuate(xnT[:, 0, :], "xT0", b)
                act_evacuate(xnT[:, 1, :], "xT1", b)

            def exps(t):
                wait(act, f_dve, b, f"csub{t}1")
                nc.scalar.activation(cs[:, t % 2, :], cs[:, t % 2, :], ACT.Exp).then_inc(f_act.sem, 1)

            def probs_T(t):
                if t:
                    wait(act, f_pe, b, f"co{t - 1}")
                else:
                    wait(act, f_pe, b - 1, f"co{T - 1}")
                for g in range(2):
                    act_evacuate(cpT[:, 4 * g:4 * g + 4, :].rearrange("p j q -> p (j q)"), f"cT{t}{g}", b)

            if p == 4:
                exps(0)
            if p == 5:
                exps(1)
                probs_T(0)
            if p == 6:
                exps(2)
                probs_T(1)
            if p == 8:
                exps(3)
                probs_T(2)
            if p == 9:
                probs_T(3)
            if p == 11:
                wait(act, f_pe, b - 1, "wo1")
                for c in range(C):
                    act_evacuate(coT[:, c, :], f"coT{c}", b)
            if p == 13:
                wait(act, f_dve, b, "y")
                wait(act, f_pool, b, "rms")
                for t in range(T):
                    last = nc.scalar.activation(xn[:, t, :], y[:, bass.ds(b % 2, 1), t, :].rearrange("p a d -> p (a d)"), ACT.Copy,
                                                scale=tiny[:, 5, t:t + 1])
                last.then_inc(f_act.sem, 1)
            if p == 14:
                for c in range(C):
                    act_evacuate(xnT[:, c, :], f"hT{c}", b)
            if p in (20, 23):
                m = int(p == 23)
                for n in ST_UNITS[5 * m:5 * m + 5]:
                    if n in ST_ACT:
                        st_evacuate(act, n, b)

        def st_evacuate(eng, n, b):
            wait(eng, f_pe, b, n)
            if n[2] == "k":
                m = int(n[3])
                wait(eng, a_pe, b - 1, f"s{4 * m + 3}2")
                dst = sk[:, m, :]
            else:
                s = int(n[3])
                wait(eng, a_pe, b - 1, f"s{s}2")
                dst = sq[:, s, :]
            if n in ST_ACT:
                nc.scalar.activation(dst, fb(n), ACT.Copy).then_inc(f_act.sem, 1)
            else:
                nc.vector.tensor_copy(dst, fb(n)).then_inc(f_dve.sem, 1)

        def act_attn(act, b, s, u):
            n = 3 * s + u
            wait(act, a_pe, b, f"s{s}{u}")
            if u == 0:
                wait(act, a_pe, *((b, f"pv{s - 2}") if s >= 2 else (b - 1, f"pv{PAIRS - 2 + s}")))
            nc.scalar.activation(pt[:, s % 2, UNIT_AT[u]:UNIT_AT[u] + 2 * UNIT_W[u]].rearrange("p (x n) -> p x n", x=2),
                                 ps_s[:, n % 2, :].rearrange("p (x n) -> p x n", x=2)[:, :, 0:UNIT_W[u]],
                                 ACT.Exp, scale=SCALE).then_inc(a_act.sem, 1)

        def act_back(act, p, b):
            if p == 0:
                wait(act, b_pe, b - 1, "wo1")
                for c in range(C):
                    wait(act, b_pe, b, f"oT{c}")
                    nc.scalar.activation(aoT[:, c, :], ps_b[:], ACT.Copy).then_inc(b_act.sem, 1)
            if p == 2:
                wait(act, b_dve, b - 1, "gated")
                for c in range(C):
                    wait(act, b_pe, b, f"z{c}")
                    nc.scalar.activation(gate[:, c, :], ps_b[:], ACT.Exp, bias=tiny[:, 6, 0:1], scale=-1.0).then_inc(b_act.sem, 1)
            if p == 10:
                wait(act, b_pe, b - 1, "lg")
                for c in range(C):
                    wait(act, b_pe, b, f"hT{c}")
                    nc.scalar.activation(h2T[:, c, :], ps_b[:], ACT.Copy).then_inc(b_act.sem, 1)

        def act_iteration(act, i, front, attn, back):
            for s in range(PAIRS):
                for u in range(3):
                    if attn:
                        act_attn(act, i, s, u)
                    if back:
                        act_back(act, 3 * s + u, i - 1)
                    if front:
                        act_front(act, 3 * s + u, i + 1)


        def dve_setup(dve):
            count = [0]

            def done(inst, then=True):
                count[0] += 1
                inst.then_inc(su_dve, 1)
                if then:
                    dve.wait_ge(su_dve, count[0])

            dve.wait_ge(loaded, 16 * SETUP_LOADS)
            dve.wait_ge(su_pe, 1)
            for g in range(C):
                done(nc.vector.tensor_scalar(kT[:, g, :], ps_f[:, g, :], prm("c_bk")[:, g:g + 1], None, ALU.add), False)
            for b in range(B):
                dve.wait_ge(su_pe, 2 + b)
                bank = ps_s[:, (b % 4) // 2, (b % 2) * 512:(b % 2) * 512 + D]
                if b >= 2:
                    dve.wait_ge(su_pool, 2 + b)
                done(nc.vector.tensor_tensor(xn[:, 2 + b % 2, :], bank, prm("c_bv"), ALU.add), False)
            done(nc.vector.tensor_tensor(wgt[:, :, WGT["qkv"][0]:WGT["qkv"][0] + QKV], w("qkv"),
                                    prm("ln1").unsqueeze(2).to_broadcast([P, C, QKV]), ALU.mult))
            done(nc.vector.tensor_tensor(wg, prm("Wg"), cst("same_head"), ALU.mult))
            done(nc.vector.tensor_scalar(tiny[:, 6, 0:1], prm("bg"), -1.0, None, ALU.mult))
            done(nc.vector.tensor_scalar(delta_r, delta_r, SCALE, None, ALU.mult))
            done(nc.vector.tensor_copy(delta_parts[:, 0, :], delta_r))
            done(nc.vector.tensor_tensor(delta_s, delta_r, delta_parts[:, 0, :], ALU.subtract))
            done(nc.vector.tensor_copy(delta_parts[:, 1, :], delta_s))
            done(nc.vector.tensor_tensor(delta_r, delta_s, delta_parts[:, 1, :], ALU.subtract))
            done(nc.vector.tensor_copy(delta_parts[:, 2, :], delta_r))
            done(nc.vector.tensor_scalar(delta_s, delta_parts[:, 0, :], cst("part", 3)[:, 0:1], None, ALU.mult))
            done(nc.vector.scalar_tensor_tensor(delta_r, delta_parts[:, 1, :], cst("part", 3)[:, 1:2], delta_s, ALU.mult, ALU.add))
            done(nc.vector.scalar_tensor_tensor(delta3[:], delta_parts[:, 2, :], cst("part", 3)[:, 2:3], delta_r, ALU.mult, ALU.add))
            dve.wait_ge(su_pool, 3 + B + 1)
            done(nc.vector.memset(ones3[:], 1.0))
            assert count[0] == SETUP_DVE

        def dve_stats(dve, k, src, b, st, names):
            for t in range(T):
                last = nc.vector.bn_stats(stats[:, k, t, :], src(t))
            last.then_inc(st.sem, 1)
            wait_apart(dve, st, b, names[0])
            for t in range(T):
                last = nc.vector.bn_aggr(mv[:, k, t, :], stats[:, k, t, :])
            last.then_inc(st.sem, 1)

        def dve_front(dve, p, b):
            if p == 0:
                dve.wait_ge(x_loaded, b * 16 + 16)
                wait(dve, f_pool, b - 1, "ln1_eps")
                dve_stats(dve, 0, lambda t: x_in[:, t, :], b, f_dve, ["ln1_stats"])
                wait(dve, f_pool, b, "ln1_rstd")
                wait(dve, f_pe, b - 1, "hT1")
                for t in range(T):
                    last = nc.vector.tensor_scalar(xn[:, t, :], x_in[:, t, :], mv[:, 0, t, 0:1], tiny[:, 1, t:t + 1], ALU.subtract, ALU.mult)
                last.then_inc(f_dve.sem, 1)
            if p == 2:
                wait(dve, f_pe, b - 1, "cs31")
                for g in range(C):
                    wait(dve, f_pe, b, f"cq{g}")
                    nc.vector.tensor_scalar(cqT[:, g, :], fb(f"cq{g}"), prm("c_bq")[:, g:g + 1], prm("tau")[:, bass.ds(b, 1)],
                                            ALU.add, ALU.mult).then_inc(f_dve.sem, 1)

            def softmax_shift(t):
                wait(dve, f_pe, b, f"cs{t}1")
                nc.vector.tensor_reduce(cmax[:, t % 2, :], ps_f[:].rearrange("p g (h s) -> p (g h) s", h=PAIRS), X, ALU.max).then_inc(f_dve.sem, 1)
                wait(dve, f_dve, b, f"cmax{t}")
                wait(dve, f_pe, *((b, f"cT{t - 2}1") if t >= 2 else (b - 1, f"cT{t + 2}1")))
                for g in range(C):
                    nc.vector.tensor_tensor(cs[:, t % 2, g * L:(g + 1) * L].rearrange("p (h s) -> p h s", h=PAIRS),
                                            ps_f[:, g, :].rearrange("p (h s) -> p h s", h=PAIRS),
                                            cmax[:, t % 2, g * PAIRS:(g + 1) * PAIRS].unsqueeze(2).to_broadcast([P, PAIRS, S]),
                                            ALU.subtract).then_inc(f_dve.sem, 1)

            def normalise(t):
                wait(dve, f_pe, b, f"co{t}")
                num = fb(f"co{t}")[:, 0:PAIRS * 34].rearrange("p (h e) -> p h e", e=E + 1)
                nc.vector.reciprocal(crec, num[:, :, E]).then_inc(f_dve.sem, 1)
                wait(dve, f_dve, b, f"crec{t}")
                if t == 0:
                    wait(dve, f_pe, b - 1, "coT1")
                nc.vector.tensor_tensor(co[:, t, :].rearrange("p (h e) -> p h e", e=E), num[:, :, 0:E],
                                        crec.unsqueeze(2).to_broadcast([P, H, E]), ALU.mult).then_inc(f_dve.sem, 1)

            if p == 3:
                softmax_shift(0)
            if p == 4:
                softmax_shift(1)
            if p == 5:
                softmax_shift(2)
            if p == 6:
                normalise(0)
            if p == 7:
                softmax_shift(3)
            if p == 8:
                normalise(1)
            if p == 9:
                normalise(2)
            if p == 10:
                normalise(3)
            if p == 12:
                wait(dve, f_pool, b, "xbo")
                if isinstance(b, int) and b < 2:
                    pass
                else:
                    dve.wait_ge(rows_stored, (b - 1) * 32)
                for k in range(2):
                    wait(dve, f_pe, b, f"wo{k}")
                    nc.vector.tensor_tensor(x1[:, bass.ds(b % 2, 1), 2 * k:2 * k + 2, :].rearrange("p a t d -> p (a t) d"),
                                            fb(f"wo{k}").rearrange("p (t d) -> p t d", t=2), x_in[:, 2 * k:2 * k + 2, :],
                                            ALU.add).then_inc(f_dve.sem, 1)
                wait(dve, f_dve, b, "x1_1")
                wait_apart(dve, f_pool, b - 1, "meansq")
                dve_stats(dve, 1, lambda t: x1[:, bass.ds(b % 2, 1), t, :].rearrange("p a d -> p (a d)"), b, f_dve, ["ln2_stats"])
                wait(dve, f_pool, b, "ln2_rstd")
                wait(dve, b_pool, b - 2, "res")
                for t in range(T):
                    last = nc.vector.tensor_scalar(y[:, bass.ds(b % 2, 1), t, :].rearrange("p a d -> p (a d)"),
                                                   x1[:, bass.ds(b % 2, 1), t, :].rearrange("p a d -> p (a d)"),
                                                   mv[:, 1, t, 0:1], tiny[:, 3, t:t + 1], ALU.subtract, ALU.mult)
                last.then_inc(f_dve.sem, 1)
            if p in (15, 16):
                if p == 15:
                    wait(dve, a_dve, b - 1, "v")
                    wait(dve, f_pool, b - 1, "sin2")
                for t in (2 * (p - 15), 2 * (p - 15) + 1):
                    wait(dve, f_pe, b, f"qkv{t}")
                    nc.vector.tensor_tensor(qkv[:, t, :], fb(f"qkv{t}")[:, 0:QKV], prm("bqkv"), ALU.add).then_inc(f_dve.sem, 1)
            qk = qkv[:, :, 0:HS * E].rearrange("p t (h e) -> p t h e", e=E)
            ra = rope_a[:, :, :].rearrange("p t (h e) -> p t h e", e=E)
            flat_a = rope_a[:, :, :].rearrange("p t n -> p (t n)")
            flat_b = rope_b[:, :, :].rearrange("p t n -> p (t n)")
            if p == 17:
                wait(dve, f_dve, b, "qkv3")
                cos = cst("cos").rearrange("p (t e) -> p t e", t=T)
                for half in range(2):
                    last = nc.vector.tensor_tensor(ra[:, :, :, 8 * half:8 * half + 8], qk[:, :, :, 8 * half:8 * half + 8],
                                                   cos.unsqueeze(2).to_broadcast([P, T, HS, 8]), ALU.mult)
                last.then_inc(f_dve.sem, 1)
                wait(dve, f_dve, b, "cosmul")
                wait(dve, f_pool, b, "sin2")
                nc.vector.tensor_tensor(flat_a, flat_a, flat_b, ALU.add).then_inc(f_dve.sem, 1)
                wait(dve, f_dve, b, "rope")
                nc.vector.tensor_tensor(flat_b, flat_a, flat_a, ALU.mult).then_inc(f_dve.sem, 1)
                wait(dve, f_dve, b, "square")
                nc.vector.tensor_reduce(qk_ms, flat_b.rearrange("p (h e) -> p h e", e=E), X, ALU.add).then_inc(f_dve.sem, 1)
            if p == 18:
                wait(dve, f_pool, b, "qk_rstd")
                nc.vector.tensor_tensor(flat_b.rearrange("p (h e) -> p h e", e=E), flat_a.rearrange("p (h e) -> p h e", e=E),
                                        qk_rs.unsqueeze(2).to_broadcast([P, T * HS, E]), ALU.mult).then_inc(f_dve.sem, 1)
                wait(dve, f_dve, b, "qnorm")
                nc.vector.tensor_tensor(rope_a[:, :, :], rope_b[:, :, :], prm("qkn").unsqueeze(1).to_broadcast([P, T, HS * E]),
                                        ALU.mult).then_inc(f_dve.sem, 1)
                wait(dve, f_dve, b, "qweight")
            if p in (19, 21):
                m = int(p == 21)
                if m:
                    wait(dve, f_pe, b, "stq3")
                else:
                    wait(dve, f_pe, b - 1, "stq7")
                q = ra[:, :, 8 * m:8 * m + 8, :]
                k = ra[:, :, 16 + 2 * m:18 + 2 * m, :]
                sq_, sk_ = stack[:, :, 0:8, :, :], stack[:, :, 8:10, :, :]
                for t in range(T):
                    nc.vector.tensor_scalar(sq_[:, t, :, 0:2, :].bitcast(I32), q[:, t].unsqueeze(2).to_broadcast([P, 8, 2, E]).bitcast(I32),
                                            HI_MASK, None, ALU.bitwise_and)
                    last = nc.vector.tensor_scalar(sk_[:, t, :, 0:3:2, :].bitcast(I32), k[:, t].unsqueeze(2).to_broadcast([P, 2, 2, E]).bitcast(I32),
                                                   HI_MASK, None, ALU.bitwise_and)
                last.then_inc(f_dve.sem, 1)
                wait(dve, f_dve, b, f"hi{m}")
                for t in range(T):
                    nc.vector.tensor_tensor(sq_[:, t, :, 2:4, :], q[:, t].unsqueeze(2).to_broadcast([P, 8, 2, E]), sq_[:, t, :, 0:2, :], ALU.subtract)
                    last = nc.vector.tensor_tensor(sk_[:, t, :, 1:4:2, :], k[:, t].unsqueeze(2).to_broadcast([P, 2, 2, E]), sk_[:, t, :, 0:3:2, :], ALU.subtract)
                last.then_inc(f_dve.sem, 1)
            if p in (20, 23):
                m = int(p == 23)
                for n in ST_UNITS[5 * m:5 * m + 5]:
                    if n not in ST_ACT:
                        st_evacuate(dve, n, b)

        def dve_values(dve, b):
            wait(dve, f_dve, b, "qkv3")
            wait(dve, a_pe, b - 1, f"pv{PAIRS - 1}")
            for t in range(T):
                last = nc.vector.tensor_copy(v_aug[:, t, :, 0:E], qkv[:, t, HS * E:].rearrange("p (g e) -> p g e", e=E))
            last.then_inc(a_dve.sem, 1)

        def dve_normalise(dve, b, s):
            wait(dve, a_pe, b, f"pv{s}")
            sums = ps_v[:, 0:2 * T * (E + 1)].rearrange("p (a e) -> p a e", e=E + 1)
            nc.vector.reciprocal(prec, sums[:, :, E]).then_inc(a_dve.sem, 1)
            wait(dve, a_dve, b, f"rec{s}")
            if s == 0:
                wait(dve, b_pe, b - 1, "oT1")
            nc.vector.tensor_tensor(ao[:, :, 2 * s:2 * s + 2, :], sums[:, :, 0:E].rearrange("p (t x) e -> p t x e", x=2),
                                    prec.rearrange("p (t x) -> p t x", x=2).unsqueeze(3).to_broadcast([P, T, 2, E]),
                                    ALU.mult).then_inc(a_dve.sem, 1)

        def dve_back(dve, p, b):
            fg, fa = gate[:, :, :].rearrange("p c n -> p (c n)"), aoT[:, :, :].rearrange("p c n -> p (c n)")
            if p == 3:
                wait(dve, b_act, b, "e1")
                nc.vector.tensor_scalar(fg, fg, 1.0, None, ALU.add).then_inc(b_dve.sem, 1)
                wait(dve, b_dve, b, "e1p")
                nc.vector.reciprocal(fg, fg).then_inc(b_dve.sem, 1)
                wait(dve, b_dve, b, "gate")
                nc.vector.tensor_tensor(fa, fa, fg, ALU.mult).then_inc(b_dve.sem, 1)
            yb = y[:, bass.ds(b % 2, 1), :, :].rearrange("p a t d -> p (a t) d")
            if p == 5:
                wait(dve, f_pool, b, "ybo")
                for k in range(2):
                    wait(dve, b_pe, b, f"wo{k}")
                    nc.vector.tensor_tensor(yb[:, 2 * k:2 * k + 2, :], ps_b[:].rearrange("p (t d) -> p t d", t=2), yb[:, 2 * k:2 * k + 2, :],
                                            ALU.add).then_inc(b_dve.sem, 1)
                wait(dve, b_dve, b, "in1")
                wait_apart(dve, b_pool, b - 1, "ms")
                dve_stats(dve, 2, lambda t: yb[:, t, :], b, b_dve, ["stats"])
            if p == 7:
                wait(dve, b_pool, b, "rms")
                wait(dve, b_pe, b - 1, "hT1")
                if not (isinstance(b, int) and b < 1):
                    dve.wait_ge(rows_stored, b * 32)
                for t in range(T):
                    last = nc.vector.tensor_scalar(h2[:, t, :], yb[:, t, :], tiny[:, 10, t:t + 1], None, ALU.mult)
                last.then_inc(b_dve.sem, 1)
            if p == 12:
                wait(dve, b_pe, b, "lg")
                nc.vector.tensor_tensor(logits[:, bass.ds(b * T, T), :], ps_b[:, 0:T * NE].rearrange("p (t e) -> p t e", t=T),
                                        prm("br").unsqueeze(1).to_broadcast([P, T, NE]), ALU.add).then_inc(b_dve.sem, 1)

        def dve_iteration(dve, i, front, attn, back):
            for s in range(PAIRS):
                for u in range(3):
                    if attn:
                        if s == 0 and u == 0:
                            dve_values(dve, i)
                        if u == 2 and s:
                            dve_normalise(dve, i, s - 1)
                    if back:
                        dve_back(dve, 3 * s + u, i - 1)
                    if front:
                        dve_front(dve, 3 * s + u, i + 1)
            if attn:
                dve_normalise(dve, i, PAIRS - 1)

        def pool_setup(pool):
            nc.gpsimd.memset(half_power[:], -0.5).then_inc(su_pool, 1)
            nc.gpsimd.memset(v_aug, 1.0).then_inc(su_pool, 1)
            pool.wait_ge(loaded, 16 * SETUP_LOADS)
            half = cst("half")
            nc.gpsimd.tensor_copy(vbd[:, :, :, :, E].rearrange("p b j x -> p (b j) x"),
                                  half.unsqueeze(1).to_broadcast([P, B * PAIRS, 2])).then_inc(su_pool, 1)
            for b in range(B):
                pool.wait_ge(su_dve, 3 + b)
                nc.gpsimd.tensor_tensor(vbd[:, b, :, :, 0:E], xn[:, 2 + b % 2, :].rearrange("p (j x e) -> p j x e", x=2, e=E),
                                        half.unsqueeze(1).unsqueeze(3).to_broadcast([P, PAIRS, 2, E]), ALU.mult).then_inc(su_pool, 1)
            pool.wait_ge(su_dve, 2)
            nc.gpsimd.tensor_scalar(kT.rearrange("p c n -> p (c n)"), kT.rearrange("p c n -> p (c n)"), SCALE, 0.0,
                                    ALU.mult, ALU.add).then_inc(su_pool, 1)

        def pool_front(pool, p, b):
            def ew(dst, a, c, op):
                nc.gpsimd.tensor_tensor(dst, a, c, op).then_inc(f_pool.sem, 1)

            hp = half_power[:, 0:T]
            if p == 0:
                if isinstance(b, int) and b == 0:
                    pool.wait_ge(su_pool, 4 + B)
                    pool.wait_ge(su_dve, SETUP_DVE)
                wait(pool, f_pe, b - 1, "cs31")
                for g in range(C):
                    last = nc.gpsimd.tensor_tensor(kbd[:, g, :, :], kT[:, g, bass.ds(b * S, S)].unsqueeze(1).to_broadcast([P, PAIRS, S]),
                                                   cst("head_of").unsqueeze(2).to_broadcast([P, PAIRS, S]), ALU.mult)
                last.then_inc(f_pool.sem, 1)
                wait(pool, f_dve, b, "ln1_aggr")
                wait_apart(pool, f_dve, b - 1, "xn")
                nc.gpsimd.tensor_scalar(tiny[:, 0, :], mv[:, 0, :, 1], LN_EPS, 1.0, ALU.add, ALU.mult).then_inc(f_pool.sem, 1)
                wait(pool, f_pool, b, "ln1_eps")
                ew(tiny[:, 1, :], tiny[:, 0, :], hp, ALU.pow)
                wait(pool, f_dve, b, "xn")
                ew(x_in, x_in, prm("c_bo").unsqueeze(1).to_broadcast([P, T, D]), ALU.add)
            if p == 12:
                wait(pool, f_dve, b, "ln2_aggr")
                wait_apart(pool, f_act, b - 1, "h")
                nc.gpsimd.tensor_scalar(tiny[:, 2, :], mv[:, 1, :, 1], LN_EPS, 1.0, ALU.add, ALU.mult).then_inc(f_pool.sem, 1)
                wait(pool, f_pool, b, "ln2_eps")
                ew(tiny[:, 3, :], tiny[:, 2, :], hp, ALU.pow)
                wait(pool, f_pool, b, "ln2_rstd")
                ew(tiny[:, 4, :], tiny[:, 3, :], tiny[:, 3, :], ALU.mult)
                wait(pool, f_pool, b, "rstd2")
                ew(tiny[:, 11, :], tiny[:, 4, :], mv[:, 1, :, 1], ALU.mult)
                wait_apart(pool, f_pool, b, "meansq")
                nc.gpsimd.tensor_scalar(tiny[:, 9, :], tiny[:, 11, :], RMS_EPS, 1.0, ALU.add, ALU.mult).then_inc(f_pool.sem, 1)
                wait(pool, f_pool, b, "meansq_eps")
                ew(tiny[:, 5, :], tiny[:, 9, :], hp, ALU.pow)
            if p == 14:
                wait(pool, f_act, b, "h")
                yb = y[:, bass.ds(b % 2, 1), :, :].rearrange("p a t d -> p (a t) d")
                ew(yb, yb, prm("f_bo").unsqueeze(1).to_broadcast([P, T, D]), ALU.add)
            if p == 17:
                wait(pool, f_dve, b, "qkv3")
                wait(pool, f_dve, b - 1, "qweight")
                qk = qkv[:, :, 0:HS * E].rearrange("p t (h e) -> p t h e", e=E)
                rb = rope_b[:, :, :].rearrange("p t (h e) -> p t h e", e=E)
                for lo, hi, name in ((0, 8, "negsin"), (8, 0, "sin")):
                    ew(rb[:, :, :, lo:lo + 8], qk[:, :, :, hi:hi + 8],
                       cst(name).rearrange("p (t e) -> p t e", t=T).unsqueeze(2).to_broadcast([P, T, HS, 8]), ALU.mult)
            if p == 18:
                wait_apart(pool, f_dve, b, "meansq")
                nc.gpsimd.tensor_scalar(qk_ms, qk_ms, 1.0 / E, RMS_EPS, ALU.mult, ALU.add).then_inc(f_pool.sem, 1)
                wait(pool, f_pool, b, "qk_eps")
                ew(qk_rs, qk_ms, half_power[:], ALU.pow)

        def pool_mask(pool, b, s, u):
            wait(pool, a_act, b, f"s{s}{u}")
            tri = cst("causal")
            v = pt[:, s % 2, UNIT_AT[u]:UNIT_AT[u] + 2 * UNIT_W[u]].rearrange("p (x k q) -> p x k q", x=2, q=P)
            d = v[:, :, 0:4:3, :] if u == 1 else v[:, :, 0:1, :]
            n = d.shape[2]
            nc.gpsimd.tensor_tensor(d, d, tri.unsqueeze(1).unsqueeze(1).to_broadcast([P, 2, n, P]), ALU.mult).then_inc(a_pool.sem, 1)

        def pool_back(pool, p, b):
            def ew(dst, a, c, op):
                nc.gpsimd.tensor_tensor(dst, a, c, op).then_inc(b_pool.sem, 1)

            yb = y[:, bass.ds(b % 2, 1), :, :].rearrange("p a t d -> p (a t) d")
            xb = x1[:, bass.ds(b % 2, 1), :, :].rearrange("p a t d -> p (a t) d")
            if p == 6:
                wait(pool, b_dve, b, "aggr")
                ew(tiny[:, 7, :], mv[:, 2, :, 0], mv[:, 2, :, 0], ALU.mult)
                wait(pool, b_pool, b, "msq")
                ew(tiny[:, 8, :], tiny[:, 7, :], mv[:, 2, :, 1], ALU.add)
                wait_apart(pool, b_pool, b, "ms")
                nc.gpsimd.tensor_scalar(tiny[:, 7, :], tiny[:, 8, :], RMS_EPS, 1.0, ALU.add, ALU.mult).then_inc(b_pool.sem, 1)
                wait(pool, b_pool, b, "ms_eps")
                wait(pool, b_dve, b - 1, "h2")
                ew(tiny[:, 10, :], tiny[:, 7, :], half_power[:, 0:T], ALU.pow)
            if p == 7:
                ew(xb, xb, yb, ALU.add)
            if p == 8:
                wait(pool, b_dve, b, "h2")
                ew(h2, h2, prm("ln2").unsqueeze(1).to_broadcast([P, T, D]), ALU.mult)

        def pool_iteration(pool, i, front, attn, back):
            for s in range(PAIRS):
                for u in range(3):
                    if attn:
                        pool_mask(pool, i, s, u)
                    if back:
                        pool_back(pool, 3 * s + u, i - 1)
                    if front:
                        pool_front(pool, 3 * s + u, i + 1)
        block = ctx.enter_context(nc.Block())

        @block.sync
        def _(sp):
            sp.dma_start(const[:], ins["const"]).then_inc(loaded, 16)
            sp.dma_start(par, ins["par"]).then_inc(loaded, 16)
            sp.dma_start(delta_r, ins["delta"].to_broadcast([3, B * S])).then_inc(loaded, 16)
            sp.dma_start(ctxw, ins["ctxw"].rearrange("(c p) n -> p c n", p=P)).then_inc(loaded, 16)
            sp.dma_start(wgt, ins["wgt"].rearrange("(c p) n -> p c n", p=P)).then_inc(loaded, 16)

            def load_x(b):
                wait(sp, f_dve, b - 1, "x1_1")
                sp.dma_start(x_in, ins["x"][bass.ds(b * L, L), :].rearrange("(t p) d -> p t d", p=P)).then_inc(x_loaded, 16)

            def store_rows(b):
                rows = rows_dram[bass.ds(b * L, L), :].rearrange("(t p) d -> p t d", p=P)
                wait(sp, b_pool, b, "h2w")
                sp.dma_start(rows[:, :, 0:D], h2).then_inc(rows_stored, 16)
                wait(sp, b_pool, b, "res")
                par2 = b % 2
                sp.dma_start(rows[:, :, D:2 * D], x1[:, bass.ds(par2, 1), :, :].rearrange("p a t d -> p (a t) d")).then_inc(rows_stored, 16)

            load_x(0)
            expert_weights(sp, 0)
            expert_weights(sp, 1)
            load_x(1)
            with sp.Fori(2, B) as b:
                load_x(b)
                store_rows(b - 2)
            store_rows(B - 2)
            store_rows(B - 1)
            moe_loads(sp)

        @block.tensor
        def _(pe):
            pe_setup(pe)
            pe.wait_ge(su_dve, SETUP_DVE)
            pipeline(pe, pe_iteration)
            pe_routing(pe)
            pe_moe(pe)

        @block.scalar
        def _(act):
            act.wait_ge(su_dve, SETUP_DVE)
            pipeline(act, act_iteration)
            act_moe(act)

        @block.vector
        def _(dve):
            dve_setup(dve)
            pipeline(dve, dve_iteration)
            dve_routing(dve)
            dve_moe(dve)

        @block.gpsimd
        def _(pool):
            assert pool is nc.gpsimd
            pool_setup(pool)
            pipeline(pool, pool_iteration)
            pool_routing(pool)
            pool_moe(pool)


def shape_constants():
    p, t = np.arange(P), np.arange(T)
    inv_freq = (1.0 / 10000.0 ** (np.arange(0, E, 2, dtype=np.float32) / E)).astype(np.float32)
    angle = ((t[None, :, None] * P + p[:, None, None]).astype(np.float32) * inv_freq).astype(np.float32)
    rows = {
        "ident": np.eye(P), "causal": p[:, None] <= p[None, :], "before": p[:, None] < p[None, :], "ones": np.ones((P, P)),
        "same_head": p[:, None] // E == p[None, :] // E, "row": np.tile(p, (P, 1)),
        "head_of": p[:, None] // E == np.arange(PAIRS), "half": p[:, None] // S == np.arange(2),
        "part": p[:, None] == np.arange(3),
        "cos": np.cos(angle).reshape(P, -1), "sin": np.sin(angle).reshape(P, -1), "negsin": -np.sin(angle).reshape(P, -1),
        "tile_limit": np.tile(np.where(np.arange(TT) == 0, -1, P * np.arange(TT)), (P, 1)),
        "earlier": np.tile((np.arange(NE)[None, :] < np.arange(NE)[:, None]).reshape(1, -1), (P, 1)),
        "rank": np.tile(NE - np.arange(NE), (P, 1)), "tile_no": np.tile(np.arange(NT + 1), (P, 1)),
        "token": np.arange(TT)[None, :] * P + p[:, None], "partition": p[:, None],
    }
    return np.concatenate([rows[name].astype(np.float32) for name in CONST], axis=1)


def kernel(**inputs):
    from concourse import bacc
    from concourse.bass_utils import run_bass_kernel_spmd

    a = {k: np.asarray(v) for k, v in inputs.items()}
    c, f = {k[9:]: v for k, v in a.items() if k.startswith("L0_xcond_")}, {k[7:]: v for k, v in a.items() if k.startswith("L0_ffn_")}

    order = np.array([8 * m + 4 * x + r for m in range(2) for r in range(4) for x in range(2)])
    cols = (order[:, None] * E + np.arange(E)[None, :]).reshape(-1)

    def row(v):
        return np.broadcast_to(v.reshape(1, -1), (P, v.size))

    def col(v):
        return v.reshape(-1, P).T

    par = {
        "c_bo": row(c["bo"]), "bqkv": row(np.concatenate([f["bq"][cols], f["bk"], f["bv"]])), "f_bo": row(f["bo"]), "ln2": row(f["ln2_w"]),
        "qkn": row(np.concatenate([np.tile(f["qn_w"], H), np.tile(f["kn_w"], KV)])), "br": row(f["br"]), "c_bv": row(c["bv"]),
        "tau": row(a["condB_tau"]), "c_bq": col(c["bq"]), "c_bk": col(c["bk"]),
        "bg": np.tile(f["bg"], PAIRS)[:, None], "ln1": col(f["ln1_w"]), "Wg": np.tile(f["Wg"], (PAIRS, PAIRS)),
    }
    wgt = np.concatenate([c["Wq"].T, c["Wo"].T, f["Wq"][:, cols], f["Wk"], f["Wv"], f["Wo"][cols, :], f["Wr"]], axis=1)
    ctxw = np.concatenate([c["Wk"].T, c["Wv"].T, a["ctx_1024"].reshape(B * S, D).T], axis=1)
    arrays = {
        "x": a["x"].reshape(N, D), "const": shape_constants(), "par": np.concatenate([par[name] for name in PAR], axis=1),
        "delta": a["fside_BxS2_0"].reshape(1, -1), "wgt": wgt, "ctxw": ctxw, "W1": f["W1"], "W2": f["W2"], "b1": f["b1"], "b2": f["b2"],
    }
    arrays = {k: np.ascontiguousarray(v) for k, v in arrays.items()}

    nc = bacc.Bacc("TRN2", target_bir_lowering=False, num_devices=1)
    ins = {k: nc.dram_tensor(f"in_{k}", v.shape, mybir.dt.from_np(v.dtype), kind="ExternalInput").ap() for k, v in arrays.items()}
    out = nc.dram_tensor("out", (N, D), F32, kind="ExternalOutput").ap()
    build(nc, ins, out)
    r = run_bass_kernel_spmd(nc, [{f"in_{k}": v for k, v in arrays.items()}], core_ids=[0])
    return r.results[0]["out"].reshape(B, L, D)
```

```python
from contextlib import ExitStack

import numpy as np

import concourse.bass as bass
from concourse import mybir

F32 = mybir.dt.float32
F32R = mybir.dt.float32r
BF16 = mybir.dt.bfloat16
I32 = mybir.dt.int32
U32 = mybir.dt.uint32
ALU = mybir.AluOpType
ACT = mybir.ActivationFunctionType
X = mybir.AxisListType.X

P = 128
B, L, D = 8, 512, 256
S = 64
H, E = 16, 16
KV = 4
HS = H + KV
QKV = (H + 2 * KV) * E
NE, HID = 8, 512
C = D // P
T = L // P
TT = B * T
N = B * L
NT = TT + NE - 1
PAIRS = H // 2
LN_EPS, RMS_EPS = 1e-5, 1e-6
SCALE = 0.25
HI_MASK = -4096
ARENA = 45600
OUT_OF_RANGE = 8192

def columns(parts):
    at, n = {}, 0
    for name, width in parts:
        at[name] = (n, width)
        n += width
    return at, n


CONST, CONST_N = columns([
    ("ident", P), ("causal", P), ("before", P), ("ones", P), ("same_head", P), ("row", P),
    ("head_of", PAIRS), ("half", 2), ("part", 3), ("cos", T * E // 2), ("sin", T * E // 2), ("negsin", T * E // 2),
    ("tile_limit", TT), ("earlier", NE * NE), ("rank", NE), ("tile_no", NT + 1), ("token", TT), ("pair_ones", 2 * E), ("slot_ones", 3 * E),
])
PAR, PAR_N = columns([
    ("c_bo", D), ("bqkv", QKV), ("f_bo", D), ("ln2", D), ("qkn", KV * E), ("qn", KV * E), ("br", NE), ("c_bv", D),
    ("tau", B), ("c_bq", C), ("c_bk", C), ("bg", 1), ("ln1", C), ("Wg", P),
])
WGT, WGT_N = columns([("c_q", D), ("c_o", D), ("qkv", QKV), ("f_o", D), ("r", NE)])
CTX, CTX_N = columns([("c_k", D), ("c_v", D), ("ctx", B * S)])


class Steps:

    def __init__(self, sem, names):
        self.sem, self.names = sem, list(names)
        self.n = len(self.names)
        self.index = {name: i for i, name in enumerate(self.names)}
        assert len(self.index) == self.n

    def value(self, b, name):
        return b * self.n + (self.index[name] + 1)


def wait(eng, steps, b, name):
    v = steps.value(b, name)
    if isinstance(v, int) and v <= 0:
        return
    eng.wait_ge(steps.sem, v)


POINTS = 3 * PAIRS
AT = {"xT": 0, "cq": 1, "cs0": 2, "cs1": 3, "cT0": 4, "cs2": 5, "co0": 5, "cT1": 6, "cs3": 7, "co1": 7,
      "cT2": 8, "co2": 9, "cT3": 9, "co3": 10, "wo": 11, "y": 12, "h": 13, "hT": 14, "qkv0": 15, "qkv1": 16,
      "rope": 17, "norm": 18, "split": 19, "twice": 20, "st0": 21, "st1": 23}
for t in range(T):
    AT[f"exp{t}"] = AT[f"cs{t}"] + 1
HEAD_AT = {"ln1": 19, "kbd": 20, "xn": 21}
BACK_AT = {"z0": 5, "z1": 6, "gated": 7, "wo0": 8, "wo1": 9, "rms": 9, "h2": 10, "weight": 11, "hT0": 13, "hT1": 14, "lg": 16}


def in_order(at, stages):
    return [name for p in range(POINTS) for stage, names in stages if at[stage] == p for name in names]


TILES4 = range(T)
ST0, ST1 = ["stk0", "stq0", "stq1", "stq2", "stq3"], ["stk1", "stq4", "stq5", "stq6", "stq7"]
ST_ACT = ST0[0::2] + ST1[1::2]
NEWTON = [f"{op}{k}" for k in range(3) for op in ("newton_a", "newton_b", "newton_c")]
FRONT_PE = in_order(AT, [("xT", ["xT0", "xT1"]), ("cq", ["cq0", "cq1"])]
                    + [(f"co{t}", [f"co{t}"]) for t in TILES4]
                    + [(f"cT{t}", [f"cT{t}0", f"cT{t}1"]) for t in TILES4]
                    + [(f"cs{t}", [f"cs{t}0", f"cs{t}1"]) for t in TILES4]
                    + [("wo", ["wo0", "wo1"]), ("hT", ["hT0", "hT1"]), ("qkv0", ["qkv0", "qkv1"]), ("qkv1", ["qkv2", "qkv3"]),
                       ("st0", ST0), ("st1", ST1)])
FRONT_ACT = in_order(AT, [("xT", ["xT0", "xT1"])]
                     + [(f"cT{t}", [f"cT{t}0", f"cT{t}1"]) for t in TILES4]
                     + [(f"exp{t}", [f"cexp{t}"]) for t in TILES4]
                     + [("h", ["h"]), ("hT", ["hT0", "hT1"]), ("qkv1", ["square"]), ("twice", ["twice0", "twice1"]), ("st0", [n for n in ST0 if n in ST_ACT]), ("st1", [n for n in ST1 if n in ST_ACT])])
FRONT_DVE = in_order(AT, [("cq", ["cq0", "cq1"])]
                     + [(f"co{t}", [f"crec{t}", f"co{t}"]) for t in TILES4]
                     + [(f"cs{t}", [f"cmax{t}", f"csub{t}0", f"csub{t}1"]) for t in TILES4]
                     + [("wo", ["x1_0", "x1_1", "ln2_stats", "ln2_aggr"]), ("y", ["y"]), ("qkv0", ["qkv0", "qkv1"]), ("qkv1", ["qkv2", "qkv3"]),
                        ("rope", ["cosmul", "meansq", "qk_eps", "half_bits", "guess"] + NEWTON),
                        ("norm", ["qnorm", "kweight"]), ("split", ["hi0", "lo0", "hi1", "lo1"]),
                        ("st0", [n for n in ST0 if n not in ST_ACT]), ("st1", [n for n in ST1 if n not in ST_ACT])])
FRONT_POOL = in_order(AT, [("wo", ["ln2_eps", "ln2_rstd", "rstd2", "meansq", "rms_eps", "rms"]),
                           ("hT", ["ybo"]), ("rope", ["sin1", "sin2", "rope"])])
HEAD_DVE = ["ln1_stats", "ln1_aggr", "xn"]
HEAD_POOL = ["ln1_eps", "ln1_rstd", "kbd", "vbd", "xbo"]
U = 6
UNITS = [f"s{s}{u}" for s in range(PAIRS) for u in range(U)]
POINT_UNITS = [(0, 1), (2, 3), (4, 5)]
MASKS = [f"m{s}{v}" for s in range(PAIRS) for v in range(3)]
QUADS = PAIRS // 2
ATTENDED = [f"pv{q}{kb}" for q in range(QUADS) for kb in range(T)]
BACK_PE = in_order(BACK_AT, [(n, [n]) for n in ("z0", "z1", "wo0", "wo1", "hT0", "hT1", "lg")])
BACK_ACT = in_order(BACK_AT, [("z0", ["gate0"]), ("z1", ["gate1"]), ("hT0", ["hT0"]), ("hT1", ["hT1"])])
BACK_DVE = in_order(BACK_AT, [("gated", ["gated"]), ("wo0", ["in0"]), ("wo1", ["in1", "stats", "aggr"]), ("h2", ["h2"]), ("lg", ["lg"])])
BACK_POOL = in_order(BACK_AT, [("rms", ["msq", "ms", "rms_eps", "rms"]), ("h2", ["res"]), ("weight", ["h2w"])])

FRONT_BANKS = 3
CROSS_BANK = {"cs": (0, 1), "cT": (0, 1), "co": (2, 2)}
FRONT_BANK, i = {}, 0
for name in FRONT_PE:
    if name[:2] in CROSS_BANK:
        FRONT_BANK[name] = CROSS_BANK[name[:2]][int(name[-1]) % 2]
    else:
        FRONT_BANK[name] = i % FRONT_BANKS
        i += 1
SCORE_BANKS = 2
SCORE_BANK = {name: i % SCORE_BANKS for i, name in enumerate(UNITS)}


def before_in_bank(units, bank, name):
    same = [n for n in units if bank[n] == bank[name]]
    i = same.index(name)
    return (same[i - 1], 0) if i else (same[-1], 1)


def build(nc, ins, out):
    with ExitStack() as ctx:
        def sb(name, shape, dt=F32):
            return ctx.enter_context(nc.sbuf_tensor(name, shape, dt))

        def sem(name):
            return ctx.enter_context(nc.semaphore(name))

        banks = ctx.enter_context(nc.psum_tensor("banks", [P, 8, L], F32))
        ps_s, ps_v, ps_f, ps_b = banks[:, 0:2], banks[:, 2:4], banks[:, 4:7], banks[:, 7]
        ps_up = banks[:, 0:4].rearrange("p (d half) n -> p d (half n)", d=2)

        const = sb("const", [P, CONST_N])
        routed = sb("routed", [P, 2, NT + 1], I32)
        tile_expert = sb("tile_expert", [P, NT + 1], I32)
        rows_in = sb("rows_in", [P, 2, 1], I32)
        rows_out = sb("rows_out", [P, 2, 1], I32)
        logits = sb("logits", [P, TT, NE])
        half_power = sb("half_power", [P, T])
        ln_eps, rms_eps = sb("ln_eps", [P, T]), sb("rms_eps", [P, T])
        sq = sb("sq", [P, PAIRS, L], F32R)
        sk = sb("sk", [P, 2, L], F32R)

        WEX = C * 2 * HID + HID // P * D
        arena = sb("arena", [P, ARENA])
        used = [0]

        def take(*shape):
            n = int(np.prod(shape))
            at = used[0]
            used[0] += n
            v = arena[:, at:at + n]
            if len(shape) == 2:
                return v.rearrange("p (a b) -> p a b", a=shape[0])
            if len(shape) == 3:
                return v.rearrange("p (a b c) -> p a b c", a=shape[0], b=shape[1])
            if len(shape) == 4:
                return v.rearrange("p (a b c d) -> p a b c d", a=shape[0], b=shape[1], c=shape[2])
            return v

        kT = take(C, B * S)
        kbd = take(C, PAIRS, S)
        v_all = take(B, D)
        vbd = take(PAIRS, 2 * E)
        x_in = take(T, D)
        xn = take(T, D)
        xnT = take(C, L)
        cqT = take(C, L)
        coT = cqT
        cs_at = used[0]
        cs = take(2, H * S)
        squares = arena[:, cs_at:cs_at + T * HS * E].rearrange("p (t n) -> p t n", t=T)
        cpT = take(PAIRS, P)
        rope_a = take(T, HS * E)
        rope_b = take(T, HS * E)
        stack_at = used[0]
        stack = take(2, T, PAIRS + 2, 4 * E)
        EARLY = used[0] // WEX
        par = take(PAR_N)
        wgt = take(C, WGT_N)
        x1 = take(2, T, D)
        y = take(2, T, D)
        qkv = take(T, QKV)
        pt_at = used[0]
        pt = take(4, 5 * L)
        v_pad = take(T, KV, 3 * E)
        aoT = take(C, L)
        gate = take(C, L)
        h2 = take(T, D)
        h2T = gate
        stats = take(3, T, 6)
        mv = take(3, T, 2)
        tiny = take(12, T)
        cmax = take(2, H)
        qk_ms = take(HS * T)
        qk_rs = take(HS * T)
        qk_t = take(HS * T)
        crec = take(C, P)
        rec = take(L)
        print("used", used[0])
        assert used[0] <= ARENA, used[0]
        ctxw = arena[:, pt_at:pt_at + C * CTX_N].rearrange("p (c n) -> p c n", c=C)
        delta_r = arena[0:3, stack_at:stack_at + B * S]
        delta_s = arena[0:3, stack_at + B * S:stack_at + 2 * B * S]
        delta_parts = arena[0:3, stack_at + 2 * B * S:stack_at + 4 * B * S].bitcast(BF16).rearrange("p (k n) -> p k n", k=4)
        delta3 = sb("delta3", [3, B * S], BF16)
        ones3 = sb("ones3", [3, P], BF16)

        carrier = sb("carrier", [1, 2])

        def wait_apart(eng, steps, b, name):
            wait(eng, steps, b, name)
            if eng is nc.gpsimd:
                nc.gpsimd.tensor_tensor(carrier[:, 1:2], half_power[0:1, 0:1], half_power[0:1, 0:1], ALU.mult)
            else:
                nc.vector.memset(carrier[:, 0:1], 0.0)

        def cst(name, rows=P):
            a, n = CONST[name]
            return const[0:rows, a:a + n]

        def prm(name, rows=P):
            a, n = PAR[name]
            return par[0:rows, a:a + n]

        def w(name):
            a, n = WGT[name]
            return wgt[:, :, a:a + n]

        def cx(name):
            a, n = CTX[name]
            return ctxw[:, :, a:a + n]

        ident = cst("ident")
        wg = prm("Wg")
        rows_dram = nc.dram_tensor("rows_scratch", (N, 2 * D), F32, kind="Internal").ap()

        SETUP_LOADS = 5
        SETUP_DVE = 2 + B + 15
        f_pe, f_act = Steps(sem("front_pe"), FRONT_PE), Steps(sem("front_act"), FRONT_ACT)
        h_dve, h_pool = Steps(sem("head_dve"), HEAD_DVE), Steps(sem("head_pool"), HEAD_POOL)
        f_dve, f_pool = Steps(sem("front_dve"), FRONT_DVE), Steps(sem("front_pool"), FRONT_POOL)
        a_pe, a_act = Steps(sem("scores_pe"), UNITS), Steps(sem("probs_act"), UNITS)
        a_pool, v_pe = Steps(sem("masked_pool"), MASKS), Steps(sem("attended_pe"), ATTENDED)
        v_dve, n_dve = Steps(sem("values_dve"), ["v"]), Steps(sem("attention_dve"), ["rec0", "n0", "rec1", "n1"])
        b_pe, b_act = Steps(sem("back_pe"), BACK_PE), Steps(sem("back_act"), BACK_ACT)
        b_dve, b_pool = Steps(sem("back_dve"), BACK_DVE), Steps(sem("back_pool"), BACK_POOL)
        x_loaded = sem("x_loaded")
        rows_stored = sem("rows_stored")
        loaded = sem("loaded")
        su_pe, su_dve, su_pool = sem("setup_pe"), sem("setup_dve"), sem("setup_pool")

        front_reader = {}
        for n in FRONT_PE:
            if n in FRONT_ACT:
                front_reader[n] = (f_act, n)
            elif n[:2] == "cs":
                front_reader[n] = (f_dve, "csub" + n[2:])
            elif n[:2] == "wo":
                front_reader[n] = (f_dve, "x1_" + n[2:])
            else:
                front_reader[n] = (f_dve, n)
        back_reader = {"z0": (b_act, "gate0"), "z1": (b_act, "gate1"),
                       "wo0": (b_dve, "in0"), "wo1": (b_dve, "in1"), "hT0": (b_act, "hT0"), "hT1": (b_act, "hT1"),
                       "lg": (b_dve, "lg")}

        UNIT_PARTS = [
            [(0, 0, 0, L)], [(1, 0, 0, L)],
            [(0, 1, 0, 3 * P), (0, 3, 3 * P, P)], [(1, 1, 0, 3 * P), (1, 3, 3 * P, P)],
            [(0, 2, 0, 2 * P)], [(1, 2, 0, 2 * P)],
        ]
        UNIT_AT = [0, L, 2 * L, 3 * L, 4 * L, 4 * L + 2 * P, 5 * L]

        def probs(s, x, kb):
            for u, parts in enumerate(UNIT_PARTS):
                for head, k, col, width in parts:
                    if (head, k) == (x, kb):
                        a = UNIT_AT[u] + col
                        return pt[:, s % 4, a:a + width]

        at = [0]

        def take2(*shape):
            n = int(np.prod(shape))
            v = arena[:, at[0]:at[0] + n]
            at[0] += n
            if len(shape) == 2:
                return v.rearrange("p (a b) -> p a b", a=shape[0])
            if len(shape) == 3:
                return v.rearrange("p (a b c) -> p a b c", a=shape[0], b=shape[1])
            return v

        wex = take2(NE, WEX)
        b1 = take2(NE, 2 * HID)
        b2 = take2(NE, D)
        hot_at = at[0]
        got = take2(2, 2 * D)
        gT = take2(2, C, P)
        ub = take2(2, 2 * HID)
        sg = take2(2, HID)
        act_ = take2(2, HID)
        actT = take2(2, HID)
        res = take2(2, D)
        yo = take2(2, D)
        small = [take2(TT, NE) for _ in range(9)]
        rsmall = take2(12, TT + NE)
        assert at[0] <= ARENA, at[0]
        at[0] = hot_at
        row_hot = take2(TT, P)
        tile_hot = take2(TT, 2, NT + 1)

        w_ready = [sem(f"expert{e}_loaded") for e in range(NE)]
        r_pe, r_dve = sem("routing_pe"), sem("routing_dve")
        up_pe, down_pe = Steps(sem("up_pe"), ["gT", "u"]), Steps(sem("down_pe"), ["aT", "y"])
        up_act, down_act = Steps(sem("up_act"), ["gT", "res"]), Steps(sem("down_act"), ["sig", "aT"])
        m_dve = Steps(sem("expert_dve"), ["ub", "act", "y_b2", "y"])
        m_pool = Steps(sem("expert_rows_pool"), ["in"])
        m_pool_out = Steps(sem("expert_rows_out_pool"), ["out"])
        rows_got = [sem(f"rows_got{d}") for d in range(2)]
        out_stored = [sem(f"out_stored{d}") for d in range(2)]

        def expert_weights(sp, e):
            sp.dma_start(wex[:, e, 0:C * 2 * HID].rearrange("p (c n) -> p c n", c=C),
                         ins["W1"][e].rearrange("(c p) n -> p c n", p=P)).then_inc(w_ready[e], 16)
            sp.dma_start(wex[:, e, C * 2 * HID:WEX].rearrange("p (c n) -> p c n", c=HID // P),
                         ins["W2"][e].rearrange("(c p) n -> p c n", p=P)).then_inc(w_ready[e], 16)

        def early_loads(sp):
            for steps in (f_pe, f_act, f_dve, f_pool, h_dve, h_pool):
                sp.wait_ge(steps.sem, B * steps.n)
            for e in range(EARLY):
                expert_weights(sp, e)

        def moe_loads(sp):
            sp.wait_ge(b_dve.sem, B * b_dve.n)
            sp.wait_ge(rows_stored, 32 * B)
            for e in range(NE):
                if e >= EARLY:
                    expert_weights(sp, e)
                sp.dma_start(b1[:, e, :], ins["b1"][e:e + 1, :].to_broadcast([P, 2 * HID])).then_inc(w_ready[e], 16)
                sp.dma_start(b2[:, e, :], ins["b2"][e:e + 1, :].to_broadcast([P, D])).then_inc(w_ready[e], 16)

        def pe_routing(pe):
            pe.wait_ge(r_dve, R_HOT)
            hot = small[2].rearrange("p t e -> p (t e)")
            nc.tensor.matmul(ps_f[:, 0, 0:TT * NE], cst("before"), hot, start=True, stop=True)
            nc.tensor.matmul(ps_f[:, 1, 0:TT * NE], cst("ones"), hot, start=True, stop=True).then_inc(r_pe, 1)
            pe.wait_ge(r_dve, R_ONE_HOTS)
            for t in range(TT):
                last = nc.tensor.matmul(ps_v[:, 0, 0:2 * (NT + 1)], row_hot[:, t, :], tile_hot[:, t, :, :].rearrange("p a j -> p (a j)"),
                                        start=(t == 0), stop=(t == TT - 1))
            last.then_inc(r_pe, 1)

        R_HOT, R_ONE_HOTS, R_DONE = 5, 29, 35

        def dve_routing(dve):
            count = [0]

            def done(inst):
                count[0] += 1
                inst.then_inc(r_dve, 1)
                dve.wait_ge(r_dve, count[0])

            def over_e(v):
                return v.unsqueeze(2).to_broadcast([P, TT, NE])

            v = nc.vector
            tt = v.tensor_tensor
            wait(dve, b_dve, B - 1, "lg")
            dve.wait_ge(rows_stored, 32 * B)
            mx, rank = rsmall[:, 0, 0:TT], cst("rank")
            eq, score, hot = small[0], small[1], small[2]
            done(v.tensor_reduce(mx, logits[:], X, ALU.max))
            done(tt(eq, logits[:], over_e(mx), ALU.is_ge))
            done(tt(score, eq, rank.unsqueeze(1).to_broadcast([P, TT, NE]), ALU.mult))
            done(v.tensor_reduce(mx, score, X, ALU.max))
            done(tt(hot, score, over_e(mx), ALU.is_equal))
            assert count[0] == R_HOT
            dve.wait_ge(r_pe, 1)
            et = [small[i].rearrange("p t e -> p (t e)").rearrange("p (e t) -> p e t", e=NE) for i in (3, 4, 5, 6)]
            tot, run = et[0], et[1]
            done(v.tensor_copy(tot, ps_f[:, 1, 0:TT * NE].rearrange("p (t e) -> p e t", e=NE)))
            cur, k = tot, 1
            for nxt in (et[1], et[2], et[1], et[2], et[1]):
                v.tensor_copy(nxt[:, :, 0:k], cur[:, :, 0:k])
                done(tt(nxt[:, :, k:], cur[:, :, k:], cur[:, :, 0:TT - k], ALU.add))
                cur, k = nxt, 2 * k
            run = cur
            before = et[2]
            done(tt(before, run, tot, ALU.subtract))
            done(tt(et[3], run[:, :, TT - 1:TT].to_broadcast([P, NE, TT]), cst("tile_limit").unsqueeze(1).to_broadcast([P, NE, TT]), ALU.is_gt))
            tiles, first, first_row = rsmall[:, 1, 0:NE], rsmall[:, 2, 0:NE], rsmall[:, 3, 0:NE]
            done(v.tensor_reduce(tiles, et[3], X, ALU.add))
            square = small[7].rearrange("p t e -> p (t e)")[:, 0:NE * NE].rearrange("p (a b) -> p a b", a=NE)
            done(tt(square, tiles.unsqueeze(1).to_broadcast([P, NE, NE]), cst("earlier").rearrange("p (a b) -> p a b", a=NE), ALU.mult))
            done(v.tensor_reduce(first, square, X, ALU.add))
            done(v.tensor_scalar(first_row, first, float(P), None, ALU.mult))
            base = et[3]
            done(tt(base, before, first_row.unsqueeze(2).to_broadcast([P, NE, TT]), ALU.add))
            row_te = small[8]
            done(tt(row_te, ps_f[:, 0, 0:TT * NE].rearrange("p (t e) -> p t e", e=NE), base.rearrange("p e t -> p t e"), ALU.add))
            done(tt(row_te, row_te, hot, ALU.mult))
            row = rsmall[:, 4, 0:TT]
            done(v.tensor_reduce(row, row_te, X, ALU.add))
            row_i, tile_i, in_tile_i = (rsmall[:, k, 0:TT].bitcast(I32) for k in (5, 6, 7))
            tile_f, in_tile_f = rsmall[:, 8, 0:TT], rsmall[:, 9, 0:TT]
            done(v.tensor_copy(row_i, row))
            done(v.tensor_scalar(tile_i, row_i, 7, None, ALU.logical_shift_right))
            done(v.tensor_scalar(in_tile_i, row_i, P - 1, None, ALU.bitwise_and))
            done(v.tensor_copy(tile_f, tile_i))
            done(v.tensor_copy(in_tile_f, in_tile_i))
            done(tt(row_hot, cst("row").unsqueeze(1).to_broadcast([P, TT, P]), in_tile_f.unsqueeze(2).to_broadcast([P, TT, P]), ALU.is_equal))
            done(tt(tile_hot[:, :, 0, :], cst("tile_no").unsqueeze(1).to_broadcast([P, TT, NT + 1]),
                    tile_f.unsqueeze(2).to_broadcast([P, TT, NT + 1]), ALU.is_equal))
            done(tt(tile_hot[:, :, 1, :], tile_hot[:, :, 0, :], cst("token").unsqueeze(2).to_broadcast([P, TT, NT + 1]), ALU.mult))
            assert count[0] == R_ONE_HOTS, count[0]
            nt1 = NT + 1
            cmp = arena[:, hot_at + 6656:hot_at + 6656 + nt1 * NE].rearrange("p (j e) -> p j e", e=NE)
            te = rsmall[:, 10, 0:nt1]
            done(tt(cmp, cst("tile_no").unsqueeze(2).to_broadcast([P, nt1, NE]), first.unsqueeze(1).to_broadcast([P, nt1, NE]), ALU.is_ge))
            done(v.tensor_reduce(te, cmp, X, ALU.add))
            done(v.tensor_scalar(tile_expert[:], te, -1.0, None, ALU.add))
            dve.wait_ge(r_pe, 2)
            pad = rsmall[:, 11, 0:nt1]
            done(v.tensor_scalar(pad, ps_v[:, 0, 0:nt1], -float(OUT_OF_RANGE), float(OUT_OF_RANGE), ALU.mult, ALU.add))
            done(v.tensor_copy(routed[:, 0, :], ps_v[:, 0, nt1:2 * nt1]))
            done(tt(routed[:, 1, :], ps_v[:, 0, nt1:2 * nt1], pad, ALU.add))
            assert count[0] == R_DONE, count[0]

        def tiles(eng, first, iteration, last):
            first()
            for j in range(8):
                iteration(j, j // 2, j % 2)
            with eng.Fori(4, (NT - 1) // 2) as k:
                for d in range(2):
                    iteration(2 * k + d, k, d)
            last()

        def pe_up(pe, j, d):
            e = pe.value_load(tile_expert[0:1, bass.ds(j, 1)], min_val=0, max_val=NE - 1)
            wait_rows(pe, j, d)
            wait(pe, up_act, j - 1, "gT")
            for c in range(C):
                last = nc.tensor.transpose(ps_f[:, 0, c * P:(c + 1) * P], got[:, d, c * P:(c + 1) * P], ident)
            last.then_inc(up_pe.sem, 1)
            if isinstance(j, int) and j < NE:
                pe.wait_ge(w_ready[j], 64)
            wait(pe, up_act, j, "gT")
            wait(pe, m_dve, j - 2, "ub")
            for half in range(2):
                for c in range(C):
                    a = c * 2 * HID + half * HID
                    last = nc.tensor.matmul(ps_up[:, d, half * HID:(half + 1) * HID], gT[:, d, c, :],
                                            wex[:, bass.ds(e, 1), a:a + HID].rearrange("p x n -> p (x n)"),
                                            start=(c == 0), stop=(c == C - 1))
            last.then_inc(up_pe.sem, 1)
            return e

        def pe_down(pe, j, d, e):
            wait(pe, m_dve, j, "act")
            wait(pe, down_act, j - 1, "aT")
            for c in range(HID // P):
                last = nc.tensor.transpose(ps_f[:, 1, c * P:(c + 1) * P], act_[:, d, c * P:(c + 1) * P], ident)
            last.then_inc(down_pe.sem, 1)
            wait(pe, down_act, j, "aT")
            wait(pe, m_dve, j - 2, "y_b2")
            for c in range(HID // P):
                a = C * 2 * HID + c * D
                last = nc.tensor.matmul(y_bank(d), actT[:, d, c * P:(c + 1) * P],
                                        wex[:, bass.ds(e, 1), a:a + D].rearrange("p x n -> p (x n)"),
                                        start=(c == 0), stop=(c == HID // P - 1))
            last.then_inc(down_pe.sem, 1)

        def y_bank(d):
            return ps_f[:, 2, 0:D] if d else ps_b[:, 0:D]

        def wait_rows(eng, j, d):
            eng.wait_ge(rows_got[d], ((j - d) // 2) * 16 + 16)

        def pe_moe(pe):
            pe.wait_ge(r_dve, R_DONE)

            def step(j, k, d):
                pe_up(pe, j + 1, 1 - d)
                e = pe.value_load(tile_expert[0:1, bass.ds(j, 1)], min_val=0, max_val=NE - 1)
                pe_down(pe, j, d, e)

            def last():
                e = pe.value_load(tile_expert[0:1, NT - 1:NT], min_val=0, max_val=NE - 1)
                pe_down(pe, NT - 1, 0, e)

            tiles(pe, lambda: pe_up(pe, 0, 0), step, last)

        def act_moe(act):
            act.wait_ge(r_dve, R_DONE)

            def up(j, d):
                wait(act, up_pe, j, "gT")
                wait(act, up_pe, j - 2, "u")
                nc.scalar.activation(gT[:, d, :, :].rearrange("p c n -> p (c n)"), ps_f[:, 0, 0:C * P], ACT.Copy).then_inc(up_act.sem, 1)
                wait(act, m_dve, j - 2, "y")
                wait_rows(act, j, d)
                nc.scalar.activation(res[:, d, :], got[:, d, D:2 * D], ACT.Copy).then_inc(up_act.sem, 1)

            def down(j, d):
                wait(act, m_dve, j, "ub")
                wait(act, m_dve, j - 2, "act")
                nc.scalar.activation(sg[:, d, :], ub[:, d, HID:2 * HID], ACT.Sigmoid).then_inc(down_act.sem, 1)
                wait(act, down_pe, j, "aT")
                wait(act, down_pe, j - 2, "y")
                nc.scalar.activation(actT[:, d, :], ps_f[:, 1, :], ACT.Copy).then_inc(down_act.sem, 1)

            def step(j, k, d):
                up(j + 1, 1 - d)
                down(j, d)

            tiles(act, lambda: up(0, 0), step, lambda: down(NT - 1, 0))

        def dve_moe(dve):
            def step(j, k, d):
                if isinstance(j, int) and j < NE:
                    dve.wait_ge(w_ready[j], 64)
                e = dve.value_load(tile_expert[0:1, bass.ds(j, 1)], min_val=0, max_val=NE - 1)
                wait(dve, up_pe, j, "u")
                nc.vector.tensor_tensor(ub[:, d, :], ps_up[:, d, :], b1[:, bass.ds(e, 1), :].rearrange("p x n -> p (x n)"), ALU.add).then_inc(m_dve.sem, 1)
                wait(dve, down_act, j, "sig")
                wait(dve, down_pe, j - 2, "aT")
                nc.vector.tensor_tensor(act_[:, d, :], ub[:, d, 0:HID], sg[:, d, :], ALU.mult).then_inc(m_dve.sem, 1)
                wait(dve, down_pe, j, "y")
                stored(dve, k - 1, d)
                nc.vector.tensor_tensor(yo[:, d, :], y_bank(d), b2[:, bass.ds(e, 1), :].rearrange("p x n -> p (x n)"), ALU.add).then_inc(m_dve.sem, 1)
                wait(dve, m_dve, j, "y_b2")
                wait(dve, up_act, j, "res")
                nc.vector.tensor_tensor(yo[:, d, :], yo[:, d, :], res[:, d, :], ALU.add).then_inc(m_dve.sem, 1)

            tiles(dve, lambda: None, step, lambda: step(NT - 1, (NT - 1) // 2, 0))

        def stored(eng, k, d):
            if isinstance(k, int) and k < 0:
                return
            eng.wait_ge(out_stored[d], k * 16 + 16)

        def pool_routing(pool):
            pool.wait_ge(r_dve, R_DONE)

        def pool_moe(pool):
            def gather(j, k, d):
                if not (isinstance(k, int) and k < 1):
                    pool.wait_ge(rows_got[d], k * 16)
                wait(pool, up_pe, j - 2, "gT")
                wait(pool, up_act, j - 2, "res")
                nc.gpsimd.tensor_copy(rows_in[:, d, :], routed[:, 0, bass.ds(j, 1)]).then_inc(m_pool.sem, 1)
                wait_apart(pool, m_pool, j, "in")
                nc.gpsimd.indirect_dma_start(out=got[:, d, :], out_offset=None, in_=rows_dram,
                                             in_offset=bass.IndirectOffsetOnAxis(ap=rows_in[:, d, :].bitcast(U32), axis=0)).then_inc(rows_got[d], 16)

            def scatter(j, k, d):
                stored(pool, k - 1, d)
                nc.gpsimd.tensor_copy(rows_out[:, d, :], routed[:, 1, bass.ds(j, 1)]).then_inc(m_pool_out.sem, 1)
                wait(pool, m_pool_out, j, "out")
                wait_apart(pool, m_dve, j, "y")
                nc.gpsimd.indirect_dma_start(out=out, out_offset=bass.IndirectOffsetOnAxis(ap=rows_out[:, d, :].bitcast(U32), axis=0),
                                             in_=yo[:, d, :], in_offset=None, bounds_check=N - 1, oob_is_err=False).then_inc(out_stored[d], 16)

            def step(j, k, d):
                if not (isinstance(j, int) and j + 2 >= NT):
                    gather(j + 2, k + 1, d)
                scatter(j, k, d)

            def first():
                gather(0, 0, 0)
                gather(1, 0, 1)

            first()
            for j in range(8):
                step(j, j // 2, j % 2)
            with pool.Fori(4, (NT - 1) // 2 - 1) as k:
                for d in range(2):
                    step(2 * k + d, k, d)
            for j in range(NT - 3, NT):
                step(j, j // 2, j % 2)
            for d in range(2):
                stored(pool, (NT - 1 - d) // 2, d)




        def bank_free(eng, unit, b):
            prev, ago = before_in_bank(FRONT_PE, FRONT_BANK, unit)
            st, name = front_reader[prev]
            wait(eng, st, b - ago, name)

        def fb(unit):
            return ps_f[:, FRONT_BANK[unit], :]

        def pe_transposes(unit, b, blocks):
            for i, blk in enumerate(blocks):
                last = nc.tensor.transpose(fb(unit)[:, i * P:(i + 1) * P], blk, ident)
            last.then_inc(f_pe.sem, 1)

        def pe_setup(pe):
            pe.wait_ge(loaded, 16 * SETUP_LOADS)
            for g in range(C):
                for c in range(C):
                    last = nc.tensor.matmul(ps_f[:, g, :], cx("c_k")[:, c, g * P:(g + 1) * P], cx("ctx")[:, c, :],
                                            start=(c == 0), stop=(c == C - 1))
            last.then_inc(su_pe, 1)
            for b in range(B):
                bank = ps_s[:, b % SCORE_BANKS, 0:D]
                if b >= SCORE_BANKS:
                    pe.wait_ge(su_dve, 2 + b - SCORE_BANKS + 1)
                for x in range(2):
                    for c in range(C):
                        last = nc.tensor.matmul(bank[x * S:(x + 1) * S, :], cx("ctx")[:, c, b * S:(b + 1) * S], cx("c_v")[:, c, :],
                                                start=(c == 0), stop=(c == C - 1))
                last.then_inc(su_pe, 1)

        def pe_front(pe, p, b):
            def at(stage):
                return p == AT[stage]

            def scores(t):
                if t == 0:
                    wait(pe, f_dve, b, "cq1")
                    wait(pe, h_pool, b, "kbd")
                for g in range(C):
                    bank_free(pe, f"cs{t}{g}", b)
                    nc.tensor.matmul(fb(f"cs{t}{g}"), cqT[:, g, t * P:(t + 1) * P], kbd[:, g, :, :].rearrange("p h s -> p (h s)"),
                                     start=True, stop=False)
                    nc.tensor.matmul(fb(f"cs{t}{g}").rearrange("p (h s) -> p h s", h=PAIRS), ones3[:],
                                     delta3[:, bass.ds(b * S, S)].unsqueeze(1).to_broadcast([3, PAIRS, S]),
                                     start=False, stop=True).then_inc(f_pe.sem, 1)

            def probs_T(t):
                wait(pe, f_act, b, f"cexp{t}")
                for g in range(2):
                    bank_free(pe, f"cT{t}{g}", b)
                    pe_transposes(f"cT{t}{g}", b, [cs[:, t % 2, (4 * g + i) * P:(4 * g + i + 1) * P] for i in range(4)])

            def attended(t):
                wait(pe, f_act, b, f"cT{t}1")
                wait(pe, h_pool, b, "vbd")
                bank_free(pe, f"co{t}", b)
                for kind in range(2):
                    for j in range(PAIRS):
                        stationary = cst("pair_ones") if kind else vbd[:, j, :]
                        rows, a = 2 * E * (j % 4), (2 * kind + j // 4) * P
                        last = nc.tensor.matmul(fb(f"co{t}")[rows:rows + 2 * E, a:a + P], stationary, cpT[:, j, :],
                                                start=True, stop=True, tile_position=(0, rows))
                last.then_inc(f_pe.sem, 1)

            if at("xT"):
                wait(pe, h_dve, b, "xn")
                for c in range(C):
                    bank_free(pe, f"xT{c}", b)
                    pe_transposes(f"xT{c}", b, [xn[:, t, c * P:(c + 1) * P] for t in range(T)])
            if at("cq"):
                wait(pe, f_act, b, "xT1")
                for g in range(C):
                    bank_free(pe, f"cq{g}", b)
                    for c in range(C):
                        last = nc.tensor.matmul(fb(f"cq{g}"), w("c_q")[:, c, g * P:(g + 1) * P], xnT[:, c, :],
                                                start=(c == 0), stop=(c == C - 1))
                    last.then_inc(f_pe.sem, 1)
            for t in range(T):
                if at(f"co{t}"):
                    attended(t)
            for t in range(T):
                if at(f"cT{t}"):
                    probs_T(t)
            for t in range(T):
                if at(f"cs{t}"):
                    scores(t)
            if at("wo"):
                wait(pe, f_dve, b, "co3")
                for k in range(2):
                    bank_free(pe, f"wo{k}", b)
                    for i in range(2):
                        t = 2 * k + i
                        for c in range(C):
                            last = nc.tensor.matmul(fb(f"wo{k}")[:, i * D:(i + 1) * D], coT[:, c, t * P:(t + 1) * P], w("c_o")[:, c, :],
                                                    start=(c == 0), stop=(c == C - 1))
                    last.then_inc(f_pe.sem, 1)
            if at("hT"):
                wait(pe, f_act, b, "h")
                for c in range(C):
                    bank_free(pe, f"hT{c}", b)
                    pe_transposes(f"hT{c}", b, [xn[:, t, c * P:(c + 1) * P] for t in range(T)])
            for k in range(2):
                if at(f"qkv{k}"):
                    wait(pe, f_act, b, "hT1")
                    for t in (2 * k, 2 * k + 1):
                        bank_free(pe, f"qkv{t}", b)
                        for c in range(C):
                            last = nc.tensor.matmul(fb(f"qkv{t}")[:, 0:QKV], xnT[:, c, t * P:(t + 1) * P], w("qkv")[:, c, :],
                                                    start=(c == 0), stop=(c == C - 1))
                        last.then_inc(f_pe.sem, 1)
            for m, units in enumerate((ST0, ST1)):
                if at(f"st{m}"):
                    wait(pe, f_act, b, f"twice{m}")
                    for n in units:
                        bank_free(pe, n, b)
                        h = 8 if n[2] == "k" else 2 * (int(n[3]) % 4)
                        pe_transposes(n, b, [stack[:, m, t, h:h + 2, :].rearrange("p x n -> p (x n)") for t in range(T)])

        def pe_scores(pe, b, s, u):
            if u == 0:
                unit = f"stq{s}"
                wait(pe, *((f_act if unit in ST_ACT else f_dve), b, unit))
                if s % 4 == 0:
                    unit = f"stk{s // 4}"
                    wait(pe, *((f_act if unit in ST_ACT else f_dve), b, unit))
            prev, ago = before_in_bank(UNITS, SCORE_BANK, f"s{s}{u}")
            wait(pe, a_act, b - ago, prev)
            m, bank = s // 4, SCORE_BANK[f"s{s}{u}"]
            for x, kb, a, width in UNIT_PARTS[u]:
                last = nc.tensor.matmul(ps_s[:, bank, a:a + width], sk[x * 64:(x + 1) * 64, m, kb * P:(kb + 1) * P],
                                        sq[x * 64:(x + 1) * 64, s, kb * P:kb * P + width], start=True, stop=True)
            last.then_inc(a_pe.sem, 1)

        def pe_attended(pe, b, q, kb):
            if kb == 0:
                wait(pe, a_pool, b, f"m{2 * q + 1}2")
                if q == 0:
                    wait(pe, v_dve, b, "v")
                if q % 2 == 0:
                    wait(pe, n_dve, *((b, "n0") if q else (b - 1, "n1")))
            slot, ones = q % 2, cst("slot_ones")
            for kind in range(2):
                for i in range(2):
                    for x in range(2):
                        rows, a = 2 * E * (2 * i + x), E * (1 - slot)
                        stationary = ones[:, a:a + 2 * E] if kind else v_pad[:, kb, 2 * (q // 2) + x, a:a + 2 * E]
                        last = nc.tensor.matmul(ps_v[rows:rows + 2 * E, kind, kb * P:L], stationary, probs(2 * q + i, x, kb),
                                                start=(slot == 0 and kb == 0), stop=(slot == 1 and kb == T - 1), tile_position=(0, rows))
            last.then_inc(v_pe.sem, 1)

        def back_free(eng, unit, b):
            i = BACK_PE.index(unit)
            st, name = back_reader[BACK_PE[i - 1]]
            wait(eng, st, b if i else b - 1, name)

        def pe_back(pe, p, b):
            for c in range(C):
                if p == BACK_AT[f"z{c}"]:
                    back_free(pe, f"z{c}", b)
                    wait(pe, n_dve, b, f"n{c}")
                    nc.tensor.matmul(ps_b, wg, aoT[:, c, :], start=True, stop=True).then_inc(b_pe.sem, 1)
            for k in range(2):
                if p == BACK_AT[f"wo{k}"]:
                    wait(pe, b_dve, b, "gated")
                    back_free(pe, f"wo{k}", b)
                    for i in range(2):
                        t = 2 * k + i
                        for c in range(C):
                            last = nc.tensor.matmul(ps_b[:, i * D:(i + 1) * D], aoT[:, c, t * P:(t + 1) * P], w("f_o")[:, c, :],
                                                    start=(c == 0), stop=(c == C - 1))
                    last.then_inc(b_pe.sem, 1)
            for c in range(C):
                if p == BACK_AT[f"hT{c}"]:
                    wait(pe, b_pool, b, "h2w")
                    back_free(pe, f"hT{c}", b)
                    for t in range(T):
                        last = nc.tensor.transpose(ps_b[:, t * P:(t + 1) * P], h2[:, t, c * P:(c + 1) * P], ident)
                    last.then_inc(b_pe.sem, 1)
            if p == BACK_AT["lg"]:
                back_free(pe, "lg", b)
                for t in range(T):
                    for c in range(C):
                        last = nc.tensor.matmul(ps_b[:, t * NE:(t + 1) * NE], h2T[:, c, t * P:(t + 1) * P], w("r")[:, c, :],
                                                start=(c == 0), stop=(c == C - 1))
                last.then_inc(b_pe.sem, 1)

        def attend_at(p, i, attn, back):
            quad, kb = p // 6, p % 6 - 1
            if kb not in range(T):
                return None
            if quad:
                return (i, quad - 1, kb) if attn else None
            return (i - 1, QUADS - 1, kb) if back else None

        def pe_iteration(pe, i, head, front, attn, back):
            for p in range(POINTS):
                if attn:
                    for u in POINT_UNITS[p % 3]:
                        pe_scores(pe, i, p // 3, u)
                tile = attend_at(p, i, attn, back)
                if tile:
                    pe_attended(pe, *tile)
                if back:
                    pe_back(pe, p, i - 1)
                if front:
                    pe_front(pe, p, i + 1)

        def pipeline(eng, iteration):
            iteration(eng, -2, True, False, False, False)
            iteration(eng, -1, True, True, False, False)
            iteration(eng, 0, True, True, True, False)
            iteration(eng, 1, True, True, True, True)
            with eng.Fori(2, B - 2) as i:
                iteration(eng, i, True, True, True, True)
            iteration(eng, B - 2, False, True, True, True)
            iteration(eng, B - 1, False, False, True, True)
            iteration(eng, B, False, False, False, True)

        def act_evacuate(dst, unit, b, first=None):
            wait(nc.scalar, f_pe, b, unit)
            nc.scalar.activation(dst, fb(unit), ACT.Copy).then_inc(f_act.sem, 1)

        def act_front(act, p, b):
            def at(stage):
                return p == AT[stage]

            if at("xT"):
                wait(act, f_pe, b - 1, "qkv3")
                act_evacuate(xnT[:, 0, :], "xT0", b)
                act_evacuate(xnT[:, 1, :], "xT1", b)
            for t in range(T):
                if at(f"cT{t}"):
                    if t:
                        wait(act, f_pe, b, f"co{t - 1}")
                    else:
                        wait(act, f_pe, b - 1, f"co{T - 1}")
                    for g in range(2):
                        act_evacuate(cpT[:, 4 * g:4 * g + 4, :].rearrange("p j q -> p (j q)"), f"cT{t}{g}", b)
            for t in range(T):
                if at(f"exp{t}"):
                    wait(act, f_dve, b, f"csub{t}1")
                    nc.scalar.activation(cs[:, t % 2, :], cs[:, t % 2, :], ACT.Exp).then_inc(f_act.sem, 1)
            if at("h"):
                wait(act, f_dve, b, "y")
                wait(act, f_pool, b, "rms")
                for t in range(T):
                    last = nc.scalar.activation(xn[:, t, :], y[:, bass.ds(b % 2, 1), t, :].rearrange("p a d -> p (a d)"), ACT.Copy,
                                                scale=tiny[:, 5, t:t + 1])
                last.then_inc(f_act.sem, 1)
            if at("hT"):
                for c in range(C):
                    act_evacuate(xnT[:, c, :], f"hT{c}", b)
            if at("qkv1"):
                wait(act, f_dve, b, "qkv3")
                wait(act, f_dve, b - 1, "meansq")
                nc.scalar.activation(squares, qkv[:, :, 0:HS * E], ACT.Square).then_inc(f_act.sem, 1)
            if at("twice"):
                for m in range(2):
                    wait(act, f_dve, b, f"lo{m}")
                    queries = stack[:, m, :, 0:8, :].rearrange("p t h (k two e) -> p t (h k) two e", k=2, e=E)
                    nc.scalar.activation(queries[:, :, :, 1], queries[:, :, :, 0], ACT.Copy)
                    keys = stack[:, m, :, 8:10, :].rearrange("p t h (two n) -> p t h two n", two=2)
                    nc.scalar.activation(keys[:, :, :, 1], keys[:, :, :, 0], ACT.Copy).then_inc(f_act.sem, 1)
            for m, units in enumerate((ST0, ST1)):
                if at(f"st{m}"):
                    for n in units:
                        if n in ST_ACT:
                            st_evacuate(act, n, b)

        def st_evacuate(eng, n, b):
            wait(eng, f_pe, b, n)
            if n[2] == "k":
                m = int(n[3])
                wait(eng, a_pe, b - 1, f"s{4 * m + 3}{U - 1}")
                dst = sk[:, m, :]
            else:
                s = int(n[3])
                wait(eng, a_pe, b - 1, f"s{s}{U - 1}")
                dst = sq[:, s, :]
            if n in ST_ACT:
                nc.scalar.activation(dst, fb(n), ACT.Copy).then_inc(f_act.sem, 1)
            else:
                nc.vector.tensor_copy(dst, fb(n)).then_inc(f_dve.sem, 1)

        def act_attn(act, b, s, u):
            wait(act, a_pe, b, f"s{s}{u}")
            if u == 0:
                q = s // 2 - 2
                wait(act, v_pe, *((b, f"pv{q}{T - 1}") if q >= 0 else (b - 1, f"pv{q + QUADS}{T - 1}")))
            nc.scalar.activation(pt[:, s % 4, UNIT_AT[u]:UNIT_AT[u + 1]], ps_s[:, SCORE_BANK[f"s{s}{u}"], 0:UNIT_AT[u + 1] - UNIT_AT[u]], ACT.Exp, scale=SCALE).then_inc(a_act.sem, 1)

        def act_back(act, p, b):
            for c in range(C):
                if p == BACK_AT[f"z{c}"]:
                    wait(act, b_pe, b - 1, "lg")
                    wait(act, b_pe, b, f"z{c}")
                    nc.scalar.activation(gate[:, c, :], ps_b, ACT.Tanh, bias=tiny[:, 6, 0:1], scale=0.5).then_inc(b_act.sem, 1)
            for c in range(C):
                if p == BACK_AT[f"hT{c}"]:
                    wait(act, b_pe, b, f"hT{c}")
                    nc.scalar.activation(h2T[:, c, :], ps_b, ACT.Copy).then_inc(b_act.sem, 1)

        def act_iteration(act, i, head, front, attn, back):
            for p in range(POINTS):
                if attn:
                    for u in POINT_UNITS[p % 3]:
                        act_attn(act, i, p // 3, u)
                if back:
                    act_back(act, p, i - 1)
                if front:
                    act_front(act, p, i + 1)


        def dve_setup(dve):
            count = [0]

            def done(inst, then=True):
                count[0] += 1
                inst.then_inc(su_dve, 1)
                if then:
                    dve.wait_ge(su_dve, count[0])

            dve.wait_ge(loaded, 16 * SETUP_LOADS)
            dve.wait_ge(su_pe, 1)
            for g in range(C):
                done(nc.vector.tensor_scalar(kT[:, g, :], ps_f[:, g, :], prm("c_bk")[:, g:g + 1], None, ALU.add), False)
            for b in range(B):
                dve.wait_ge(su_pe, 2 + b)
                bank = ps_s[:, b % SCORE_BANKS, 0:D]
                done(nc.vector.tensor_tensor(v_all[:, b, :], bank, prm("c_bv"), ALU.add), False)
            done(nc.vector.tensor_tensor(wgt[:, :, WGT["qkv"][0]:WGT["qkv"][0] + QKV], w("qkv"),
                                    prm("ln1").unsqueeze(2).to_broadcast([P, C, QKV]), ALU.mult))
            done(nc.vector.tensor_scalar(w("f_o"), w("f_o"), 0.5, None, ALU.mult))
            done(nc.vector.tensor_tensor(prm("qkn"), prm("qkn"), prm("qn"), ALU.mult))
            done(nc.vector.tensor_tensor(wg, prm("Wg"), cst("same_head"), ALU.mult))
            done(nc.vector.tensor_scalar(tiny[:, 6, 0:1], prm("bg"), 0.5, None, ALU.mult))
            done(nc.vector.tensor_scalar(delta_r, delta_r, SCALE, None, ALU.mult))
            done(nc.vector.tensor_copy(delta_parts[:, 0, :], delta_r))
            done(nc.vector.tensor_tensor(delta_s, delta_r, delta_parts[:, 0, :], ALU.subtract))
            done(nc.vector.tensor_copy(delta_parts[:, 1, :], delta_s))
            done(nc.vector.tensor_tensor(delta_r, delta_s, delta_parts[:, 1, :], ALU.subtract))
            done(nc.vector.tensor_copy(delta_parts[:, 2, :], delta_r))
            done(nc.vector.tensor_scalar(delta_s, delta_parts[:, 0, :], cst("part", 3)[:, 0:1], None, ALU.mult))
            done(nc.vector.scalar_tensor_tensor(delta_r, delta_parts[:, 1, :], cst("part", 3)[:, 1:2], delta_s, ALU.mult, ALU.add))
            done(nc.vector.scalar_tensor_tensor(delta3[:], delta_parts[:, 2, :], cst("part", 3)[:, 2:3], delta_r, ALU.mult, ALU.add))
            done(nc.vector.memset(ones3[:], 1.0))
            assert count[0] == SETUP_DVE

        def dve_stats(dve, k, src, b, st, names):
            for t in range(T):
                last = nc.vector.bn_stats(stats[:, k, t, :], src(t))
            last.then_inc(st.sem, 1)
            wait_apart(dve, st, b, names[0])
            for t in range(T):
                last = nc.vector.bn_aggr(mv[:, k, t, :], stats[:, k, t, :])
            last.then_inc(st.sem, 1)

        def dve_head(dve, p, b):
            if p == HEAD_AT["ln1"]:
                dve.wait_ge(x_loaded, b * 16 + 16)
                wait(dve, h_pool, b - 1, "ln1_rstd")
                dve_stats(dve, 0, lambda t: x_in[:, t, :], b, h_dve, ["ln1_stats"])
            if p == HEAD_AT["xn"]:
                wait(dve, h_pool, b, "ln1_rstd")
                wait(dve, f_pe, b - 1, "hT1")
                for t in range(T):
                    last = nc.vector.tensor_scalar(xn[:, t, :], x_in[:, t, :], mv[:, 0, t, 0:1], tiny[:, 1, t:t + 1], ALU.subtract, ALU.mult)
                last.then_inc(h_dve.sem, 1)

        def dve_front(dve, p, b):
            def at(stage):
                return p == AT[stage]

            if at("cq"):
                wait(dve, f_pe, b - 1, "wo1")
                for g in range(C):
                    wait(dve, f_pe, b, f"cq{g}")
                    nc.vector.tensor_scalar(cqT[:, g, :], fb(f"cq{g}"), prm("c_bq")[:, g:g + 1], prm("tau")[:, bass.ds(b, 1)],
                                            ALU.add, ALU.mult).then_inc(f_dve.sem, 1)

            def softmax_shift(t):
                wait(dve, f_pe, b, f"cs{t}1")
                nc.vector.tensor_reduce(cmax[:, t % 2, :], ps_f[:, 0:C].rearrange("p g (h s) -> p (g h) s", h=PAIRS), X, ALU.max).then_inc(f_dve.sem, 1)
                wait(dve, f_dve, b, f"cmax{t}")
                wait(dve, f_pe, *((b, f"cT{t - 2}1") if t >= 2 else (b - 1, f"cT{t + 2}1")))
                for g in range(C):
                    nc.vector.tensor_tensor(cs[:, t % 2, g * L:(g + 1) * L].rearrange("p (h s) -> p h s", h=PAIRS),
                                            ps_f[:, g, :].rearrange("p (h s) -> p h s", h=PAIRS),
                                            cmax[:, t % 2, g * PAIRS:(g + 1) * PAIRS].unsqueeze(2).to_broadcast([P, PAIRS, S]),
                                            ALU.subtract).then_inc(f_dve.sem, 1)

            def normalise(t):
                wait(dve, f_pe, b, f"co{t}")
                sums = fb(f"co{t}").rearrange("p (k c q) -> p k c q", k=2, c=C)
                nc.vector.reciprocal(crec, sums[:, 1]).then_inc(f_dve.sem, 1)
                wait(dve, f_dve, b, f"crec{t}")
                nc.vector.tensor_tensor(coT[:, :, t * P:(t + 1) * P], sums[:, 0], crec, ALU.mult).then_inc(f_dve.sem, 1)

            for t in range(T):
                if at(f"co{t}"):
                    normalise(t)
            for t in range(T):
                if at(f"cs{t}"):
                    softmax_shift(t)
            if at("wo"):
                wait(dve, h_pool, b, "xbo")
                if isinstance(b, int) and b < 2:
                    pass
                else:
                    dve.wait_ge(rows_stored, (b - 1) * 32)
                for k in range(2):
                    wait(dve, f_pe, b, f"wo{k}")
                    nc.vector.tensor_tensor(x1[:, bass.ds(b % 2, 1), 2 * k:2 * k + 2, :].rearrange("p a t d -> p (a t) d"),
                                            fb(f"wo{k}").rearrange("p (t d) -> p t d", t=2), x_in[:, 2 * k:2 * k + 2, :],
                                            ALU.add).then_inc(f_dve.sem, 1)
                wait(dve, f_dve, b, "x1_1")
                wait_apart(dve, f_pool, b - 1, "meansq")
                dve_stats(dve, 1, lambda t: x1[:, bass.ds(b % 2, 1), t, :].rearrange("p a d -> p (a d)"), b, f_dve, ["ln2_stats"])
            if at("y"):
                wait(dve, f_pool, b, "ln2_rstd")
                wait(dve, b_pool, b - 2, "res")
                for t in range(T):
                    last = nc.vector.tensor_scalar(y[:, bass.ds(b % 2, 1), t, :].rearrange("p a d -> p (a d)"),
                                                   x1[:, bass.ds(b % 2, 1), t, :].rearrange("p a d -> p (a d)"),
                                                   mv[:, 1, t, 0:1], tiny[:, 3, t:t + 1], ALU.subtract, ALU.mult)
                last.then_inc(f_dve.sem, 1)
            for k in range(2):
                if not at(f"qkv{k}"):
                    continue
                if k == 0:
                    wait(dve, v_dve, b - 1, "v")
                    wait(dve, f_pool, b - 1, "sin2")
                for t in (2 * k, 2 * k + 1):
                    wait(dve, f_pe, b, f"qkv{t}")
                    nc.vector.tensor_tensor(qkv[:, t, :], fb(f"qkv{t}")[:, 0:QKV], prm("bqkv"), ALU.add).then_inc(f_dve.sem, 1)
            qk = qkv[:, :, 0:HS * E].rearrange("p t (h e) -> p t h e", e=E)
            ra = rope_a[:, :, :].rearrange("p t (h e) -> p t h e", e=E)
            flat_a = rope_a[:, :, :].rearrange("p t n -> p (t n)")
            flat_b = rope_b[:, :, :].rearrange("p t n -> p (t n)")
            if at("rope"):
                wait(dve, f_dve, b, "qkv3")
                cos = cst("cos").rearrange("p (t e) -> p t e", t=T)
                for half in range(2):
                    last = nc.vector.tensor_tensor(ra[:, :, :, 8 * half:8 * half + 8], qk[:, :, :, 8 * half:8 * half + 8],
                                                   cos.unsqueeze(2).to_broadcast([P, T, HS, 8]), ALU.mult)
                last.then_inc(f_dve.sem, 1)
                wait(dve, f_act, b, "square")
                nc.vector.tensor_reduce(qk_ms, squares.rearrange("p t (h e) -> p (t h) e", e=E), X, ALU.add).then_inc(f_dve.sem, 1)
                wait(dve, f_dve, b, "meansq")
                nc.vector.tensor_scalar(qk_ms, qk_ms, 1.0 / E, RMS_EPS, ALU.mult, ALU.add).then_inc(f_dve.sem, 1)
                wait(dve, f_dve, b, "qk_eps")
                nc.vector.tensor_scalar(qk_rs.bitcast(I32), qk_ms.bitcast(I32), 1, None, ALU.logical_shift_right).then_inc(f_dve.sem, 1)
                wait(dve, f_dve, b, "half_bits")
                nc.vector.tensor_scalar(qk_rs.bitcast(I32), qk_rs.bitcast(I32), -1.0, float(0x5F375A86), ALU.mult, ALU.add).then_inc(f_dve.sem, 1)
                before = "guess"
                for k in range(3):
                    wait(dve, f_dve, b, before)
                    nc.vector.scalar_tensor_tensor(qk_t, qk_rs, -0.5, qk_rs, ALU.mult, ALU.mult).then_inc(f_dve.sem, 1)
                    wait(dve, f_dve, b, f"newton_a{k}")
                    nc.vector.tensor_tensor(qk_t, qk_t, qk_ms, ALU.mult).then_inc(f_dve.sem, 1)
                    wait(dve, f_dve, b, f"newton_b{k}")
                    nc.vector.scalar_tensor_tensor(qk_rs, qk_t, 1.5, qk_rs, ALU.add, ALU.mult).then_inc(f_dve.sem, 1)
                    before = f"newton_c{k}"
            if at("norm"):
                wait(dve, f_pool, b, "rope")
                wait(dve, f_dve, b, "newton_c2")
                nc.vector.tensor_tensor(flat_a.rearrange("p (h e) -> p h e", e=E), flat_a.rearrange("p (h e) -> p h e", e=E),
                                        qk_rs.unsqueeze(2).to_broadcast([P, T * HS, E]), ALU.mult).then_inc(f_dve.sem, 1)
                wait(dve, f_dve, b, "qnorm")
                keys = rope_a[:, :, H * E:HS * E]
                nc.vector.tensor_tensor(keys, keys, prm("qkn").unsqueeze(1).to_broadcast([P, T, KV * E]), ALU.mult).then_inc(f_dve.sem, 1)
            if at("split"):
                wait(dve, f_dve, b, "kweight")
                for m in range(2):
                    wait(dve, f_pe, b - 1, (ST0, ST1)[m][-1])
                    groups = [(ra[:, :, 8 * m:8 * m + 8, :], stack[:, m, :, 0:8, :], 2), (ra[:, :, H + 2 * m:H + 2 * m + 2, :], stack[:, m, :, 8:10, :], 1)]
                    for value, heads, lo in groups:
                        last = nc.vector.tensor_scalar(heads[:, :, :, 0:E].bitcast(I32), value.bitcast(I32), HI_MASK, None, ALU.bitwise_and)
                    last.then_inc(f_dve.sem, 1)
                    wait(dve, f_dve, b, f"hi{m}")
                    for value, heads, lo in groups:
                        last = nc.vector.tensor_tensor(heads[:, :, :, lo * E:(lo + 1) * E], value, heads[:, :, :, 0:E], ALU.subtract)
                    last.then_inc(f_dve.sem, 1)
            for m, units in enumerate((ST0, ST1)):
                if at(f"st{m}"):
                    for n in units:
                        if n not in ST_ACT:
                            st_evacuate(dve, n, b)

        def dve_values(dve, b):
            wait(dve, f_dve, b, "qkv3")
            wait(dve, v_pe, b - 1, ATTENDED[-1])
            for t in range(T):
                last = nc.vector.tensor_copy(v_pad[:, t, :, E:2 * E], qkv[:, t, HS * E:].rearrange("p (g e) -> p g e", e=E))
            last.then_inc(v_dve.sem, 1)

        def dve_normalise(dve, b, m):
            wait(dve, v_pe, b, f"pv{2 * m + 1}{T - 1}")
            if m == 0:
                wait(dve, b_pe, b - 1, "wo1")
            nc.vector.reciprocal(rec, ps_v[:, 1, :]).then_inc(n_dve.sem, 1)
            wait(dve, n_dve, b, f"rec{m}")
            nc.vector.tensor_tensor(aoT[:, m, :], ps_v[:, 0, :], rec, ALU.mult).then_inc(n_dve.sem, 1)

        def dve_back(dve, p, b):
            fg, fa = gate[:, :, :].rearrange("p c n -> p (c n)"), aoT[:, :, :].rearrange("p c n -> p (c n)")
            if p == BACK_AT["gated"]:
                wait(dve, b_act, b, "gate1")
                nc.vector.scalar_tensor_tensor(fa, fg, 1.0, fa, ALU.add, ALU.mult).then_inc(b_dve.sem, 1)
            yb = y[:, bass.ds(b % 2, 1), :, :].rearrange("p a t d -> p (a t) d")
            for k in range(2):
                if p == BACK_AT[f"wo{k}"]:
                    wait(dve, f_pool, b, "ybo")
                    wait(dve, b_pe, b, f"wo{k}")
                    nc.vector.tensor_tensor(yb[:, 2 * k:2 * k + 2, :], ps_b.rearrange("p (t d) -> p t d", t=2), yb[:, 2 * k:2 * k + 2, :],
                                            ALU.add).then_inc(b_dve.sem, 1)
            if p == BACK_AT["wo1"]:
                wait(dve, b_dve, b, "in1")
                wait_apart(dve, b_pool, b - 1, "ms")
                dve_stats(dve, 2, lambda t: yb[:, t, :], b, b_dve, ["stats"])
            if p == BACK_AT["h2"]:
                wait(dve, b_pool, b, "rms")
                wait(dve, b_pe, b - 1, "hT1")
                if not (isinstance(b, int) and b < 1):
                    dve.wait_ge(rows_stored, b * 32)
                for t in range(T):
                    last = nc.vector.tensor_scalar(h2[:, t, :], yb[:, t, :], tiny[:, 10, t:t + 1], None, ALU.mult)
                last.then_inc(b_dve.sem, 1)
            if p == BACK_AT["lg"]:
                wait(dve, b_pe, b, "lg")
                nc.vector.tensor_tensor(logits[:, bass.ds(b * T, T), :], ps_b[:, 0:T * NE].rearrange("p (t e) -> p t e", t=T),
                                        prm("br").unsqueeze(1).to_broadcast([P, T, NE]), ALU.add).then_inc(b_dve.sem, 1)

        def dve_iteration(dve, i, head, front, attn, back):
            for p in range(POINTS):
                if p == 5:
                    if back:
                        dve_normalise(dve, i - 1, 1)
                    if attn:
                        dve_values(dve, i)
                if p == 17 and attn:
                    dve_normalise(dve, i, 0)
                if back:
                    dve_back(dve, p, i - 1)
                if front:
                    dve_front(dve, p, i + 1)
                if head:
                    dve_head(dve, p, i + 2)

        def pool_setup(pool):
            nc.gpsimd.memset(ln_eps[:], LN_EPS)
            nc.gpsimd.memset(rms_eps[:], RMS_EPS)
            nc.gpsimd.memset(half_power[:], -0.5).then_inc(su_pool, 1)
            nc.gpsimd.memset(v_pad, 0.0).then_inc(su_pool, 1)
            pool.wait_ge(su_dve, 2)
            nc.gpsimd.tensor_scalar(kT.rearrange("p c n -> p (c n)"), kT.rearrange("p c n -> p (c n)"), SCALE, 0.0,
                                    ALU.mult, ALU.add).then_inc(su_pool, 1)

        def rsqrt(dst, src, eps, steps, b, names):
            nc.gpsimd.tensor_tensor(dst, src, eps, ALU.add).then_inc(steps.sem, 1)
            wait(nc.gpsimd, steps, b, names[0])
            nc.gpsimd.tensor_tensor(dst, dst, half_power[:], ALU.pow).then_inc(steps.sem, 1)

        def pool_head(pool, p, b):
            if p == HEAD_AT["ln1"]:
                if isinstance(b, int) and b == 0:
                    pool.wait_ge(su_pool, 3)
                    pool.wait_ge(su_dve, SETUP_DVE)
                wait(pool, h_dve, b, "ln1_aggr")
                rsqrt(tiny[:, 1, :], mv[:, 0, :, 1], ln_eps[:], h_pool, b, ["ln1_eps"])
            if p == HEAD_AT["kbd"]:
                wait(pool, f_pe, b - 1, "cs31")
                for g in range(C):
                    last = nc.gpsimd.tensor_tensor(kbd[:, g, :, :], kT[:, g, bass.ds(b * S, S)].unsqueeze(1).to_broadcast([P, PAIRS, S]),
                                                   cst("head_of").unsqueeze(2).to_broadcast([P, PAIRS, S]), ALU.mult)
                last.then_inc(h_pool.sem, 1)
                wait(pool, f_pe, b - 1, "co3")
                nc.gpsimd.tensor_tensor(vbd.rearrange("p j (x e) -> p j x e", x=2), v_all[:, bass.ds(b, 1), :].rearrange("p a (j x e) -> p (a j) x e", x=2, e=E),
                                        cst("half").unsqueeze(1).unsqueeze(3).to_broadcast([P, PAIRS, 2, E]), ALU.mult).then_inc(h_pool.sem, 1)
            if p == HEAD_AT["xn"]:
                wait(pool, h_dve, b, "xn")
                nc.gpsimd.tensor_tensor(x_in, x_in, prm("c_bo").unsqueeze(1).to_broadcast([P, T, D]), ALU.add).then_inc(h_pool.sem, 1)

        def pool_front(pool, p, b):
            def ew(dst, a, c, op):
                nc.gpsimd.tensor_tensor(dst, a, c, op).then_inc(f_pool.sem, 1)

            def at(stage):
                return p == AT[stage]

            if at("wo"):
                wait(pool, f_dve, b, "ln2_aggr")
                rsqrt(tiny[:, 3, :], mv[:, 1, :, 1], ln_eps[:], f_pool, b, ["ln2_eps"])
                wait(pool, f_pool, b, "ln2_rstd")
                ew(tiny[:, 4, :], tiny[:, 3, :], tiny[:, 3, :], ALU.mult)
                wait(pool, f_pool, b, "rstd2")
                ew(tiny[:, 11, :], tiny[:, 4, :], mv[:, 1, :, 1], ALU.mult)
                wait(pool, f_pool, b, "meansq")
                rsqrt(tiny[:, 5, :], tiny[:, 11, :], rms_eps[:], f_pool, b, ["rms_eps"])
            if at("hT"):
                wait(pool, f_act, b, "h")
                yb = y[:, bass.ds(b % 2, 1), :, :].rearrange("p a t d -> p (a t) d")
                ew(yb, yb, prm("f_bo").unsqueeze(1).to_broadcast([P, T, D]), ALU.add)
            if at("rope"):
                wait(pool, f_dve, b, "qkv3")
                qk = qkv[:, :, 0:HS * E].rearrange("p t (h e) -> p t h e", e=E)
                rb = rope_b[:, :, :].rearrange("p t (h e) -> p t h e", e=E)
                for lo, hi, name in ((0, 8, "negsin"), (8, 0, "sin")):
                    ew(rb[:, :, :, lo:lo + 8], qk[:, :, :, hi:hi + 8],
                       cst(name).rearrange("p (t e) -> p t e", t=T).unsqueeze(2).to_broadcast([P, T, HS, 8]), ALU.mult)
                wait(pool, f_pool, b, "sin2")
                wait(pool, f_dve, b, "cosmul")
                ew(rope_a[:, :, :], rope_a[:, :, :], rope_b[:, :, :], ALU.add)

        def pool_mask(pool, b, s, v):
            units = POINT_UNITS[v]
            wait(pool, a_act, b, f"s{s}{units[-1]}")
            a, width = UNIT_AT[units[0]], UNIT_AT[units[1]] - UNIT_AT[units[0]]
            k = 4 if v == 1 else 1
            d = pt[:, s % 4, a:a + 2 * width].rearrange("p (x k q) -> p x k q", x=2, q=P)[:, :, 0:k:3, :]
            nc.gpsimd.tensor_tensor(d, d, cst("causal").unsqueeze(1).unsqueeze(1).to_broadcast([P, 2, d.shape[2], P]), ALU.mult).then_inc(a_pool.sem, 1)

        def pool_back(pool, p, b):
            def ew(dst, a, c, op):
                nc.gpsimd.tensor_tensor(dst, a, c, op).then_inc(b_pool.sem, 1)

            yb = y[:, bass.ds(b % 2, 1), :, :].rearrange("p a t d -> p (a t) d")
            xb = x1[:, bass.ds(b % 2, 1), :, :].rearrange("p a t d -> p (a t) d")
            if p == BACK_AT["rms"]:
                wait(pool, b_dve, b, "aggr")
                ew(tiny[:, 7, :], mv[:, 2, :, 0], mv[:, 2, :, 0], ALU.mult)
                wait(pool, b_pool, b, "msq")
                ew(tiny[:, 8, :], tiny[:, 7, :], mv[:, 2, :, 1], ALU.add)
                wait(pool, b_pool, b, "ms")
                rsqrt(tiny[:, 10, :], tiny[:, 8, :], rms_eps[:], b_pool, b, ["rms_eps"])
            if p == BACK_AT["h2"]:
                ew(xb, xb, yb, ALU.add)
            if p == BACK_AT["weight"]:
                wait(pool, b_dve, b, "h2")
                ew(h2, h2, prm("ln2").unsqueeze(1).to_broadcast([P, T, D]), ALU.mult)

        def pool_iteration(pool, i, head, front, attn, back):
            for p in range(POINTS):
                if attn:
                    pool_mask(pool, i, p // 3, p % 3)
                if back:
                    pool_back(pool, p, i - 1)
                if front:
                    pool_front(pool, p, i + 1)
                if head:
                    pool_head(pool, p, i + 2)

        block = ctx.enter_context(nc.Block())

        @block.sync
        def _(sp):
            sp.dma_start(const[:], ins["const"]).then_inc(loaded, 16)
            sp.dma_start(par, ins["par"]).then_inc(loaded, 16)
            sp.dma_start(delta_r, ins["delta"].to_broadcast([3, B * S])).then_inc(loaded, 16)
            sp.dma_start(ctxw, ins["ctxw"].rearrange("(c p) n -> p c n", p=P)).then_inc(loaded, 16)
            sp.dma_start(wgt, ins["wgt"].rearrange("(c p) n -> p c n", p=P)).then_inc(loaded, 16)

            def load_x(b):
                wait(sp, f_dve, b - 1, "x1_1")
                sp.dma_start(x_in, ins["x"][bass.ds(b * L, L), :].rearrange("(t p) d -> p t d", p=P)).then_inc(x_loaded, 16)

            def store_rows(b):
                rows = rows_dram[bass.ds(b * L, L), :].rearrange("(t p) d -> p t d", p=P)
                wait(sp, b_pool, b, "h2w")
                sp.dma_start(rows[:, :, 0:D], h2).then_inc(rows_stored, 16)
                wait(sp, b_pool, b, "res")
                par2 = b % 2
                sp.dma_start(rows[:, :, D:2 * D], x1[:, bass.ds(par2, 1), :, :].rearrange("p a t d -> p (a t) d")).then_inc(rows_stored, 16)

            load_x(0)
            load_x(1)
            with sp.Fori(2, B) as b:
                load_x(b)
                store_rows(b - 2)
            early_loads(sp)
            store_rows(B - 2)
            store_rows(B - 1)
            moe_loads(sp)

        @block.tensor
        def _(pe):
            pe_setup(pe)
            pe.wait_ge(su_dve, SETUP_DVE)
            pipeline(pe, pe_iteration)
            pe_routing(pe)
            pe_moe(pe)

        @block.scalar
        def _(act):
            act.wait_ge(su_dve, SETUP_DVE)
            pipeline(act, act_iteration)
            act_moe(act)

        @block.vector
        def _(dve):
            dve_setup(dve)
            pipeline(dve, dve_iteration)
            dve_routing(dve)
            dve_moe(dve)

        @block.gpsimd
        def _(pool):
            assert pool is nc.gpsimd
            pool_setup(pool)
            pipeline(pool, pool_iteration)
            pool_routing(pool)
            pool_moe(pool)


def shape_constants():
    p, t = np.arange(P), np.arange(T)
    inv_freq = (1.0 / 10000.0 ** (np.arange(0, E, 2, dtype=np.float32) / E)).astype(np.float32)
    angle = ((t[None, :, None] * P + p[:, None, None]).astype(np.float32) * inv_freq).astype(np.float32)
    rows = {
        "ident": np.eye(P), "causal": p[:, None] <= p[None, :], "before": p[:, None] < p[None, :], "ones": np.ones((P, P)),
        "same_head": p[:, None] // E == p[None, :] // E, "row": np.tile(p, (P, 1)),
        "head_of": p[:, None] // E == np.arange(PAIRS), "half": p[:, None] // S == np.arange(2),
        "part": p[:, None] == np.arange(3),
        "cos": np.cos(angle).reshape(P, -1), "sin": np.sin(angle).reshape(P, -1), "negsin": -np.sin(angle).reshape(P, -1),
        "tile_limit": np.tile(np.where(np.arange(TT) == 0, -1, P * np.arange(TT)), (P, 1)),
        "earlier": np.tile((np.arange(NE)[None, :] < np.arange(NE)[:, None]).reshape(1, -1), (P, 1)),
        "rank": np.tile(NE - np.arange(NE), (P, 1)), "tile_no": np.tile(np.arange(NT + 1), (P, 1)),
        "token": np.arange(TT)[None, :] * P + p[:, None],
        "pair_ones": p[:, None] // S == np.arange(2 * E) // E,
        "slot_ones": np.tile(np.arange(3 * E) // E == 1, (P, 1)),
    }
    return np.concatenate([rows[name].astype(np.float32) for name in CONST], axis=1)


def kernel(**inputs):
    from concourse import bacc
    from concourse.bass_utils import run_bass_kernel_spmd

    a = {k: np.asarray(v) for k, v in inputs.items()}
    c, f = {k[9:]: v for k, v in a.items() if k.startswith("L0_xcond_")}, {k[7:]: v for k, v in a.items() if k.startswith("L0_ffn_")}

    order = np.array([8 * m + 4 * x + r for m in range(2) for r in range(4) for x in range(2)])
    cols = (order[:, None] * E + np.arange(E)[None, :]).reshape(-1)

    order_o = np.array([8 * m + 4 * x + 2 * j + i for m in range(2) for i in range(2) for x in range(2) for j in range(2)])
    rows_o = (order_o[:, None] * E + np.arange(E)[None, :]).reshape(-1)

    def row(v):
        return np.broadcast_to(v.reshape(1, -1), (P, v.size))

    def col(v):
        return v.reshape(-1, P).T

    par = {
        "c_bo": row(c["bo"]), "bqkv": row(np.concatenate([f["bq"][cols], f["bk"], f["bv"]])), "f_bo": row(f["bo"]), "ln2": row(f["ln2_w"]),
        "qkn": row(np.tile(f["kn_w"], KV)), "qn": row(np.tile(f["qn_w"], KV)), "br": row(f["br"]), "c_bv": row(c["bv"]),
        "tau": row(a["condB_tau"]), "c_bq": col(c["bq"]), "c_bk": col(c["bk"]),
        "bg": np.tile(f["bg"], PAIRS)[:, None], "ln1": col(f["ln1_w"]), "Wg": np.tile(f["Wg"], (PAIRS, PAIRS)),
    }
    wgt = np.concatenate([c["Wq"].T, c["Wo"].T, f["Wq"][:, cols], f["Wk"], f["Wv"], f["Wo"][rows_o, :], f["Wr"]], axis=1)
    ctxw = np.concatenate([c["Wk"].T, c["Wv"].T, a["ctx_1024"].reshape(B * S, D).T], axis=1)
    arrays = {
        "x": a["x"].reshape(N, D), "const": shape_constants(), "par": np.concatenate([par[name] for name in PAR], axis=1),
        "delta": a["fside_BxS2_0"].reshape(1, -1), "wgt": wgt, "ctxw": ctxw, "W1": f["W1"], "W2": f["W2"], "b1": f["b1"], "b2": f["b2"],
    }
    arrays = {k: np.ascontiguousarray(v) for k, v in arrays.items()}

    nc = bacc.Bacc("TRN2", target_bir_lowering=False, num_devices=1)
    ins = {k: nc.dram_tensor(f"in_{k}", v.shape, mybir.dt.from_np(v.dtype), kind="ExternalInput").ap() for k, v in arrays.items()}
    out = nc.dram_tensor("out", (N, D), F32, kind="ExternalOutput").ap()
    build(nc, ins, out)
    r = run_bass_kernel_spmd(nc, [{f"in_{k}": v for k, v in arrays.items()}], core_ids=[0])
    return r.results[0]["out"].reshape(B, L, D)
```

```python
from contextlib import ExitStack

import numpy as np

import concourse.bass as bass
from concourse import mybir

F32 = mybir.dt.float32
F32R = mybir.dt.float32r
BF16 = mybir.dt.bfloat16
I32 = mybir.dt.int32
U32 = mybir.dt.uint32
ALU = mybir.AluOpType
ACT = mybir.ActivationFunctionType
X = mybir.AxisListType.X

P = 128
B, L, D = 8, 512, 256
S = 64
H, E = 16, 16
KV = 4
HS = H + KV
QKV = (H + 2 * KV) * E
NE, HID = 8, 512
C = D // P
T = L // P
TT = B * T
N = B * L
NT = TT + NE - 1
PAIRS = H // 2
LN_EPS, RMS_EPS = 1e-5, 1e-6
SCALE = 0.25
HI_MASK = -4096
ARENA = 45600
OUT_OF_RANGE = 8192

def columns(parts):
    at, n = {}, 0
    for name, width in parts:
        at[name] = (n, width)
        n += width
    return at, n


CONST, CONST_N = columns([
    ("ident", P), ("causal", P), ("before", P), ("ones", P), ("same_head", P), ("row", P),
    ("head_of", PAIRS), ("half", 2), ("part", 3), ("cos", T * E // 2), ("sin", T * E // 2), ("negsin", T * E // 2),
    ("tile_limit", TT), ("earlier", NE * NE), ("rank", NE), ("tile_no", NT + 1), ("token", TT), ("pair_ones", 2 * E), ("slot_ones", 3 * E),
])
PAR, PAR_N = columns([
    ("c_bo", D), ("bqkv", QKV), ("f_bo", D), ("ln2", D), ("qkn", KV * E), ("qn", KV * E), ("br", NE), ("c_bv", D),
    ("tau", B), ("c_bq", C), ("c_bk", C), ("bg", 1), ("ln1", C), ("Wg", P),
])
WGT, WGT_N = columns([("c_q", D), ("c_o", D), ("qkv", QKV), ("f_o", D), ("r", NE)])
CTX, CTX_N = columns([("c_k", D), ("c_v", D), ("ctx", B * S)])


class Steps:

    def __init__(self, sem, names):
        self.sem, self.names = sem, list(names)
        self.n = len(self.names)
        self.index = {name: i for i, name in enumerate(self.names)}
        assert len(self.index) == self.n

    def value(self, b, name=None):
        return b * self.n + (self.index[name] + 1 if name else self.n)


def begun(b):
    return not (isinstance(b, int) and b < 0)


POINTS = 3 * PAIRS
AT = {"cs0": 0, "cs1": 1, "cT0": 2, "cs2": 3, "co0": 3, "cT1": 4, "cs3": 5, "co1": 5,
      "cT2": 6, "co2": 7, "cT3": 8, "co3": 9, "wo": 10, "ln2": 11, "y": 11, "h": 13, "hT": 14, "qkv0": 15, "qkv1": 16,
      "rope": 17, "norm": 17, "split": 18, "twice": 21, "st0": 21, "st1": 23}
for t in range(T):
    AT[f"exp{t}"] = AT[f"cs{t}"] + 1
HEAD_AT = {"ln1": 14, "kbd": 15, "xn": 15, "xT": 17, "cq": 18}
HEAD_POINTS = sorted(set(HEAD_AT.values()))
BACK_AT = {"z0": 4, "z1": 6, "gated": 6, "wo0": 7, "wo1": 8, "rms": 9, "h2": 9, "res": 9, "hT0": 14, "hT1": 16, "lg": 18}


def in_order(at, stages):
    return [name for p in range(POINTS) for stage, names in stages if at[stage] == p for name in names]


TILES4 = range(T)
ST0, ST1 = ["stk0", "stq0", "stq1", "stq2", "stq3"], ["stk1", "stq4", "stq5", "stq6", "stq7"]
ST_ACT = ST0[0::2] + ST1[1::2]
NEWTON = [f"{op}{k}" for k in range(3) for op in ("newton_a", "newton_b", "newton_c")]
FRONT_PE = in_order(AT, [(f"co{t}", [f"co{t}"]) for t in TILES4]
                    + [(f"cT{t}", [f"cT{t}0", f"cT{t}1"]) for t in TILES4]
                    + [(f"cs{t}", [f"cs{t}0", f"cs{t}1"]) for t in TILES4]
                    + [("wo", ["wo0", "wo1"]), ("hT", ["hT0", "hT1"]), ("qkv0", ["qkv0", "qkv1"]), ("qkv1", ["qkv2", "qkv3"]),
                       ("st0", ST0), ("st1", ST1)])
FRONT_ACT = in_order(AT, [(f"cT{t}", [f"cT{t}0", f"cT{t}1"]) for t in TILES4]
                     + [(f"exp{t}", [f"cexp{t}"]) for t in TILES4]
                     + [("h", ["h"]), ("hT", ["hT0", "hT1"]), ("qkv1", ["square"]), ("twice", ["twice0", "twice1"]), ("st0", [n for n in ST0 if n in ST_ACT]), ("st1", [n for n in ST1 if n in ST_ACT])])
FRONT_DVE = in_order(AT, [(f"co{t}", [f"crec{t}", f"co{t}"]) for t in TILES4]
                     + [(f"cs{t}", [f"cmax{t}", f"csub{t}0", f"csub{t}1"]) for t in TILES4]
                     + [("wo", ["x1_0", "x1_1", "ln2_stats", "ln2_aggr"]), ("y", ["y"]), ("qkv0", ["qkv0", "qkv1"]), ("qkv1", ["qkv2", "qkv3"]),
                        ("rope", ["cosmul", "meansq", "qk_eps", "half_bits", "guess"] + NEWTON),
                        ("norm", ["qnorm", "kweight"]), ("split", ["hi0", "lo0", "hi1", "lo1"]),
                        ("st0", [n for n in ST0 if n not in ST_ACT]), ("st1", [n for n in ST1 if n not in ST_ACT])])
FRONT_POOL = in_order(AT, [("ln2", ["ln2_eps", "ln2_rstd", "rstd2", "meansq", "rms_eps", "rms"]),
                           ("hT", ["ybo"]), ("rope", ["sin1", "sin2", "rope"])])
HEAD_PE, HEAD_ACT = ["xT0", "xT1", "cq0", "cq1"], ["xT0", "xT1"]
HEAD_DVE = ["ln1_stats", "ln1_aggr", "xn", "cq0", "cq1"]
HEAD_POOL = ["ln1_eps", "ln1_rstd", "kbd", "vbd", "xbo"]
U = 6
UNITS = [f"s{s}{u}" for s in range(PAIRS) for u in range(U)]
POINT_UNITS = [(0, 1), (2, 3), (4, 5)]
MASKS = [f"m{s}{v}" for s in range(PAIRS) for v in range(3)]
QUADS = PAIRS // 2
ATTENDED = [f"pv{q}{kb}" for q in range(QUADS) for kb in range(T)]
BACK_PE = in_order(BACK_AT, [(n, [n]) for n in ("z0", "z1", "wo0", "wo1", "hT0", "hT1", "lg")])
BACK_ACT = in_order(BACK_AT, [("z0", ["gate0"]), ("z1", ["gate1"]), ("hT0", ["hT0"]), ("hT1", ["hT1"])])
BACK_DVE = in_order(BACK_AT, [("gated", ["gated"]), ("wo0", ["in0"]), ("wo1", ["in1", "stats", "aggr"]), ("h2", ["h2"]), ("lg", ["lg"])])
BACK_POOL = in_order(BACK_AT, [("rms", ["msq", "ms", "rms_eps", "rms"]), ("res", ["res"])])

FRONT_BANKS = 3
CROSS_BANK = {"cs": (0, 1), "cT": (0, 1), "co": (2, 2)}
assert AT["qkv1"] < HEAD_AT["xT"] < HEAD_AT["cq"] < AT["st0"]
k = FRONT_PE.index("stk0")
BANKED = FRONT_PE[:k] + HEAD_PE + FRONT_PE[k:]
FRONT_BANK, i = {}, 0
for name in BANKED:
    if name[:2] in CROSS_BANK:
        FRONT_BANK[name] = CROSS_BANK[name[:2]][int(name[-1]) % 2]
    else:
        FRONT_BANK[name] = i % FRONT_BANKS
        i += 1
SCORE_BANKS = 2
SCORE_BANK = {name: i % SCORE_BANKS for i, name in enumerate(UNITS)}


def before_in_ring(units, bank, name):
    same = [n for n in units if bank[n] == bank[name]]
    i = same.index(name)
    return (same[i - 1], 0) if i else (same[-1], 1)


def before_in_bank(name, head):
    i = BANKED.index(name)
    for j in range(i - 1, i - len(BANKED) - 1, -1):
        n = BANKED[j]
        if FRONT_BANK[n] == FRONT_BANK[name] and (head or j < 0 or n not in HEAD_PE):
            return n, (name in HEAD_PE) - (n in HEAD_PE) + (j < 0)
    raise ValueError(name)


def build(nc, ins, out):
    with ExitStack() as ctx:
        def sb(name, shape, dt=F32):
            return ctx.enter_context(nc.sbuf_tensor(name, shape, dt))

        def sem(name):
            return ctx.enter_context(nc.semaphore(name))

        banks = ctx.enter_context(nc.psum_tensor("banks", [P, 8, L], F32))
        ps_s, ps_v, ps_f, ps_b = banks[:, 0:2], banks[:, 2:4], banks[:, 4:7], banks[:, 7]
        ps_up = banks[:, 0:4].rearrange("p (d half) n -> p d (half n)", d=2)

        const = sb("const", [P, CONST_N])
        routed = sb("routed", [P, 2, NT + 1], I32)
        tile_expert = sb("tile_expert", [P, NT + 1], I32)
        rows_in = sb("rows_in", [P, 2, 1], I32)
        rows_out = sb("rows_out", [P, 2, 1], I32)
        logits = sb("logits", [P, TT, NE])
        half_power = sb("half_power", [P, T])
        ln_eps, rms_eps = sb("ln_eps", [P, T]), sb("rms_eps", [P, T])
        sq = sb("sq", [P, PAIRS, L], F32R)
        sk = sb("sk", [P, 2, L], F32R)

        WEX = C * 2 * HID + HID // P * D
        arena = sb("arena", [P, ARENA])
        used = [0]

        def take(*shape):
            n = int(np.prod(shape))
            at = used[0]
            used[0] += n
            v = arena[:, at:at + n]
            if len(shape) == 2:
                return v.rearrange("p (a b) -> p a b", a=shape[0])
            if len(shape) == 3:
                return v.rearrange("p (a b c) -> p a b c", a=shape[0], b=shape[1])
            if len(shape) == 4:
                return v.rearrange("p (a b c d) -> p a b c d", a=shape[0], b=shape[1], c=shape[2])
            return v

        kT = take(C, B * S)
        kbd = take(C, PAIRS, S)
        v_all = take(B, D)
        vbd = take(PAIRS, 2 * E)
        x_in = take(T, D)
        xn = take(T, D)
        xnT = take(C, L)
        cqT = take(C, L)
        coT = cqT
        cs_at = used[0]
        cs = take(2, H * S)
        squares = arena[:, cs_at:cs_at + T * HS * E].rearrange("p (t n) -> p t n", t=T)
        cpT = take(PAIRS, P)
        rope_a = take(T, HS * E)
        rope_b = take(T, HS * E)
        stack_at = used[0]
        stack = take(2, T, PAIRS + 2, 4 * E)
        EARLY = used[0] // WEX
        par = take(PAR_N)
        wgt = take(C, WGT_N)
        x1 = take(2, T, D)
        y = take(2, T, D)
        qkv = take(T, QKV)
        pt_at = used[0]
        pt = take(4, 5 * L)
        v_pad = take(T, KV, 3 * E)
        aoT = take(C, L)
        gate = take(C, L)
        h2 = take(T, D)
        residual = take(T, D)
        h2T = gate
        stats = take(3, T, 6)
        mv = take(3, T, 2)
        tiny = take(12, T)
        cmax = take(2, H)
        qk_ms = take(HS * T)
        qk_rs = take(HS * T)
        qk_t = take(HS * T)
        crec = take(C, P)
        rec = take(L)
        assert used[0] <= ARENA, used[0]
        ctxw = arena[:, pt_at:pt_at + C * CTX_N].rearrange("p (c n) -> p c n", c=C)
        delta_r = arena[0:3, stack_at:stack_at + B * S]
        delta_s = arena[0:3, stack_at + B * S:stack_at + 2 * B * S]
        delta_parts = arena[0:3, stack_at + 2 * B * S:stack_at + 4 * B * S].bitcast(BF16).rearrange("p (k n) -> p k n", k=4)
        delta3 = sb("delta3", [3, B * S], BF16)
        ones3 = sb("ones3", [3, P], BF16)

        carrier = sb("carrier", [1, 2])

        def carry(eng):
            if eng is nc.gpsimd:
                nc.gpsimd.tensor_tensor(carrier[:, 1:2], half_power[0:1, 0:1], half_power[0:1, 0:1], ALU.mult)
            else:
                nc.vector.memset(carrier[:, 0:1], 0.0)

        def cst(name, rows=P):
            a, n = CONST[name]
            return const[0:rows, a:a + n]

        def prm(name, rows=P):
            a, n = PAR[name]
            return par[0:rows, a:a + n]

        def w(name):
            a, n = WGT[name]
            return wgt[:, :, a:a + n]

        def cx(name):
            a, n = CTX[name]
            return ctxw[:, :, a:a + n]

        ident = cst("ident")
        wg = prm("Wg")
        rows_dram = nc.dram_tensor("rows_scratch", (N, 2 * D), F32, kind="Internal").ap()

        SETUP_WEIGHTS = 15
        SETUP_DVE = SETUP_WEIGHTS + C + B
        f_pe, f_act = Steps(sem("front_pe"), FRONT_PE), Steps(sem("front_act"), FRONT_ACT)
        h_pe, h_act = Steps(sem("head_pe"), HEAD_PE), Steps(sem("head_act"), HEAD_ACT)
        h_dve, h_pool = Steps(sem("head_dve"), HEAD_DVE), Steps(sem("head_pool"), HEAD_POOL)
        f_dve, f_pool = Steps(sem("front_dve"), FRONT_DVE), Steps(sem("front_pool"), FRONT_POOL)
        a_pe, a_act = Steps(sem("scores_pe"), UNITS), Steps(sem("probs_act"), UNITS)
        a_pool, v_pe = Steps(sem("masked_pool"), MASKS), Steps(sem("attended_pe"), ATTENDED)
        v_dve, n_dve = Steps(sem("values_dve"), ["v"]), Steps(sem("attention_dve"), ["rec0", "n0", "rec1", "n1"])
        b_pe, b_act = Steps(sem("back_pe"), BACK_PE), Steps(sem("back_act"), BACK_ACT)
        b_dve, b_pool = Steps(sem("back_dve"), BACK_DVE), Steps(sem("back_pool"), BACK_POOL)
        x_loaded = sem("x_loaded")
        rows_stored = sem("rows_stored")
        const_loaded, weights_loaded, context_loaded = sem("const_loaded"), sem("weights_loaded"), sem("context_loaded")
        su_pe, su_dve, su_pool = sem("setup_pe"), sem("setup_dve"), sem("setup_pool")

        front_reader = {}
        for n in BANKED:
            if n in HEAD_PE:
                front_reader[n] = (h_act, n) if n in HEAD_ACT else (h_dve, n)
            elif n in FRONT_ACT:
                front_reader[n] = (f_act, n)
            elif n[:2] == "cs":
                front_reader[n] = (f_dve, "csub" + n[2:])
            elif n[:2] == "wo":
                front_reader[n] = (f_dve, "x1_" + n[2:])
            else:
                front_reader[n] = (f_dve, n)
        back_reader = {"z0": (b_act, "gate0"), "z1": (b_act, "gate1"),
                       "wo0": (b_dve, "in0"), "wo1": (b_dve, "in1"), "hT0": (b_act, "hT0"), "hT1": (b_act, "hT1"),
                       "lg": (b_dve, "lg")}

        UNIT_PARTS = [
            [(0, 0, 0, L)], [(1, 0, 0, L)],
            [(0, 1, 0, 3 * P), (0, 3, 3 * P, P)], [(1, 1, 0, 3 * P), (1, 3, 3 * P, P)],
            [(0, 2, 0, 2 * P)], [(1, 2, 0, 2 * P)],
        ]
        UNIT_AT = [0, L, 2 * L, 3 * L, 4 * L, 4 * L + 2 * P, 5 * L]

        def probs(s, x, kb):
            for u, parts in enumerate(UNIT_PARTS):
                for head, k, col, width in parts:
                    if (head, k) == (x, kb):
                        a = UNIT_AT[u] + col
                        return pt[:, s % 4, a:a + width]

        at = [0]

        def take2(*shape):
            n = int(np.prod(shape))
            v = arena[:, at[0]:at[0] + n]
            at[0] += n
            if len(shape) == 2:
                return v.rearrange("p (a b) -> p a b", a=shape[0])
            if len(shape) == 3:
                return v.rearrange("p (a b c) -> p a b c", a=shape[0], b=shape[1])
            return v

        wex = take2(NE, WEX)
        b1 = take2(NE, 2 * HID)
        b2 = take2(NE, D)
        hot_at = at[0]
        res = take2(4, D)
        got = take2(2, 2 * D)
        gT = take2(2, C, P)
        ub = take2(2, 2 * HID)
        sg = take2(2, HID)
        actT = take2(2, HID)
        yo = take2(2, D)
        small = [take2(TT, NE) for _ in range(9)]
        rsmall = take2(12, TT + NE)
        assert at[0] <= ARENA, at[0]
        at[0] = hot_at
        half_width = lambda n: arena[:, at[0]:at[0] + n // 2].bitcast(BF16)
        row_hot = half_width(TT * P).rearrange("p (t n) -> p t n", t=TT)
        at[0] += TT * P // 2
        tile_hot = half_width(3 * TT * (NT + 1)).rearrange("p (t a j) -> p t a j", t=TT, a=3)
        HOT_CHUNK = 8

        w_ready = [sem(f"expert{e}_loaded") for e in range(NE)]
        r_pe, r_dve = sem("routing_pe"), sem("routing_dve")
        g_pe, u_pe, t_pe, y_pe = (Steps(sem(name), ["done"]) for name in ("rows_T_pe", "up_pe", "hidden_T_pe", "down_pe"))
        g_act, sig_act, t_act = (Steps(sem(name), ["done"]) for name in ("rows_T_act", "sigmoid_act", "hidden_T_act"))
        ub_dve, hid_dve = (Steps(sem(name), ["done"]) for name in ("up_bias_dve", "hidden_dve"))
        yb_dve, out_dve = (Steps(sem(name), ["done"]) for name in ("down_bias_dve", "output_dve"))
        in_pool, out_pool = (Steps(sem(name), ["done"]) for name in ("rows_in_pool", "rows_out_pool"))
        rows_got = [sem(f"rows_got{d}") for d in range(2)]
        res_act = Steps(sem("residual_act"), ["done"])
        out_stored = [sem(f"out_stored{d}") for d in range(2)]

        def expert_weights(sp, e):
            sp.dma_start(wex[:, e, 0:C * 2 * HID].rearrange("p (c n) -> p c n", c=C),
                         ins["W1"][e].rearrange("(c p) n -> p c n", p=P)).then_inc(w_ready[e], 16)
            sp.dma_start(wex[:, e, C * 2 * HID:WEX].rearrange("p (c n) -> p c n", c=HID // P),
                         ins["W2"][e].rearrange("(c p) n -> p c n", p=P)).then_inc(w_ready[e], 16)

        def early_loads(sp):
            for steps in (f_pe, f_act, f_dve, f_pool, h_pe, h_act, h_dve, h_pool):
                sp.wait_ge(steps.sem, B * steps.n)
            for e in range(EARLY):
                expert_weights(sp, e)

        def moe_loads(sp):
            sp.wait_ge(b_dve.sem, B * b_dve.n)
            sp.wait_ge(rows_stored, 32 * B)
            for e in range(NE):
                if e >= EARLY:
                    expert_weights(sp, e)
                sp.dma_start(b1[:, e, :], ins["b1"][e:e + 1, :].to_broadcast([P, 2 * HID])).then_inc(w_ready[e], 16)
                sp.dma_start(b2[:, e, :], ins["b2"][e:e + 1, :].to_broadcast([P, D])).then_inc(w_ready[e], 16)

        def pe_routing(pe):
            pe.wait_ge(r_dve, R_HOT)
            hot = small[2].rearrange("p t e -> p (t e)")
            nc.tensor.matmul(ps_f[:, 0, 0:TT * NE], cst("before"), hot, start=True, stop=True)
            nc.tensor.matmul(ps_f[:, 1, 0:TT * NE], cst("ones"), hot, start=True, stop=True).then_inc(r_pe, 1)
            for t in range(TT):
                pe.wait_ge(r_dve, R_TILE_HOT + t // HOT_CHUNK + 1)
                last = nc.tensor.matmul(ps_v[:, 0, 0:3 * (NT + 1)], row_hot[:, t, :], tile_hot[:, t, :, :].rearrange("p a j -> p (a j)"),
                                        start=(t == 0), stop=(t == TT - 1))
            last.then_inc(r_pe, 1)

        R_HOT, R_TILE_HOT = 5, 29
        R_DONE = R_TILE_HOT + TT // HOT_CHUNK + 7

        def dve_routing(dve):
            count = [0]

            def done(inst):
                count[0] += 1
                inst.then_inc(r_dve, 1)
                dve.wait_ge(r_dve, count[0])

            def over_e(v):
                return v.unsqueeze(2).to_broadcast([P, TT, NE])

            v = nc.vector
            tt = v.tensor_tensor
            dve.wait_ge(b_dve.sem, b_dve.value(B - 1, "lg"))
            dve.wait_ge(rows_stored, 32 * B)
            mx, rank = rsmall[:, 0, 0:TT], cst("rank")
            eq, score, hot = small[0], small[1], small[2]
            done(v.tensor_reduce(mx, logits[:], X, ALU.max))
            done(tt(eq, logits[:], over_e(mx), ALU.is_ge))
            done(tt(score, eq, rank.unsqueeze(1).to_broadcast([P, TT, NE]), ALU.mult))
            done(v.tensor_reduce(mx, score, X, ALU.max))
            done(tt(hot, score, over_e(mx), ALU.is_equal))
            assert count[0] == R_HOT
            dve.wait_ge(r_pe, 1)
            et = [small[i].rearrange("p t e -> p (t e)").rearrange("p (e t) -> p e t", e=NE) for i in (3, 4, 5, 6)]
            tot, run = et[0], et[1]
            done(v.tensor_copy(tot, ps_f[:, 1, 0:TT * NE].rearrange("p (t e) -> p e t", e=NE)))
            cur, k = tot, 1
            for nxt in (et[1], et[2], et[1], et[2], et[1]):
                v.tensor_copy(nxt[:, :, 0:k], cur[:, :, 0:k])
                done(tt(nxt[:, :, k:], cur[:, :, k:], cur[:, :, 0:TT - k], ALU.add))
                cur, k = nxt, 2 * k
            run = cur
            before = et[2]
            done(tt(before, run, tot, ALU.subtract))
            done(tt(et[3], run[:, :, TT - 1:TT].to_broadcast([P, NE, TT]), cst("tile_limit").unsqueeze(1).to_broadcast([P, NE, TT]), ALU.is_gt))
            tiles, first, first_row = rsmall[:, 1, 0:NE], rsmall[:, 2, 0:NE], rsmall[:, 3, 0:NE]
            done(v.tensor_reduce(tiles, et[3], X, ALU.add))
            square = small[7].rearrange("p t e -> p (t e)")[:, 0:NE * NE].rearrange("p (a b) -> p a b", a=NE)
            done(tt(square, tiles.unsqueeze(1).to_broadcast([P, NE, NE]), cst("earlier").rearrange("p (a b) -> p a b", a=NE), ALU.mult))
            done(v.tensor_reduce(first, square, X, ALU.add))
            done(v.tensor_scalar(first_row, first, float(P), None, ALU.mult))
            base = et[3]
            done(tt(base, before, first_row.unsqueeze(2).to_broadcast([P, NE, TT]), ALU.add))
            row_te = small[8]
            done(tt(row_te, ps_f[:, 0, 0:TT * NE].rearrange("p (t e) -> p t e", e=NE), base.rearrange("p e t -> p t e"), ALU.add))
            done(tt(row_te, row_te, hot, ALU.mult))
            row = rsmall[:, 4, 0:TT]
            done(v.tensor_reduce(row, row_te, X, ALU.add))
            row_i, tile_i, in_tile_i = (rsmall[:, k, 0:TT].bitcast(I32) for k in (5, 6, 7))
            tile_f, in_tile_f = rsmall[:, 8, 0:TT], rsmall[:, 9, 0:TT]
            done(v.tensor_copy(row_i, row))
            done(v.tensor_scalar(tile_i, row_i, 7, None, ALU.logical_shift_right))
            done(v.tensor_scalar(in_tile_i, row_i, P - 1, None, ALU.bitwise_and))
            done(v.tensor_copy(tile_f, tile_i))
            done(v.tensor_copy(in_tile_f, in_tile_i))
            done(tt(tile_hot[:, :, 0, :], cst("tile_no").unsqueeze(1).to_broadcast([P, TT, NT + 1]),
                    tile_f.unsqueeze(2).to_broadcast([P, TT, NT + 1]), ALU.is_equal))
            done(v.tensor_scalar(tile_hot[:, :, 1, :], tile_hot[:, :, 0, :], cst("token")[:, 0:1], None, ALU.mult))
            done(tt(tile_hot[:, :, 2, :], tile_hot[:, :, 0, :], cst("tile_no")[:, 0:TT].unsqueeze(2).to_broadcast([P, TT, NT + 1]), ALU.mult))
            assert count[0] == R_TILE_HOT, count[0]
            for t in range(0, TT, HOT_CHUNK):
                done(tt(row_hot[:, t:t + HOT_CHUNK, :], cst("row").unsqueeze(1).to_broadcast([P, HOT_CHUNK, P]),
                        in_tile_f[:, t:t + HOT_CHUNK].unsqueeze(2).to_broadcast([P, HOT_CHUNK, P]), ALU.is_equal))
            nt1 = NT + 1
            cmp = arena[:, hot_at + 6656:hot_at + 6656 + nt1 * NE].rearrange("p (j e) -> p j e", e=NE)
            te = rsmall[:, 10, 0:nt1]
            done(tt(cmp, cst("tile_no").unsqueeze(2).to_broadcast([P, nt1, NE]), first.unsqueeze(1).to_broadcast([P, nt1, NE]), ALU.is_ge))
            done(v.tensor_reduce(te, cmp, X, ALU.add))
            done(v.tensor_scalar(tile_expert[:], te, -1.0, None, ALU.add))
            dve.wait_ge(r_pe, 2)
            pad = rsmall[:, 11, 0:nt1]
            done(v.tensor_scalar(pad, ps_v[:, 0, 0:nt1], -float(OUT_OF_RANGE), float(OUT_OF_RANGE), ALU.mult, ALU.add))
            token = rsmall[:, 10, 0:nt1]
            done(v.tensor_scalar(token, ps_v[:, 0, 2 * nt1:3 * nt1], float(P), None, ALU.mult))
            done(tt(routed[:, 0, :], token, ps_v[:, 0, nt1:2 * nt1], ALU.add))
            done(tt(routed[:, 1, :], routed[:, 0, :], pad, ALU.add))
            assert count[0] == R_DONE, count[0]

        def tiles(eng, first, step, last):
            first()
            for j in range(8):
                step(j, j // 4, j % 4)
            loops = (NT - 3) // 4
            with eng.Fori(2, loops) as k:
                for d in range(4):
                    step(4 * k + d, k, d)
            for j in range(4 * loops, NT):
                step(j, j // 4, j % 4)
            last()

        def no_tile(j):
            return isinstance(j, int) and not 0 <= j < NT

        def expert(eng, j):
            return eng.value_load(tile_expert[0:1, bass.ds(j, 1)], min_val=0, max_val=NE - 1)

        def dma_done(eng, sems, k, d):
            n = 2 * k + d // 2 + 1
            if not (isinstance(n, int) and n <= 0):
                eng.wait_ge(sems[d % 2], n * 16)

        def rows_there(eng, k, d):
            dma_done(eng, rows_got, k, d)

        def stored(eng, k, d):
            dma_done(eng, out_stored, k, d)

        def y_bank(d):
            return ps_f[:, 2, 0:D] if d % 2 else ps_b[:, 0:D]

        def pe_moe(pe):
            pe.wait_ge(r_dve, R_DONE)

            def rows_T(j, k, d):
                if no_tile(j):
                    return
                rows_there(pe, k, d)
                if begun(j - 1):
                    pe.wait_ge(g_act.sem, g_act.value(j - 1))
                for c in range(C):
                    last = nc.tensor.transpose(ps_f[:, 0, c * P:(c + 1) * P], got[:, d % 2, c * P:(c + 1) * P], ident)
                last.then_inc(g_pe.sem, 1)

            def up(j, d):
                if no_tile(j):
                    return
                e = expert(pe, j)
                if isinstance(j, int) and j < NE:
                    pe.wait_ge(w_ready[j], 64)
                pe.wait_ge(g_act.sem, g_act.value(j))
                if begun(j - 2):
                    pe.wait_ge(ub_dve.sem, ub_dve.value(j - 2))
                for half in range(2):
                    for c in range(C):
                        a = c * 2 * HID + half * HID
                        last = nc.tensor.matmul(ps_up[:, d % 2, half * HID:(half + 1) * HID], gT[:, d % 2, c, :],
                                                wex[:, bass.ds(e, 1), a:a + HID].rearrange("p x n -> p (x n)"),
                                                start=(c == 0), stop=(c == C - 1))
                last.then_inc(u_pe.sem, 1)

            def hidden_T(j, d):
                pe.wait_ge(hid_dve.sem, hid_dve.value(j))
                if begun(j - 1):
                    pe.wait_ge(t_act.sem, t_act.value(j - 1))
                for c in range(HID // P):
                    last = nc.tensor.transpose(ps_f[:, 1, c * P:(c + 1) * P], sg[:, d % 2, c * P:(c + 1) * P], ident)
                last.then_inc(t_pe.sem, 1)

            def down(j, d):
                if no_tile(j):
                    return
                e = expert(pe, j)
                pe.wait_ge(t_act.sem, t_act.value(j))
                if begun(j - 2):
                    pe.wait_ge(yb_dve.sem, yb_dve.value(j - 2))
                for c in range(HID // P):
                    a = C * 2 * HID + c * D
                    last = nc.tensor.matmul(y_bank(d), actT[:, d % 2, c * P:(c + 1) * P],
                                            wex[:, bass.ds(e, 1), a:a + D].rearrange("p x n -> p (x n)"),
                                            start=(c == 0), stop=(c == HID // P - 1))
                last.then_inc(y_pe.sem, 1)

            def first():
                rows_T(0, 0, 0)
                rows_T(1, 0, 1)
                up(0, 0)

            def step(j, k, d):
                up(j + 1, d + 1)
                rows_T(j + 2, k, d + 2)
                hidden_T(j, d)
                down(j - 1, d - 1)

            tiles(pe, first, step, lambda: down(NT - 1, (NT - 1) % 4))

        def act_moe(act):
            act.wait_ge(r_dve, R_DONE)

            def rows_T(j, d):
                if no_tile(j):
                    return
                act.wait_ge(g_pe.sem, g_pe.value(j))
                if begun(j - 2):
                    act.wait_ge(u_pe.sem, u_pe.value(j - 2))
                nc.scalar.activation(gT[:, d % 2, :, :].rearrange("p c n -> p (c n)"), ps_f[:, 0, 0:C * P], ACT.Copy).then_inc(g_act.sem, 1)

            def residual(j, k, d):
                if no_tile(j):
                    return
                rows_there(act, k, d)
                if begun(j - 4):
                    act.wait_ge(out_dve.sem, out_dve.value(j - 4))
                nc.scalar.activation(res[:, d % 4, :], got[:, d % 2, D:2 * D], ACT.Copy).then_inc(res_act.sem, 1)

            def hidden_T(j, d):
                act.wait_ge(t_pe.sem, t_pe.value(j))
                if begun(j - 2):
                    act.wait_ge(y_pe.sem, y_pe.value(j - 2))
                nc.scalar.activation(actT[:, d % 2, :], ps_f[:, 1, :], ACT.Copy).then_inc(t_act.sem, 1)

            def sigmoid(j, d):
                if no_tile(j):
                    return
                act.wait_ge(ub_dve.sem, ub_dve.value(j))
                if begun(j - 2):
                    act.wait_ge(t_pe.sem, t_pe.value(j - 2))
                nc.scalar.activation(sg[:, d % 2, :], ub[:, d % 2, HID:2 * HID], ACT.Sigmoid).then_inc(sig_act.sem, 1)

            def first():
                rows_T(0, 0)
                rows_T(1, 1)
                residual(0, 0, 0)
                residual(1, 0, 1)
                sigmoid(0, 0)

            def step(j, k, d):
                rows_T(j + 2, d)
                hidden_T(j, d)
                sigmoid(j + 1, d + 1)
                residual(j + 2, k, d + 2)

            tiles(act, first, step, lambda: None)

        def dve_moe(dve):
            def hidden(j, d):
                if no_tile(j):
                    return
                if isinstance(j, int) and j < NE:
                    dve.wait_ge(w_ready[j], 64)
                e = expert(dve, j)
                dve.wait_ge(u_pe.sem, u_pe.value(j))
                nc.vector.tensor_tensor(ub[:, d % 2, :], ps_up[:, d % 2, :], b1[:, bass.ds(e, 1), :].rearrange("p x n -> p (x n)"), ALU.add).then_inc(ub_dve.sem, 1)
                dve.wait_ge(sig_act.sem, sig_act.value(j))
                nc.vector.tensor_tensor(sg[:, d % 2, :], ub[:, d % 2, 0:HID], sg[:, d % 2, :], ALU.mult).then_inc(hid_dve.sem, 1)

            def output(j, k, d):
                if no_tile(j):
                    return
                e = expert(dve, j)
                dve.wait_ge(y_pe.sem, y_pe.value(j))
                stored(dve, k, d - 2)
                nc.vector.tensor_tensor(yo[:, d % 2, :], y_bank(d), b2[:, bass.ds(e, 1), :].rearrange("p x n -> p (x n)"), ALU.add).then_inc(yb_dve.sem, 1)
                dve.wait_ge(res_act.sem, res_act.value(j))
                dve.wait_ge(yb_dve.sem, yb_dve.value(j))
                nc.vector.tensor_tensor(yo[:, d % 2, :], yo[:, d % 2, :], res[:, d % 4, :], ALU.add).then_inc(out_dve.sem, 1)

            def step(j, k, d):
                hidden(j + 1, d + 1)
                output(j - 1, k, d - 1)

            tiles(dve, lambda: hidden(0, 0), step, lambda: output(NT - 1, (NT - 1) // 4, (NT - 1) % 4))

        def pool_moe(pool):
            pool.wait_ge(r_dve, R_DONE)

            def gather(j, k, d):
                if no_tile(j):
                    return
                q = d % 2
                rows_there(pool, k, d - 2)
                if begun(j - 2):
                    pool.wait_ge(g_pe.sem, g_pe.value(j - 2))
                if begun(j - 2):
                    pool.wait_ge(res_act.sem, res_act.value(j - 2))
                nc.gpsimd.tensor_copy(rows_in[:, q, :], routed[:, 0, bass.ds(j, 1)]).then_inc(in_pool.sem, 1)
                pool.wait_ge(in_pool.sem, in_pool.value(j))
                carry(pool)
                nc.gpsimd.indirect_dma_start(out=got[:, q, :], out_offset=None, in_=rows_dram,
                                             in_offset=bass.IndirectOffsetOnAxis(ap=rows_in[:, q, :].bitcast(U32), axis=0)).then_inc(rows_got[q], 16)

            def scatter(j, k, d):
                if no_tile(j):
                    return
                q = d % 2
                stored(pool, k, d - 2)
                nc.gpsimd.tensor_copy(rows_out[:, q, :], routed[:, 1, bass.ds(j, 1)]).then_inc(out_pool.sem, 1)
                pool.wait_ge(out_pool.sem, out_pool.value(j))
                pool.wait_ge(out_dve.sem, out_dve.value(j))
                carry(pool)
                nc.gpsimd.indirect_dma_start(out=out, out_offset=bass.IndirectOffsetOnAxis(ap=rows_out[:, q, :].bitcast(U32), axis=0),
                                             in_=yo[:, q, :], in_offset=None, bounds_check=N - 1, oob_is_err=False).then_inc(out_stored[q], 16)

            def first():
                for j in range(3):
                    gather(j, 0, j)

            def step(j, k, d):
                gather(j + 3, k, d + 3)
                scatter(j - 1, k, d - 1)

            def last():
                scatter(NT - 1, (NT - 1) // 4, (NT - 1) % 4)
                for j in (NT - 2, NT - 1):
                    stored(pool, j // 4, j % 4)

            tiles(pool, first, step, last)

        def bank_free(eng, unit, b, head=True):
            prev, ago = before_in_bank(unit, head)
            st, name = front_reader[prev]
            if begun(b - ago):
                eng.wait_ge(st.sem, st.value(b - ago, name))

        def fb(unit):
            return ps_f[:, FRONT_BANK[unit], :]

        def pe_transposes(unit, b, blocks, steps):
            for i, blk in enumerate(blocks):
                last = nc.tensor.transpose(fb(unit)[:, i * P:(i + 1) * P], blk, ident)
            last.then_inc(steps.sem, 1)

        def pe_setup(pe):
            pe.wait_ge(context_loaded, 16)
            pe.wait_ge(h_dve.sem, h_dve.value(0, "cq1"))
            for g in range(C):
                for c in range(C):
                    last = nc.tensor.matmul(ps_f[:, g, :], cx("c_k")[:, c, g * P:(g + 1) * P], cx("ctx")[:, c, :],
                                            start=(c == 0), stop=(c == C - 1))
            last.then_inc(su_pe, 1)
            for b in range(B):
                bank = ps_s[:, b % SCORE_BANKS, 0:D]
                if b >= SCORE_BANKS:
                    pe.wait_ge(su_dve, SETUP_WEIGHTS + C + b - SCORE_BANKS + 1)
                for x in range(2):
                    for c in range(C):
                        last = nc.tensor.matmul(bank[x * S:(x + 1) * S, :], cx("ctx")[:, c, b * S:(b + 1) * S], cx("c_v")[:, c, :],
                                                start=(c == 0), stop=(c == C - 1))
                last.then_inc(su_pe, 1)

        def pe_head(pe, p, b):
            if p == HEAD_AT["xT"]:
                pe.wait_ge(h_dve.sem, h_dve.value(b, "xn"))
                for c in range(C):
                    bank_free(pe, f"xT{c}", b)
                    pe_transposes(f"xT{c}", b, [xn[:, t, c * P:(c + 1) * P] for t in range(T)], h_pe)
            if p == HEAD_AT["cq"]:
                pe.wait_ge(h_act.sem, h_act.value(b, "xT1"))
                for g in range(C):
                    bank_free(pe, f"cq{g}", b)
                    for c in range(C):
                        last = nc.tensor.matmul(fb(f"cq{g}"), w("c_q")[:, c, g * P:(g + 1) * P], xnT[:, c, :],
                                                start=(c == 0), stop=(c == C - 1))
                    last.then_inc(h_pe.sem, 1)

        def pe_front(pe, p, b, head):
            def at(stage):
                return p == AT[stage]

            def scores(t):
                if t == 0:
                    pe.wait_ge(h_dve.sem, h_dve.value(b, "cq1"))
                    pe.wait_ge(h_pool.sem, h_pool.value(b, "kbd"))
                for g in range(C):
                    bank_free(pe, f"cs{t}{g}", b)
                    nc.tensor.matmul(fb(f"cs{t}{g}"), cqT[:, g, t * P:(t + 1) * P], kbd[:, g, :, :].rearrange("p h s -> p (h s)"),
                                     start=True, stop=False)
                    nc.tensor.matmul(fb(f"cs{t}{g}").rearrange("p (h s) -> p h s", h=PAIRS), ones3[:],
                                     delta3[:, bass.ds(b * S, S)].unsqueeze(1).to_broadcast([3, PAIRS, S]),
                                     start=False, stop=True).then_inc(f_pe.sem, 1)

            def probs_T(t):
                pe.wait_ge(f_act.sem, f_act.value(b, f"cexp{t}"))
                for g in range(2):
                    bank_free(pe, f"cT{t}{g}", b)
                    pe_transposes(f"cT{t}{g}", b, [cs[:, t % 2, (4 * g + i) * P:(4 * g + i + 1) * P] for i in range(4)], f_pe)

            def attended(t):
                pe.wait_ge(f_act.sem, f_act.value(b, f"cT{t}1"))
                pe.wait_ge(h_pool.sem, h_pool.value(b, "vbd"))
                bank_free(pe, f"co{t}", b)
                for kind in range(2):
                    for j in range(PAIRS):
                        stationary = cst("pair_ones") if kind else vbd[:, j, :]
                        rows, a = 2 * E * (j % 4), (2 * kind + j // 4) * P
                        last = nc.tensor.matmul(fb(f"co{t}")[rows:rows + 2 * E, a:a + P], stationary, cpT[:, j, :],
                                                start=True, stop=True, tile_position=(0, rows))
                last.then_inc(f_pe.sem, 1)

            for t in range(T):
                if at(f"co{t}"):
                    attended(t)
            for t in range(T):
                if at(f"cT{t}"):
                    probs_T(t)
            for t in range(T):
                if at(f"cs{t}"):
                    scores(t)
            if at("wo"):
                pe.wait_ge(f_dve.sem, f_dve.value(b, "co3"))
                for k in range(2):
                    bank_free(pe, f"wo{k}", b)
                    for i in range(2):
                        t = 2 * k + i
                        for c in range(C):
                            last = nc.tensor.matmul(fb(f"wo{k}")[:, i * D:(i + 1) * D], coT[:, c, t * P:(t + 1) * P], w("c_o")[:, c, :],
                                                    start=(c == 0), stop=(c == C - 1))
                    last.then_inc(f_pe.sem, 1)
            if at("hT"):
                pe.wait_ge(f_act.sem, f_act.value(b, "h"))
                for c in range(C):
                    bank_free(pe, f"hT{c}", b)
                    pe_transposes(f"hT{c}", b, [xn[:, t, c * P:(c + 1) * P] for t in range(T)], f_pe)
            for k in range(2):
                if at(f"qkv{k}"):
                    pe.wait_ge(f_act.sem, f_act.value(b, "hT1"))
                    for t in (2 * k, 2 * k + 1):
                        bank_free(pe, f"qkv{t}", b)
                        for c in range(C):
                            last = nc.tensor.matmul(fb(f"qkv{t}")[:, 0:QKV], xnT[:, c, t * P:(t + 1) * P], w("qkv")[:, c, :],
                                                    start=(c == 0), stop=(c == C - 1))
                        last.then_inc(f_pe.sem, 1)
            for m, units in enumerate((ST0, ST1)):
                if at(f"st{m}"):
                    pe.wait_ge(f_act.sem, f_act.value(b, f"twice{m}"))
                    for n in units:
                        bank_free(pe, n, b, head)
                        h = 8 if n[2] == "k" else 2 * (int(n[3]) % 4)
                        pe_transposes(n, b, [stack[:, m, t, h:h + 2, :].rearrange("p x n -> p (x n)") for t in range(T)], f_pe)

        def pe_scores(pe, b, s, u):
            if u == 0:
                for unit in [f"stq{s}"] + ([f"stk{s // 4}"] if s % 4 == 0 else []):
                    if unit in ST_ACT:
                        pe.wait_ge(f_act.sem, f_act.value(b, unit))
                    else:
                        pe.wait_ge(f_dve.sem, f_dve.value(b, unit))
            prev, ago = before_in_ring(UNITS, SCORE_BANK, f"s{s}{u}")
            if begun(b - ago):
                pe.wait_ge(a_act.sem, a_act.value(b - ago, prev))
            m, bank = s // 4, SCORE_BANK[f"s{s}{u}"]
            for x, kb, a, width in UNIT_PARTS[u]:
                last = nc.tensor.matmul(ps_s[:, bank, a:a + width], sk[x * 64:(x + 1) * 64, m, kb * P:(kb + 1) * P],
                                        sq[x * 64:(x + 1) * 64, s, kb * P:kb * P + width], start=True, stop=True)
            last.then_inc(a_pe.sem, 1)

        def pe_attended(pe, b, q, kb):
            if kb == 0:
                pe.wait_ge(a_pool.sem, a_pool.value(b, f"m{2 * q + 1}2"))
                if q == 0:
                    pe.wait_ge(v_dve.sem, v_dve.value(b, "v"))
                if q == 2:
                    pe.wait_ge(n_dve.sem, n_dve.value(b, "n0"))
                if q == 0 and begun(b - 1):
                    pe.wait_ge(n_dve.sem, n_dve.value(b - 1, "n1"))
            slot, ones = q % 2, cst("slot_ones")
            for kind in range(2):
                for i in range(2):
                    for x in range(2):
                        rows, a = 2 * E * (2 * i + x), E * (1 - slot)
                        stationary = ones[:, a:a + 2 * E] if kind else v_pad[:, kb, 2 * (q // 2) + x, a:a + 2 * E]
                        last = nc.tensor.matmul(ps_v[rows:rows + 2 * E, kind, kb * P:L], stationary, probs(2 * q + i, x, kb),
                                                start=(slot == 0 and kb == 0), stop=(slot == 1 and kb == T - 1), tile_position=(0, rows))
            last.then_inc(v_pe.sem, 1)

        def back_free(eng, unit, b):
            i = BACK_PE.index(unit)
            st, name = back_reader[BACK_PE[i - 1]]
            if i or begun(b - 1):
                eng.wait_ge(st.sem, st.value(b if i else b - 1, name))

        def pe_back(pe, p, b):
            for c in range(C):
                if p == BACK_AT[f"z{c}"]:
                    back_free(pe, f"z{c}", b)
                    pe.wait_ge(n_dve.sem, n_dve.value(b, f"n{c}"))
                    nc.tensor.matmul(ps_b, wg, aoT[:, c, :], start=True, stop=True).then_inc(b_pe.sem, 1)
            for k in range(2):
                if p == BACK_AT[f"wo{k}"]:
                    pe.wait_ge(b_dve.sem, b_dve.value(b, "gated"))
                    back_free(pe, f"wo{k}", b)
                    for i in range(2):
                        t = 2 * k + i
                        for c in range(C):
                            last = nc.tensor.matmul(ps_b[:, i * D:(i + 1) * D], aoT[:, c, t * P:(t + 1) * P], w("f_o")[:, c, :],
                                                    start=(c == 0), stop=(c == C - 1))
                    last.then_inc(b_pe.sem, 1)
            for c in range(C):
                if p == BACK_AT[f"hT{c}"]:
                    pe.wait_ge(b_dve.sem, b_dve.value(b, "h2"))
                    back_free(pe, f"hT{c}", b)
                    for t in range(T):
                        last = nc.tensor.transpose(ps_b[:, t * P:(t + 1) * P], h2[:, t, c * P:(c + 1) * P], ident)
                    last.then_inc(b_pe.sem, 1)
            if p == BACK_AT["lg"]:
                back_free(pe, "lg", b)
                for t in range(T):
                    for c in range(C):
                        last = nc.tensor.matmul(ps_b[:, t * NE:(t + 1) * NE], h2T[:, c, t * P:(t + 1) * P], w("r")[:, c, :],
                                                start=(c == 0), stop=(c == C - 1))
                last.then_inc(b_pe.sem, 1)

        def attend_at(p, i, attn, back):
            quad, kb = p // 6, p % 6 - 1
            if kb not in range(T):
                return None
            if quad:
                return (i, quad - 1, kb) if attn else None
            return (i - 1, QUADS - 1, kb) if back else None

        def pe_iteration(pe, i, head, front, attn, back):
            for p in range(POINTS):
                if attn:
                    for u in POINT_UNITS[p % 3]:
                        pe_scores(pe, i, p // 3, u)
                tile = attend_at(p, i, attn, back)
                if tile:
                    pe_attended(pe, *tile)
                if back:
                    pe_back(pe, p, i - 1)
                if front:
                    pe_front(pe, p, i + 1, head)
                if head:
                    pe_head(pe, p, i + 2)

        def pipeline(eng, iteration):
            iteration(eng, -1, True, True, False, False)
            iteration(eng, 0, True, True, True, False)
            iteration(eng, 1, True, True, True, True)
            with eng.Fori(2, B - 2) as i:
                iteration(eng, i, True, True, True, True)
            iteration(eng, B - 2, False, True, True, True)
            iteration(eng, B - 1, False, False, True, True)
            iteration(eng, B, False, False, False, True)

        def act_evacuate(dst, unit, b, first=None):
            nc.scalar.wait_ge(f_pe.sem, f_pe.value(b, unit))
            nc.scalar.activation(dst, fb(unit), ACT.Copy).then_inc(f_act.sem, 1)

        def act_head(act, p, b):
            if p == HEAD_AT["xT"]:
                if begun(b - 1):
                    act.wait_ge(f_pe.sem, f_pe.value(b - 1, "qkv3"))
                for c in range(C):
                    act.wait_ge(h_pe.sem, h_pe.value(b, f"xT{c}"))
                    nc.scalar.activation(xnT[:, c, :], fb(f"xT{c}"), ACT.Copy).then_inc(h_act.sem, 1)

        def act_front(act, p, b):
            def at(stage):
                return p == AT[stage]

            for t in range(T):
                if at(f"cT{t}"):
                    if t:
                        act.wait_ge(f_pe.sem, f_pe.value(b, f"co{t - 1}"))
                    else:
                        if begun(b - 1):
                            act.wait_ge(f_pe.sem, f_pe.value(b - 1, f"co{T - 1}"))
                    for g in range(2):
                        act_evacuate(cpT[:, 4 * g:4 * g + 4, :].rearrange("p j q -> p (j q)"), f"cT{t}{g}", b)
            for t in range(T):
                if at(f"exp{t}"):
                    act.wait_ge(f_dve.sem, f_dve.value(b, f"csub{t}1"))
                    nc.scalar.activation(cs[:, t % 2, :], cs[:, t % 2, :], ACT.Exp).then_inc(f_act.sem, 1)
            if at("h"):
                act.wait_ge(f_dve.sem, f_dve.value(b, "y"))
                act.wait_ge(f_pool.sem, f_pool.value(b, "rms"))
                for t in range(T):
                    last = nc.scalar.activation(xn[:, t, :], y[:, bass.ds(b % 2, 1), t, :].rearrange("p a d -> p (a d)"), ACT.Copy,
                                                scale=tiny[:, 5, t:t + 1])
                last.then_inc(f_act.sem, 1)
            if at("hT"):
                for c in range(C):
                    act_evacuate(xnT[:, c, :], f"hT{c}", b)
            if at("qkv1"):
                act.wait_ge(f_dve.sem, f_dve.value(b, "qkv3"))
                if begun(b - 1):
                    act.wait_ge(f_dve.sem, f_dve.value(b - 1, "meansq"))
                nc.scalar.activation(squares, qkv[:, :, 0:HS * E], ACT.Square).then_inc(f_act.sem, 1)
            if at("twice"):
                for m in range(2):
                    act.wait_ge(f_dve.sem, f_dve.value(b, f"lo{m}"))
                    queries = stack[:, m, :, 0:8, :].rearrange("p t h (k two e) -> p t (h k) two e", k=2, e=E)
                    nc.scalar.activation(queries[:, :, :, 1], queries[:, :, :, 0], ACT.Copy)
                    keys = stack[:, m, :, 8:10, :].rearrange("p t h (two n) -> p t h two n", two=2)
                    nc.scalar.activation(keys[:, :, :, 1], keys[:, :, :, 0], ACT.Copy).then_inc(f_act.sem, 1)
            for m, units in enumerate((ST0, ST1)):
                if at(f"st{m}"):
                    for n in units:
                        if n in ST_ACT:
                            st_evacuate(act, n, b)

        def st_evacuate(eng, n, b):
            eng.wait_ge(f_pe.sem, f_pe.value(b, n))
            if n[2] == "k":
                m = int(n[3])
                if begun(b - 1):
                    eng.wait_ge(a_pe.sem, a_pe.value(b - 1, f"s{4 * m + 3}{U - 1}"))
                dst = sk[:, m, :]
            else:
                s = int(n[3])
                if begun(b - 1):
                    eng.wait_ge(a_pe.sem, a_pe.value(b - 1, f"s{s}{U - 1}"))
                dst = sq[:, s, :]
            if n in ST_ACT:
                nc.scalar.activation(dst, fb(n), ACT.Copy).then_inc(f_act.sem, 1)
            else:
                nc.vector.tensor_copy(dst, fb(n)).then_inc(f_dve.sem, 1)

        def act_attn(act, b, s, u):
            act.wait_ge(a_pe.sem, a_pe.value(b, f"s{s}{u}"))
            if u == 0:
                q = s // 2 - 2
                if q >= 0:
                    act.wait_ge(v_pe.sem, v_pe.value(b, f"pv{q}{T - 1}"))
                elif begun(b - 1):
                    act.wait_ge(v_pe.sem, v_pe.value(b - 1, f"pv{q + QUADS}{T - 1}"))
            nc.scalar.activation(pt[:, s % 4, UNIT_AT[u]:UNIT_AT[u + 1]], ps_s[:, SCORE_BANK[f"s{s}{u}"], 0:UNIT_AT[u + 1] - UNIT_AT[u]], ACT.Exp, scale=SCALE).then_inc(a_act.sem, 1)

        def act_back(act, p, b):
            for c in range(C):
                if p == BACK_AT[f"z{c}"]:
                    if begun(b - 1):
                        act.wait_ge(b_pe.sem, b_pe.value(b - 1, "lg"))
                    act.wait_ge(b_pe.sem, b_pe.value(b, f"z{c}"))
                    nc.scalar.activation(gate[:, c, :], ps_b, ACT.Tanh, bias=tiny[:, 6, 0:1], scale=0.5).then_inc(b_act.sem, 1)
            for c in range(C):
                if p == BACK_AT[f"hT{c}"]:
                    act.wait_ge(b_pe.sem, b_pe.value(b, f"hT{c}"))
                    nc.scalar.activation(h2T[:, c, :], ps_b, ACT.Copy).then_inc(b_act.sem, 1)

        def act_iteration(act, i, head, front, attn, back):
            for p in range(POINTS):
                if attn:
                    for u in POINT_UNITS[p % 3]:
                        act_attn(act, i, p // 3, u)
                if back:
                    act_back(act, p, i - 1)
                if front:
                    act_front(act, p, i + 1)
                if head:
                    act_head(act, p, i + 2)


        def dve_steps(dve, count):
            def done(inst, then=True):
                count[0] += 1
                inst.then_inc(su_dve, 1)
                if then:
                    dve.wait_ge(su_dve, count[0])
            return done

        def dve_setup_weights(dve):
            count = [0]
            done = dve_steps(dve, count)
            dve.wait_ge(const_loaded, 32)
            dve.wait_ge(weights_loaded, 32)
            done(nc.vector.tensor_scalar(delta_r, delta_r, SCALE, None, ALU.mult))
            done(nc.vector.tensor_copy(delta_parts[:, 0, :], delta_r))
            done(nc.vector.tensor_tensor(delta_s, delta_r, delta_parts[:, 0, :], ALU.subtract))
            done(nc.vector.tensor_copy(delta_parts[:, 1, :], delta_s))
            done(nc.vector.tensor_tensor(delta_r, delta_s, delta_parts[:, 1, :], ALU.subtract))
            done(nc.vector.tensor_copy(delta_parts[:, 2, :], delta_r))
            done(nc.vector.tensor_scalar(delta_s, delta_parts[:, 0, :], cst("part", 3)[:, 0:1], None, ALU.mult))
            done(nc.vector.scalar_tensor_tensor(delta_r, delta_parts[:, 1, :], cst("part", 3)[:, 1:2], delta_s, ALU.mult, ALU.add))
            done(nc.vector.scalar_tensor_tensor(delta3[:], delta_parts[:, 2, :], cst("part", 3)[:, 2:3], delta_r, ALU.mult, ALU.add))
            done(nc.vector.memset(ones3[:], 1.0))
            done(nc.vector.tensor_tensor(w("qkv"), w("qkv"), prm("ln1").unsqueeze(2).to_broadcast([P, C, QKV]), ALU.mult))
            done(nc.vector.tensor_scalar(w("f_o"), w("f_o"), 0.5, None, ALU.mult))
            done(nc.vector.tensor_tensor(prm("qkn"), prm("qkn"), prm("qn"), ALU.mult))
            done(nc.vector.tensor_tensor(wg, prm("Wg"), cst("same_head"), ALU.mult))
            done(nc.vector.tensor_scalar(tiny[:, 6, 0:1], prm("bg"), 0.5, None, ALU.mult))
            assert count[0] == SETUP_WEIGHTS, count[0]

        def dve_setup_context(dve):
            count = [SETUP_WEIGHTS]
            done = dve_steps(dve, count)
            dve.wait_ge(su_pe, 1)
            for g in range(C):
                done(nc.vector.tensor_scalar(kT[:, g, :], ps_f[:, g, :], prm("c_bk")[:, g:g + 1], None, ALU.add), False)
            for b in range(B):
                dve.wait_ge(su_pe, 2 + b)
                done(nc.vector.tensor_tensor(v_all[:, b, :], ps_s[:, b % SCORE_BANKS, 0:D], prm("c_bv"), ALU.add), False)
            assert count[0] == SETUP_DVE, count[0]

        def dve_stats(dve, k, src, b, st, names):
            for t in range(T):
                last = nc.vector.bn_stats(stats[:, k, t, :], src(t))
            last.then_inc(st.sem, 1)
            dve.wait_ge(st.sem, st.value(b, names[0]))
            carry(dve)
            for t in range(T):
                last = nc.vector.bn_aggr(mv[:, k, t, :], stats[:, k, t, :])
            last.then_inc(st.sem, 1)

        def dve_head(dve, p, b):
            if p == HEAD_AT["ln1"]:
                dve.wait_ge(x_loaded, b * 16 + 16)
                if begun(b - 1):
                    dve.wait_ge(h_pool.sem, h_pool.value(b - 1, "ln1_rstd"))
                dve_stats(dve, 0, lambda t: x_in[:, t, :], b, h_dve, ["ln1_stats"])
            if p == HEAD_AT["xn"]:
                dve.wait_ge(h_pool.sem, h_pool.value(b, "ln1_rstd"))
                if begun(b - 1):
                    dve.wait_ge(f_pe.sem, f_pe.value(b - 1, "hT1"))
                for t in range(T):
                    last = nc.vector.tensor_scalar(xn[:, t, :], x_in[:, t, :], mv[:, 0, t, 0:1], tiny[:, 1, t:t + 1], ALU.subtract, ALU.mult)
                last.then_inc(h_dve.sem, 1)

            if p == HEAD_AT["cq"]:
                if begun(b - 1):
                    dve.wait_ge(f_pe.sem, f_pe.value(b - 1, "wo1"))
                for g in range(C):
                    dve.wait_ge(h_pe.sem, h_pe.value(b, f"cq{g}"))
                    nc.vector.tensor_scalar(cqT[:, g, :], fb(f"cq{g}"), prm("c_bq")[:, g:g + 1], prm("tau")[:, bass.ds(b, 1)],
                                            ALU.add, ALU.mult).then_inc(h_dve.sem, 1)

        def dve_front(dve, p, b):
            def at(stage):
                return p == AT[stage]

            def softmax_shift(t):
                dve.wait_ge(f_pe.sem, f_pe.value(b, f"cs{t}1"))
                nc.vector.tensor_reduce(cmax[:, t % 2, :], ps_f[:, 0:C].rearrange("p g (h s) -> p (g h) s", h=PAIRS), X, ALU.max).then_inc(f_dve.sem, 1)
                dve.wait_ge(f_dve.sem, f_dve.value(b, f"cmax{t}"))
                if t >= 2:
                    dve.wait_ge(f_pe.sem, f_pe.value(b, f"cT{t - 2}1"))
                elif begun(b - 1):
                    dve.wait_ge(f_pe.sem, f_pe.value(b - 1, f"cT{t + 2}1"))
                for g in range(C):
                    nc.vector.tensor_tensor(cs[:, t % 2, g * L:(g + 1) * L].rearrange("p (h s) -> p h s", h=PAIRS),
                                            ps_f[:, g, :].rearrange("p (h s) -> p h s", h=PAIRS),
                                            cmax[:, t % 2, g * PAIRS:(g + 1) * PAIRS].unsqueeze(2).to_broadcast([P, PAIRS, S]),
                                            ALU.subtract).then_inc(f_dve.sem, 1)

            def normalise(t):
                dve.wait_ge(f_pe.sem, f_pe.value(b, f"co{t}"))
                sums = fb(f"co{t}").rearrange("p (k c q) -> p k c q", k=2, c=C)
                nc.vector.reciprocal(crec, sums[:, 1]).then_inc(f_dve.sem, 1)
                dve.wait_ge(f_dve.sem, f_dve.value(b, f"crec{t}"))
                nc.vector.tensor_tensor(coT[:, :, t * P:(t + 1) * P], sums[:, 0], crec, ALU.mult).then_inc(f_dve.sem, 1)

            for t in range(T):
                if at(f"co{t}"):
                    normalise(t)
            for t in range(T):
                if at(f"cs{t}"):
                    softmax_shift(t)
            if at("wo"):
                dve.wait_ge(h_pool.sem, h_pool.value(b, "xbo"))
                if begun(b - 2):
                    dve.wait_ge(b_pool.sem, b_pool.value(b - 2, "res"))
                for k in range(2):
                    dve.wait_ge(f_pe.sem, f_pe.value(b, f"wo{k}"))
                    nc.vector.tensor_tensor(x1[:, bass.ds(b % 2, 1), 2 * k:2 * k + 2, :].rearrange("p a t d -> p (a t) d"),
                                            fb(f"wo{k}").rearrange("p (t d) -> p t d", t=2), x_in[:, 2 * k:2 * k + 2, :],
                                            ALU.add).then_inc(f_dve.sem, 1)
                dve.wait_ge(f_dve.sem, f_dve.value(b, "x1_1"))
                if begun(b - 1):
                    dve.wait_ge(f_pool.sem, f_pool.value(b - 1, "meansq"))
                carry(dve)
                dve_stats(dve, 1, lambda t: x1[:, bass.ds(b % 2, 1), t, :].rearrange("p a d -> p (a d)"), b, f_dve, ["ln2_stats"])
            if at("y"):
                dve.wait_ge(f_pool.sem, f_pool.value(b, "ln2_rstd"))
                if begun(b - 2):
                    dve.wait_ge(b_pool.sem, b_pool.value(b - 2, "res"))
                for t in range(T):
                    last = nc.vector.tensor_scalar(y[:, bass.ds(b % 2, 1), t, :].rearrange("p a d -> p (a d)"),
                                                   x1[:, bass.ds(b % 2, 1), t, :].rearrange("p a d -> p (a d)"),
                                                   mv[:, 1, t, 0:1], tiny[:, 3, t:t + 1], ALU.subtract, ALU.mult)
                last.then_inc(f_dve.sem, 1)
            for k in range(2):
                if not at(f"qkv{k}"):
                    continue
                if k == 0:
                    if begun(b - 1):
                        dve.wait_ge(v_dve.sem, v_dve.value(b - 1, "v"))
                    if begun(b - 1):
                        dve.wait_ge(f_pool.sem, f_pool.value(b - 1, "sin2"))
                for t in (2 * k, 2 * k + 1):
                    dve.wait_ge(f_pe.sem, f_pe.value(b, f"qkv{t}"))
                    nc.vector.tensor_tensor(qkv[:, t, :], fb(f"qkv{t}")[:, 0:QKV], prm("bqkv"), ALU.add).then_inc(f_dve.sem, 1)
            qk = qkv[:, :, 0:HS * E].rearrange("p t (h e) -> p t h e", e=E)
            ra = rope_a[:, :, :].rearrange("p t (h e) -> p t h e", e=E)
            flat_a = rope_a[:, :, :].rearrange("p t n -> p (t n)")
            flat_b = rope_b[:, :, :].rearrange("p t n -> p (t n)")
            if at("rope"):
                dve.wait_ge(f_dve.sem, f_dve.value(b, "qkv3"))
                cos = cst("cos").rearrange("p (t e) -> p t e", t=T)
                for half in range(2):
                    last = nc.vector.tensor_tensor(ra[:, :, :, 8 * half:8 * half + 8], qk[:, :, :, 8 * half:8 * half + 8],
                                                   cos.unsqueeze(2).to_broadcast([P, T, HS, 8]), ALU.mult)
                last.then_inc(f_dve.sem, 1)
                dve.wait_ge(f_act.sem, f_act.value(b, "square"))
                nc.vector.tensor_reduce(qk_ms, squares.rearrange("p t (h e) -> p (t h) e", e=E), X, ALU.add).then_inc(f_dve.sem, 1)
                dve.wait_ge(f_dve.sem, f_dve.value(b, "meansq"))
                nc.vector.tensor_scalar(qk_ms, qk_ms, 1.0 / E, RMS_EPS, ALU.mult, ALU.add).then_inc(f_dve.sem, 1)
                dve.wait_ge(f_dve.sem, f_dve.value(b, "qk_eps"))
                nc.vector.tensor_scalar(qk_rs.bitcast(I32), qk_ms.bitcast(I32), 1, None, ALU.logical_shift_right).then_inc(f_dve.sem, 1)
                dve.wait_ge(f_dve.sem, f_dve.value(b, "half_bits"))
                nc.vector.tensor_scalar(qk_rs.bitcast(I32), qk_rs.bitcast(I32), -1.0, float(0x5F375A86), ALU.mult, ALU.add).then_inc(f_dve.sem, 1)
                before = "guess"
                for k in range(3):
                    dve.wait_ge(f_dve.sem, f_dve.value(b, before))
                    nc.vector.scalar_tensor_tensor(qk_t, qk_rs, -0.5, qk_rs, ALU.mult, ALU.mult).then_inc(f_dve.sem, 1)
                    dve.wait_ge(f_dve.sem, f_dve.value(b, f"newton_a{k}"))
                    nc.vector.tensor_tensor(qk_t, qk_t, qk_ms, ALU.mult).then_inc(f_dve.sem, 1)
                    dve.wait_ge(f_dve.sem, f_dve.value(b, f"newton_b{k}"))
                    nc.vector.scalar_tensor_tensor(qk_rs, qk_t, 1.5, qk_rs, ALU.add, ALU.mult).then_inc(f_dve.sem, 1)
                    before = f"newton_c{k}"
            if at("norm"):
                dve.wait_ge(f_pool.sem, f_pool.value(b, "rope"))
                dve.wait_ge(f_dve.sem, f_dve.value(b, "newton_c2"))
                nc.vector.tensor_tensor(flat_a.rearrange("p (h e) -> p h e", e=E), flat_a.rearrange("p (h e) -> p h e", e=E),
                                        qk_rs.unsqueeze(2).to_broadcast([P, T * HS, E]), ALU.mult).then_inc(f_dve.sem, 1)
                dve.wait_ge(f_dve.sem, f_dve.value(b, "qnorm"))
                keys = rope_a[:, :, H * E:HS * E]
                nc.vector.tensor_tensor(keys, keys, prm("qkn").unsqueeze(1).to_broadcast([P, T, KV * E]), ALU.mult).then_inc(f_dve.sem, 1)
            if at("split"):
                dve.wait_ge(f_dve.sem, f_dve.value(b, "kweight"))
                for m in range(2):
                    if begun(b - 1):
                        dve.wait_ge(f_pe.sem, f_pe.value(b - 1, (ST0, ST1)[m][-1]))
                    groups = [(ra[:, :, 8 * m:8 * m + 8, :], stack[:, m, :, 0:8, :], 2), (ra[:, :, H + 2 * m:H + 2 * m + 2, :], stack[:, m, :, 8:10, :], 1)]
                    for value, heads, lo in groups:
                        last = nc.vector.tensor_scalar(heads[:, :, :, 0:E].bitcast(I32), value.bitcast(I32), HI_MASK, None, ALU.bitwise_and)
                    last.then_inc(f_dve.sem, 1)
                    dve.wait_ge(f_dve.sem, f_dve.value(b, f"hi{m}"))
                    for value, heads, lo in groups:
                        last = nc.vector.tensor_tensor(heads[:, :, :, lo * E:(lo + 1) * E], value, heads[:, :, :, 0:E], ALU.subtract)
                    last.then_inc(f_dve.sem, 1)
            for m, units in enumerate((ST0, ST1)):
                if at(f"st{m}"):
                    for n in units:
                        if n not in ST_ACT:
                            st_evacuate(dve, n, b)

        def dve_values(dve, b):
            dve.wait_ge(f_dve.sem, f_dve.value(b, "qkv3"))
            if begun(b - 1):
                dve.wait_ge(v_pe.sem, v_pe.value(b - 1, ATTENDED[-1]))
            for t in range(T):
                last = nc.vector.tensor_copy(v_pad[:, t, :, E:2 * E], qkv[:, t, HS * E:].rearrange("p (g e) -> p g e", e=E))
            last.then_inc(v_dve.sem, 1)

        def dve_normalise(dve, b, m):
            dve.wait_ge(v_pe.sem, v_pe.value(b, f"pv{2 * m + 1}{T - 1}"))
            if m == 0:
                if begun(b - 1):
                    dve.wait_ge(b_pe.sem, b_pe.value(b - 1, "wo1"))
            nc.vector.reciprocal(rec, ps_v[:, 1, :]).then_inc(n_dve.sem, 1)
            dve.wait_ge(n_dve.sem, n_dve.value(b, f"rec{m}"))
            nc.vector.tensor_tensor(aoT[:, m, :], ps_v[:, 0, :], rec, ALU.mult).then_inc(n_dve.sem, 1)

        def dve_back(dve, p, b):
            fg, fa = gate[:, :, :].rearrange("p c n -> p (c n)"), aoT[:, :, :].rearrange("p c n -> p (c n)")
            if p == BACK_AT["gated"]:
                dve.wait_ge(b_act.sem, b_act.value(b, "gate1"))
                nc.vector.scalar_tensor_tensor(fa, fg, 1.0, fa, ALU.add, ALU.mult).then_inc(b_dve.sem, 1)
            yb = y[:, bass.ds(b % 2, 1), :, :].rearrange("p a t d -> p (a t) d")
            for k in range(2):
                if p == BACK_AT[f"wo{k}"]:
                    dve.wait_ge(f_pool.sem, f_pool.value(b, "ybo"))
                    dve.wait_ge(b_pe.sem, b_pe.value(b, f"wo{k}"))
                    nc.vector.tensor_tensor(yb[:, 2 * k:2 * k + 2, :], ps_b.rearrange("p (t d) -> p t d", t=2), yb[:, 2 * k:2 * k + 2, :],
                                            ALU.add).then_inc(b_dve.sem, 1)
            if p == BACK_AT["wo1"]:
                dve.wait_ge(b_dve.sem, b_dve.value(b, "in1"))
                if begun(b - 1):
                    dve.wait_ge(b_pool.sem, b_pool.value(b - 1, "ms"))
                carry(dve)
                dve_stats(dve, 2, lambda t: yb[:, t, :], b, b_dve, ["stats"])
            if p == BACK_AT["h2"]:
                dve.wait_ge(b_pool.sem, b_pool.value(b, "rms"))
                if begun(b - 1):
                    dve.wait_ge(b_pe.sem, b_pe.value(b - 1, "hT1"))
                if not (isinstance(b, int) and b < 1):
                    dve.wait_ge(rows_stored, b * 32)
                for t in range(T):
                    last = nc.vector.scalar_tensor_tensor(h2[:, t, :], yb[:, t, :], tiny[:, 10, t:t + 1], prm("ln2"), ALU.mult, ALU.mult)
                last.then_inc(b_dve.sem, 1)
            if p == BACK_AT["lg"]:
                dve.wait_ge(b_pe.sem, b_pe.value(b, "lg"))
                nc.vector.tensor_tensor(logits[:, bass.ds(b * T, T), :], ps_b[:, 0:T * NE].rearrange("p (t e) -> p t e", t=T),
                                        prm("br").unsqueeze(1).to_broadcast([P, T, NE]), ALU.add).then_inc(b_dve.sem, 1)

        def dve_iteration(dve, i, head, front, attn, back):
            for p in range(POINTS):
                if p == 5:
                    if back:
                        dve_normalise(dve, i - 1, 1)
                    if attn:
                        dve_values(dve, i)
                if p == 17 and attn:
                    dve_normalise(dve, i, 0)
                if front:
                    dve_front(dve, p, i + 1)
                if back:
                    dve_back(dve, p, i - 1)
                if head:
                    dve_head(dve, p, i + 2)

        def pool_setup(pool):
            nc.gpsimd.memset(ln_eps[:], LN_EPS)
            nc.gpsimd.memset(rms_eps[:], RMS_EPS)
            nc.gpsimd.memset(half_power[:], -0.5).then_inc(su_pool, 1)
            nc.gpsimd.memset(v_pad, 0.0).then_inc(su_pool, 1)
            pool.wait_ge(su_pool, 2)

        def pool_scale_keys(pool):
            pool.wait_ge(su_dve, SETUP_WEIGHTS + C)
            nc.gpsimd.tensor_scalar(kT.rearrange("p c n -> p (c n)"), kT.rearrange("p c n -> p (c n)"), SCALE, 0.0,
                                    ALU.mult, ALU.add).then_inc(su_pool, 1)

        def rsqrt(dst, src, eps, steps, b, names):
            nc.gpsimd.tensor_tensor(dst, src, eps, ALU.add).then_inc(steps.sem, 1)
            nc.gpsimd.wait_ge(steps.sem, steps.value(b, names[0]))
            nc.gpsimd.tensor_tensor(dst, dst, half_power[:], ALU.pow).then_inc(steps.sem, 1)

        def pool_head(pool, p, b):
            if p == HEAD_AT["ln1"]:
                pool.wait_ge(h_dve.sem, h_dve.value(b, "ln1_aggr"))
                rsqrt(tiny[:, 1, :], mv[:, 0, :, 1], ln_eps[:], h_pool, b, ["ln1_eps"])
            if p == HEAD_AT["kbd"]:
                if isinstance(b, int) and b == 0:
                    pool.wait_ge(su_pool, 3)
                if begun(b - 1):
                    pool.wait_ge(f_pe.sem, f_pe.value(b - 1, "cs31"))
                for g in range(C):
                    last = nc.gpsimd.tensor_tensor(kbd[:, g, :, :], kT[:, g, bass.ds(b * S, S)].unsqueeze(1).to_broadcast([P, PAIRS, S]),
                                                   cst("head_of").unsqueeze(2).to_broadcast([P, PAIRS, S]), ALU.mult)
                last.then_inc(h_pool.sem, 1)
                if begun(b - 1):
                    pool.wait_ge(f_pe.sem, f_pe.value(b - 1, "co3"))
                if isinstance(b, int) and b == 0:
                    pool.wait_ge(su_dve, SETUP_DVE)
                nc.gpsimd.tensor_tensor(vbd.rearrange("p j (x e) -> p j x e", x=2), v_all[:, bass.ds(b, 1), :].rearrange("p a (j x e) -> p (a j) x e", x=2, e=E),
                                        cst("half").unsqueeze(1).unsqueeze(3).to_broadcast([P, PAIRS, 2, E]), ALU.mult).then_inc(h_pool.sem, 1)
            if p == HEAD_AT["xn"]:
                pool.wait_ge(h_dve.sem, h_dve.value(b, "xn"))
                nc.gpsimd.tensor_tensor(x_in, x_in, prm("c_bo").unsqueeze(1).to_broadcast([P, T, D]), ALU.add).then_inc(h_pool.sem, 1)

        def pool_front(pool, p, b):
            def ew(dst, a, c, op):
                nc.gpsimd.tensor_tensor(dst, a, c, op).then_inc(f_pool.sem, 1)

            def at(stage):
                return p == AT[stage]

            if at("ln2"):
                pool.wait_ge(f_dve.sem, f_dve.value(b, "ln2_aggr"))
                rsqrt(tiny[:, 3, :], mv[:, 1, :, 1], ln_eps[:], f_pool, b, ["ln2_eps"])
                pool.wait_ge(f_pool.sem, f_pool.value(b, "ln2_rstd"))
                ew(tiny[:, 4, :], tiny[:, 3, :], tiny[:, 3, :], ALU.mult)
                pool.wait_ge(f_pool.sem, f_pool.value(b, "rstd2"))
                ew(tiny[:, 11, :], tiny[:, 4, :], mv[:, 1, :, 1], ALU.mult)
                pool.wait_ge(f_pool.sem, f_pool.value(b, "meansq"))
                rsqrt(tiny[:, 5, :], tiny[:, 11, :], rms_eps[:], f_pool, b, ["rms_eps"])
            if at("hT"):
                pool.wait_ge(f_act.sem, f_act.value(b, "h"))
                yb = y[:, bass.ds(b % 2, 1), :, :].rearrange("p a t d -> p (a t) d")
                ew(yb, yb, prm("f_bo").unsqueeze(1).to_broadcast([P, T, D]), ALU.add)
            if at("rope"):
                pool.wait_ge(f_dve.sem, f_dve.value(b, "qkv3"))
                qk = qkv[:, :, 0:HS * E].rearrange("p t (h e) -> p t h e", e=E)
                rb = rope_b[:, :, :].rearrange("p t (h e) -> p t h e", e=E)
                for lo, hi, name in ((0, 8, "negsin"), (8, 0, "sin")):
                    ew(rb[:, :, :, lo:lo + 8], qk[:, :, :, hi:hi + 8],
                       cst(name).rearrange("p (t e) -> p t e", t=T).unsqueeze(2).to_broadcast([P, T, HS, 8]), ALU.mult)
                pool.wait_ge(f_pool.sem, f_pool.value(b, "sin2"))
                pool.wait_ge(f_dve.sem, f_dve.value(b, "cosmul"))
                ew(rope_a[:, :, :], rope_a[:, :, :], rope_b[:, :, :], ALU.add)

        def pool_mask(pool, b, s, v):
            units = POINT_UNITS[v]
            pool.wait_ge(a_act.sem, a_act.value(b, f"s{s}{units[-1]}"))
            a, width = UNIT_AT[units[0]], UNIT_AT[units[1]] - UNIT_AT[units[0]]
            k = 4 if v == 1 else 1
            d = pt[:, s % 4, a:a + 2 * width].rearrange("p (x k q) -> p x k q", x=2, q=P)[:, :, 0:k:3, :]
            nc.gpsimd.tensor_tensor(d, d, cst("causal").unsqueeze(1).unsqueeze(1).to_broadcast([P, 2, d.shape[2], P]), ALU.mult).then_inc(a_pool.sem, 1)

        def pool_back(pool, p, b):
            def ew(dst, a, c, op):
                nc.gpsimd.tensor_tensor(dst, a, c, op).then_inc(b_pool.sem, 1)

            yb = y[:, bass.ds(b % 2, 1), :, :].rearrange("p a t d -> p (a t) d")
            xb = x1[:, bass.ds(b % 2, 1), :, :].rearrange("p a t d -> p (a t) d")
            if p == BACK_AT["rms"]:
                pool.wait_ge(b_dve.sem, b_dve.value(b, "aggr"))
                ew(tiny[:, 7, :], mv[:, 2, :, 0], mv[:, 2, :, 0], ALU.mult)
                pool.wait_ge(b_pool.sem, b_pool.value(b, "msq"))
                ew(tiny[:, 8, :], tiny[:, 7, :], mv[:, 2, :, 1], ALU.add)
                pool.wait_ge(b_pool.sem, b_pool.value(b, "ms"))
                rsqrt(tiny[:, 10, :], tiny[:, 8, :], rms_eps[:], b_pool, b, ["rms_eps"])
            if p == BACK_AT["res"]:
                if not (isinstance(b, int) and b < 1):
                    pool.wait_ge(rows_stored, b * 32)
                ew(residual, xb, yb, ALU.add)

        def pool_iteration(pool, i, head, front, attn, back):
            for p in range(POINTS):
                if attn:
                    pool_mask(pool, i, p // 3, p % 3)
                if back:
                    pool_back(pool, p, i - 1)
                if front:
                    pool_front(pool, p, i + 1)
                if head:
                    pool_head(pool, p, i + 2)

        block = ctx.enter_context(nc.Block())

        @block.sync
        def _(sp):
            def load_x(b):
                if begun(b - 1):
                    sp.wait_ge(f_dve.sem, f_dve.value(b - 1, "x1_1"))
                sp.dma_start(x_in, ins["x"][bass.ds(b * L, L), :].rearrange("(t p) d -> p t d", p=P)).then_inc(x_loaded, 16)

            def store_rows(b):
                rows = rows_dram[bass.ds(b * L, L), :].rearrange("(t p) d -> p t d", p=P)
                sp.wait_ge(b_dve.sem, b_dve.value(b, "h2"))
                sp.dma_start(rows[:, :, 0:D], h2).then_inc(rows_stored, 16)
                sp.wait_ge(b_pool.sem, b_pool.value(b, "res"))
                sp.dma_start(rows[:, :, D:2 * D], residual).then_inc(rows_stored, 16)

            load_x(0)
            sp.dma_start(const[:], ins["const"]).then_inc(const_loaded, 16)
            sp.dma_start(par, ins["par"]).then_inc(const_loaded, 16)
            sp.dma_start(delta_r, ins["delta"].to_broadcast([3, B * S])).then_inc(weights_loaded, 16)
            sp.dma_start(wgt, ins["wgt"].rearrange("(c p) n -> p c n", p=P)).then_inc(weights_loaded, 16)
            sp.dma_start(ctxw, ins["ctxw"].rearrange("(c p) n -> p c n", p=P)).then_inc(context_loaded, 16)
            load_x(1)
            with sp.Fori(2, B) as b:
                load_x(b)
                store_rows(b - 2)
            early_loads(sp)
            store_rows(B - 2)
            store_rows(B - 1)
            moe_loads(sp)

        @block.tensor
        def _(pe):
            pe.wait_ge(const_loaded, 32)
            pe.wait_ge(weights_loaded, 32)
            for p in HEAD_POINTS:
                pe_head(pe, p, 0)
            pe_setup(pe)
            pe.wait_ge(su_dve, SETUP_DVE)
            pipeline(pe, pe_iteration)
            pe_routing(pe)
            pe_moe(pe)

        @block.scalar
        def _(act):
            for p in HEAD_POINTS:
                act_head(act, p, 0)
            act.wait_ge(su_dve, SETUP_DVE)
            pipeline(act, act_iteration)
            act_moe(act)

        @block.vector
        def _(dve):
            for p in HEAD_POINTS:
                if p == HEAD_AT["cq"]:
                    dve_setup_weights(dve)
                dve_head(dve, p, 0)
            dve_setup_context(dve)
            pipeline(dve, dve_iteration)
            dve_routing(dve)
            dve_moe(dve)

        @block.gpsimd
        def _(pool):
            assert pool is nc.gpsimd
            pool_setup(pool)
            for p in HEAD_POINTS:
                if p == HEAD_AT["kbd"]:
                    pool_scale_keys(pool)
                pool_head(pool, p, 0)
            pipeline(pool, pool_iteration)
            pool_moe(pool)


def shape_constants():
    p, t = np.arange(P), np.arange(T)
    inv_freq = (1.0 / 10000.0 ** (np.arange(0, E, 2, dtype=np.float32) / E)).astype(np.float32)
    angle = ((t[None, :, None] * P + p[:, None, None]).astype(np.float32) * inv_freq).astype(np.float32)
    rows = {
        "ident": np.eye(P), "causal": p[:, None] <= p[None, :], "before": p[:, None] < p[None, :], "ones": np.ones((P, P)),
        "same_head": p[:, None] // E == p[None, :] // E, "row": np.tile(p, (P, 1)),
        "head_of": p[:, None] // E == np.arange(PAIRS), "half": p[:, None] // S == np.arange(2),
        "part": p[:, None] == np.arange(3),
        "cos": np.cos(angle).reshape(P, -1), "sin": np.sin(angle).reshape(P, -1), "negsin": -np.sin(angle).reshape(P, -1),
        "tile_limit": np.tile(np.where(np.arange(TT) == 0, -1, P * np.arange(TT)), (P, 1)),
        "earlier": np.tile((np.arange(NE)[None, :] < np.arange(NE)[:, None]).reshape(1, -1), (P, 1)),
        "rank": np.tile(NE - np.arange(NE), (P, 1)), "tile_no": np.tile(np.arange(NT + 1), (P, 1)),
        "token": np.arange(TT)[None, :] * P + p[:, None],
        "pair_ones": p[:, None] // S == np.arange(2 * E) // E,
        "slot_ones": np.tile(np.arange(3 * E) // E == 1, (P, 1)),
    }
    return np.concatenate([rows[name].astype(np.float32) for name in CONST], axis=1)


def kernel(**inputs):
    from concourse import bacc
    from concourse.bass_utils import run_bass_kernel_spmd

    a = {k: np.asarray(v) for k, v in inputs.items()}
    c, f = {k[9:]: v for k, v in a.items() if k.startswith("L0_xcond_")}, {k[7:]: v for k, v in a.items() if k.startswith("L0_ffn_")}

    order = np.array([8 * m + 4 * x + r for m in range(2) for r in range(4) for x in range(2)])
    cols = (order[:, None] * E + np.arange(E)[None, :]).reshape(-1)

    order_o = np.array([8 * m + 4 * x + 2 * j + i for m in range(2) for i in range(2) for x in range(2) for j in range(2)])
    rows_o = (order_o[:, None] * E + np.arange(E)[None, :]).reshape(-1)

    def row(v):
        return np.broadcast_to(v.reshape(1, -1), (P, v.size))

    def col(v):
        return v.reshape(-1, P).T

    par = {
        "c_bo": row(c["bo"]), "bqkv": row(np.concatenate([f["bq"][cols], f["bk"], f["bv"]])), "f_bo": row(f["bo"]), "ln2": row(f["ln2_w"]),
        "qkn": row(np.tile(f["kn_w"], KV)), "qn": row(np.tile(f["qn_w"], KV)), "br": row(f["br"]), "c_bv": row(c["bv"]),
        "tau": row(a["condB_tau"]), "c_bq": col(c["bq"]), "c_bk": col(c["bk"]),
        "bg": np.tile(f["bg"], PAIRS)[:, None], "ln1": col(f["ln1_w"]), "Wg": np.tile(f["Wg"], (PAIRS, PAIRS)),
    }
    wgt = np.concatenate([c["Wq"].T, c["Wo"].T, f["Wq"][:, cols], f["Wk"], f["Wv"], f["Wo"][rows_o, :], f["Wr"]], axis=1)
    ctxw = np.concatenate([c["Wk"].T, c["Wv"].T, a["ctx_1024"].reshape(B * S, D).T], axis=1)
    arrays = {
        "x": a["x"].reshape(N, D), "const": shape_constants(), "par": np.concatenate([par[name] for name in PAR], axis=1),
        "delta": a["fside_BxS2_0"].reshape(1, -1), "wgt": wgt, "ctxw": ctxw, "W1": f["W1"], "W2": f["W2"], "b1": f["b1"], "b2": f["b2"],
    }
    arrays = {k: np.ascontiguousarray(v) for k, v in arrays.items()}

    nc = bacc.Bacc("TRN2", target_bir_lowering=False, num_devices=1)
    ins = {k: nc.dram_tensor(f"in_{k}", v.shape, mybir.dt.from_np(v.dtype), kind="ExternalInput").ap() for k, v in arrays.items()}
    out = nc.dram_tensor("out", (N, D), F32, kind="ExternalOutput").ap()
    build(nc, ins, out)
    r = run_bass_kernel_spmd(nc, [{f"in_{k}": v for k, v in arrays.items()}], core_ids=[0])
    return r.results[0]["out"].reshape(B, L, D)
```
